# Optimizing a Trainium2 kernel written in Bass

```python
import numpy as np
import jax
import jax.numpy as jnp

def _softmax(x, axis=-1):
    return jax.nn.softmax(x, axis=axis)

def _gelu(x):
    return jax.nn.gelu(x, approximate=True)

def _silu(x):
    return jax.nn.silu(x)

def _sigmoid(x):
    return jax.nn.sigmoid(x)

def _layernorm(x, axis=-1, eps=1e-05):
    m = jnp.mean(x, axis=axis, keepdims=True)
    v = jnp.var(x, axis=axis, keepdims=True)
    return (x - m) / jnp.sqrt(v + eps)

def _scatter_add(tgt, idx, src, axis=0):
    return tgt.at[idx].add(src)

def _segment_sum(src, seg, n):
    return jax.ops.segment_sum(src, seg, n)
kernel_name = 'mk_gnn_ffn_d1_gnn_r64_a5ac6f'

def setup_inputs(seed: int=0):
    np.random.seed(seed)
    _w = jnp.asarray

    def _rec_inputs():
        import jax
        import jax.numpy as jnp
        _gk = jax.random.key(seed)
        x = -8.776e-05 + 1 * jax.random.normal(jax.random.fold_in(_gk, 1), (10000, 512), jnp.float32)
        src = jax.random.randint(jax.random.fold_in(_gk, 2), (2500,), 0, 10000, jnp.int32)
        dst = jax.random.randint(jax.random.fold_in(_gk, 3), (2500,), 0, 10000, jnp.int32)
        _o = jnp.argsort(dst, stable=True)
        src = src[_o]
        dst = dst[_o]
        edge_attr_128 = 0.000283511 + 1.00007 * jax.random.normal(jax.random.fold_in(_gk, 11), (2500, 128), jnp.float32)
        return (x, src, dst, edge_attr_128)
    x, src, dst, edge_attr_128 = _rec_inputs()

    def _L0_gnn_setup():
        import jax, jax.numpy as jnp
        import numpy as np
        N, E = (10000, 150000)
        HD, ED = (512, 128)
        BN_EPS = 1e-05
        key = jax.random.key(seed)
        ks = jax.random.split(key, 16)
        s = 0.02
        return {'h': jax.random.normal(ks[0], (N, HD), jnp.float32), 'edge_index': jax.random.randint(ks[1], (2, E), 0, N, jnp.int32), 'edge_attr': jax.random.normal(ks[2], (E, ED), jnp.float32), 'W1': jax.random.normal(ks[3], (HD, HD + ED), jnp.float32) * s, 'b1': jnp.zeros((HD,), jnp.float32), 'W2': jax.random.normal(ks[4], (HD, HD), jnp.float32) * s, 'b2': jnp.zeros((HD,), jnp.float32), 'W_ih': jax.random.normal(ks[5], (3 * HD, HD), jnp.float32) * s, 'W_hh': jax.random.normal(ks[6], (3 * HD, HD), jnp.float32) * s, 'b_ih': jnp.zeros((3 * HD,), jnp.float32), 'b_hh': jnp.zeros((3 * HD,), jnp.float32), 'gamma': jnp.ones((HD,), jnp.float32), 'beta': jnp.zeros((HD,), jnp.float32), 'run_mean': jnp.zeros((HD,), jnp.float32), 'run_var': jnp.ones((HD,), jnp.float32)}
    _L0_gnn_all = _L0_gnn_setup()
    _L0_gnn_in = {k: v for k, v in _L0_gnn_all.items() if k in ('W1', 'b1', 'W2', 'b2', 'W_ih', 'W_hh', 'b_ih', 'b_hh', 'gamma', 'beta', 'run_mean', 'run_var')}
    del _L0_gnn_all

    def _L0_ffn_setup():
        import jax, jax.numpy as jnp
        import numpy as np
        S, B, D, F, E, K = (1024, 2, 512, 32, 8, 2)
        key = jax.random.key(seed)
        ks = jax.random.split(key, 12)
        s = lambda *sh: 1.0 / np.sqrt(sh[0])
        inp = {'x': jax.random.normal(ks[0], (S, B, D), dtype=jnp.float32), 'Wg': jax.random.normal(ks[1], (D, E), dtype=jnp.float32) * s(D), 'bg': jnp.zeros((E,), dtype=jnp.float32), 'W1': jax.random.normal(ks[2], (E, D, F), dtype=jnp.float32) * s(D), 'b1': jnp.zeros((E, F), dtype=jnp.float32), 'W2': jax.random.normal(ks[3], (E, F, D), dtype=jnp.float32) * s(F), 'b2': jnp.zeros((E, D), dtype=jnp.float32), 'Ws1': jax.random.normal(ks[4], (D, F), dtype=jnp.float32) * s(D), 'bs1': jnp.zeros((F,), dtype=jnp.float32), 'Ws2': jax.random.normal(ks[5], (F, D), dtype=jnp.float32) * s(F), 'bs2': jnp.zeros((D,), dtype=jnp.float32)}
        return inp
    _L0_ffn_all = _L0_ffn_setup()
    _L0_ffn_in = {k: v for k, v in _L0_ffn_all.items() if k in ('Wg', 'bg', 'W1', 'b1', 'W2', 'b2', 'Ws1', 'bs1', 'Ws2', 'bs2')}
    del _L0_ffn_all
    return {'x': x, 'src': src, 'dst': dst, 'edge_attr_128': edge_attr_128, 'L0_gnn_W1': _L0_gnn_in['W1'], 'L0_gnn_b1': _L0_gnn_in['b1'], 'L0_gnn_W2': _L0_gnn_in['W2'], 'L0_gnn_b2': _L0_gnn_in['b2'], 'L0_gnn_W_ih': _L0_gnn_in['W_ih'], 'L0_gnn_W_hh': _L0_gnn_in['W_hh'], 'L0_gnn_b_ih': _L0_gnn_in['b_ih'], 'L0_gnn_b_hh': _L0_gnn_in['b_hh'], 'L0_gnn_gamma': _L0_gnn_in['gamma'], 'L0_gnn_beta': _L0_gnn_in['beta'], 'L0_gnn_run_mean': _L0_gnn_in['run_mean'], 'L0_gnn_run_var': _L0_gnn_in['run_var'], 'L0_ffn_Wg': _L0_ffn_in['Wg'], 'L0_ffn_bg': _L0_ffn_in['bg'], 'L0_ffn_W1': _L0_ffn_in['W1'], 'L0_ffn_b1': _L0_ffn_in['b1'], 'L0_ffn_W2': _L0_ffn_in['W2'], 'L0_ffn_b2': _L0_ffn_in['b2'], 'L0_ffn_Ws1': _L0_ffn_in['Ws1'], 'L0_ffn_bs1': _L0_ffn_in['bs1'], 'L0_ffn_Ws2': _L0_ffn_in['Ws2'], 'L0_ffn_bs2': _L0_ffn_in['bs2']}

def reference(x, src, dst, edge_attr_128, L0_gnn_W1, L0_gnn_b1, L0_gnn_W2, L0_gnn_b2, L0_gnn_W_ih, L0_gnn_W_hh, L0_gnn_b_ih, L0_gnn_b_hh, L0_gnn_gamma, L0_gnn_beta, L0_gnn_run_mean, L0_gnn_run_var, L0_ffn_Wg, L0_ffn_bg, L0_ffn_W1, L0_ffn_b1, L0_ffn_W2, L0_ffn_b2, L0_ffn_Ws1, L0_ffn_bs1, L0_ffn_Ws2, L0_ffn_bs2):
    import jax
    import jax.numpy as jnp

    def _L0_gnn_ref(h, edge_index, edge_attr, W1, b1, W2, b2, W_ih, W_hh, b_ih, b_hh, gamma, beta, run_mean, run_var):
        import jax, jax.numpy as jnp
        import numpy as np
        N, E = (10000, 150000)
        HD, ED = (512, 128)
        BN_EPS = 1e-05
        src, dst = (edge_index[0], edge_index[1])
        m_in = jnp.concatenate([h[src], edge_attr], axis=1)
        m = jax.nn.relu(m_in @ W1.T + b1) @ W2.T + b2
        agg = jax.ops.segment_sum(m, dst, num_segments=h.shape[0])
        gi = agg @ W_ih.T + b_ih
        gh = h @ W_hh.T + b_hh
        i_r, i_z, i_n = jnp.split(gi, 3, axis=1)
        h_r, h_z, h_n = jnp.split(gh, 3, axis=1)
        r = jax.nn.sigmoid(i_r + h_r)
        z = jax.nn.sigmoid(i_z + h_z)
        n = jnp.tanh(i_n + r * h_n)
        h_new = (1.0 - z) * n + z * h
        bn = gamma * (h_new - run_mean) * jax.lax.rsqrt(run_var + BN_EPS) + beta
        return h + bn

    def _L0_ffn_ref(x, Wg, bg, W1, b1, W2, b2, Ws1, bs1, Ws2, bs2):
        import jax, jax.numpy as jnp
        import numpy as np
        S, B, D, F, E, K = (1024, 2, 512, 32, 8, 2)
        gate_logits = jnp.einsum('sbd,de->sbe', x, Wg) + bg
        weights, selected = jax.lax.top_k(gate_logits, K)
        weights = jax.nn.softmax(weights.astype(jnp.float32), axis=-1)
        onehot = jax.nn.one_hot(selected, E, dtype=weights.dtype)
        comb = jnp.einsum('sbk,sbke->sbe', weights, onehot)
        h = jax.nn.relu(jnp.einsum('sbd,edf->sbef', x, W1) + b1)
        y = jnp.einsum('sbef,efd->sbed', h, W2) + b2
        out = jnp.einsum('sbe,sbed->sbd', comb, y)
        hs = jax.nn.relu(jnp.einsum('sbd,df->sbf', x, Ws1) + bs1)
        shared = jnp.einsum('sbf,fd->sbd', hs, Ws2) + bs2
        out = out + 1.0 / K * shared
        return out
    edge_index = jnp.stack([src, dst])
    x = x + _L0_gnn_ref(_layernorm(x, axis=-1), edge_index, edge_attr_128, L0_gnn_W1, L0_gnn_b1, L0_gnn_W2, L0_gnn_b2, L0_gnn_W_ih, L0_gnn_W_hh, L0_gnn_b_ih, L0_gnn_b_hh, L0_gnn_gamma, L0_gnn_beta, L0_gnn_run_mean, L0_gnn_run_var)
    x = x + _L0_ffn_ref(_layernorm(x, axis=-1)[None], L0_ffn_Wg, L0_ffn_bg, L0_ffn_W1, L0_ffn_b1, L0_ffn_W2, L0_ffn_b2, L0_ffn_Ws1, L0_ffn_bs1, L0_ffn_Ws2, L0_ffn_bs2)[0]
    return x

_drawn_inputs = setup_inputs


def setup_inputs(seed=0):
    import zlib

    import numpy as np

    out = dict(_drawn_inputs(seed))
    spreads = {'L0_gnn_b1': (0.0, 0.8),
     'L0_gnn_b2': (0.0, 0.72),
     'L0_gnn_b_ih': (0.0, 0.1),
     'L0_gnn_b_hh': (0.0, 0.316),
     'L0_gnn_gamma': (1.0, 0.2),
     'L0_gnn_beta': (0.0, 0.1),
     'L0_gnn_run_mean': (0.0, 0.1),
     'L0_gnn_run_var': (1.0, 0.2),
     'L0_ffn_bg': (0.0, 0.1),
     'L0_ffn_b1': (0.0, 0.391),
     'L0_ffn_b2': (0.0, 0.275),
     'L0_ffn_bs1': (0.0, 0.519),
     'L0_ffn_bs2': (0.0, 0.403)}
    factors = {'edge_attr_128': 8.0, 'L0_gnn_W1': 5.372, 'L0_gnn_W2': 4.672, 'L0_gnn_W_ih': 4.075}
    for name, (base, spread) in spreads.items():
        noise = np.random.default_rng([zlib.crc32(name.encode()), seed]).standard_normal(out[name].shape)
        drawn = base * np.exp(spread * noise) if base else spread * noise
        out[name] = jnp.asarray(drawn.astype(out[name].dtype))
    for name, factor in factors.items():
        out[name] = (out[name] * factor).astype(out[name].dtype)
    return out
```

```python
import concourse.bass as bass
from concourse import mybir

F32 = mybir.dt.float32
F32R = mybir.dt.float32r
I32 = mybir.dt.int32
U32 = mybir.dt.uint32
ALU = mybir.AluOpType
ACT = mybir.ActivationFunctionType
AX_X = mybir.AxisListType.X

P = 128
EPS = 1e-5


def gnn_ffn(nc, x, src, dst, dst_rows, attr_t, w1t, b1, w2t, b2, wih_t, whh_t, b_ih, b_hh, gamma, beta,
            run_mean, run_var, wg, bg, ew1, eb1, ew2, eb2, ws1, bs1, ws2, bs2, out):
    N, D = x.shape
    R, EC = src.shape
    NT = N // R
    E = R * EC
    DK = D // P
    K1 = w1t.shape[0] // P
    G3 = 3 * D
    NE = wg.shape[1]
    HE = ew1.shape[1]
    HS = ws1.shape[1]
    HF = HE // NE
    F1 = NE + HE + HS
    KF = 3
    SUP = 4
    NSUP = EC // SUP
    SW = SUP * R
    assert N == R * NT and EC == SUP * NSUP and HE == 2 * P and NT % 2 == 0

    agg = nc.dram_tensor("agg", (E + R, D), F32, kind="Internal").ap()
    gates_in = nc.dram_tensor("gates_in", (E + R, G3), F32, kind="Internal").ap()
    slot_of_node = nc.dram_tensor("slot_of_node", (N, 1), I32, kind="Internal").ap()

    cursor = [(nc.sbuf_base + 63) // 64 * 64]

    def place(name, shape, dt=F32):
        size = 4
        for n in shape[1:]:
            size *= n
        at = cursor[0]
        cursor[0] = (at + size + 31) // 32 * 32
        return nc.alloc_sbuf_tensor_at(name, list(shape), dt, offset=at)

    ident = place("ident", [P, P])
    f1_hi = place("f1_hi", [P, DK, F1], F32R)
    f1_lo = place("f1_lo", [P, DK, F1], F32R)
    f2_hi = place("f2_hi", [P, KF, D], F32R)
    f2_lo = place("f2_lo", [P, KF, D], F32R)
    bn_scale = place("bn_scale", [R, D])
    bn_shift = place("bn_shift", [R, D])
    hn_bias = place("hn_bias", [R, D])
    f1_bias = place("f1_bias", [R, F1])
    minus_half = place("minus_half", [R, SUP])
    ones_col = place("ones_col", [R, SUP])
    iota8 = place("iota8", [R, NE])
    region_a = cursor[0]
    whh_hi = place("whh_hi", [P, DK, G3], F32R)
    whh_lo = place("whh_lo", [P, DK, G3], F32R)
    region_b = cursor[0]

    bank = [nc.alloc_psum_tensor(f"bank{k}", [P, 512], F32) for k in range(8)]

    def sem(name):
        return nc.alloc_semaphore(name)

    def wait_from(eng, s, n):
        if not isinstance(n, int) or n > 0:
            eng.wait_ge(s, n)

    held = {e: sem(f"held_{e}") for e in ("pool", "dve")}

    cursor[0] = region_a
    w1_hi = place("w1_hi", [P, K1, D], F32R)
    w1_lo = place("w1_lo", [P, K1, D], F32R)
    w2_hi = place("w2_hi", [P, DK, D], F32R)
    w2_lo = place("w2_lo", [P, DK, D], F32R)
    hs = place("hs", [R, SUP, D])
    msg = place("msg", [R, D])
    b2_row = place("b2_row", [R, D])
    cursor[0] = max(cursor[0], region_b)
    wih_hi = place("wih_hi", [P, DK, G3], F32R)
    wih_lo = place("wih_lo", [P, DK, G3], F32R)
    dst_i = place("dst_i", [R, EC], I32)
    region_c = cursor[0]
    src_i = place("src_i", [R, EC], I32)
    dst_f = place("dst_f", [R, EC])
    tile_base = place("tile_base", [R, EC])
    row_i = place("row_i", [R, SUP * R], I32)
    iota_row = place("iota_row", [R, R])
    node_init = place("node_init", [R, NT], I32)
    b1_col = place("b1_col", [P, DK])
    src_at = place("src_at", [R, SUP], I32)
    dst_at = place("dst_at", [R, SUP], I32)
    stage = place("stage", [P, 2, G3])
    xs = place("xs", [R, SUP, D])
    st_e = place("st_e", [R, SUP, 6])
    mv_e = place("mv_e", [R, SUP, 2])
    ve_e = place("ve_e", [R, SUP])
    nm_e = place("nm_e", [R, SUP])
    rs_e = place("rs_e", [R, SUP])
    nmr_e = place("nmr_e", [R, SUP])
    attr = place("attr", [P, SW])
    m_hi_t = place("m_hi_t", [P, K1, SW], F32R)
    m_lo_t = place("m_lo_t", [P, K1, SW], F32R)
    r32 = place("r32", [P, 2, SW])
    r_at = cursor[0]
    r_hi = place("r_hi", [P, DK, SW], F32R)
    r_lo = place("r_lo", [P, DK, SW], F32R)
    msg_hi = place("msg_hi", [R, 2, D], F32R)
    msg_hi_end = cursor[0]
    msg_lo = place("msg_lo", [R, D], F32R)
    same = place("same", [R, 2, R], F32R)
    trash = place("trash", [R, 1])
    row_no = place("row_no", [R, 1])
    sums = place("sums", [R, SUP, D])
    zeros = sums[:, 1, :]
    top_row = place("top_row", [R, EC])
    is_top = place("is_top", [R, EC])
    slot_i = place("slot_i", [R, EC], I32)
    slot_at4 = place("slot_at4", [R, SUP], I32)
    add_all = place("add_all", [R, EC], I32)
    add_at = place("add_at", [R, SUP], I32)
    assert cursor[0] <= nc.sbuf_usable_end, (cursor[0], nc.sbuf_usable_end)
    all_dst_size = (4 * E + 31) // 32 * 32
    assert msg_hi_end - r_at >= all_dst_size + 4 * E
    all_dst = nc.alloc_sbuf_tensor_at("all_dst", [R, EC, R], I32, offset=r_at)
    all_same = nc.alloc_sbuf_tensor_at("all_same", [R, EC, R], F32, offset=r_at + all_dst_size)
    var_row, mean_row = sums[:, SUP - 2, :], sums[:, SUP - 1, :]

    small_in = sem("small_in")
    rows_in = sem("rows_in")
    iotas = sem("iotas")
    consts = sem("consts")
    bn_rows = sem("bn_rows")
    staged = [sem("staged0"), sem("staged1")]
    stage_hi = sem("stage_hi")
    stage_lo = sem("stage_lo")
    attr_in = sem("attr_in")
    row_in = sem("row_in")
    dst_f_done = sem("dst_f_done")
    table_init = sem("table_init")
    src_ready = sem("src_ready")
    xs_in = [sem(f"xs_in{j}") for j in range(SUP)]
    stats_e = sem("stats_e")
    mv_ready = sem("mv_ready")
    var_e = sem("var_e")
    rs_ready = sem("rs_ready")
    nmr_ready = sem("nmr_ready")
    h_e = sem("h_e")
    t_e = sem("t_e")
    t_hi = sem("t_hi")
    t_lo = sem("t_lo")
    l1 = sem("l1")
    relu_done = sem("relu_done")
    r_hi_done = sem("r_hi_done")
    r_lo_done = sem("r_lo_done")
    l2 = sem("l2")
    msg_done = sem("msg_done")
    msg_hi_done = sem("msg_hi_done")
    msg_lo_done = sem("msg_lo_done")
    same_done = sem("same_done")
    summed = sem("summed")
    sums_done = sem("sums_done")
    all_dst_in = sem("all_dst_in")
    top_step = sem("top_step")
    index_step = sem("index_step")
    slots_in = sem("slots_in")
    slots_out = sem("slots_out")
    add_at_ready = sem("add_at_ready")
    scattered = sem("scattered")

    w1v = w1t.rearrange("(k p) n -> p k n", p=P)
    w2v = w2t.rearrange("(k p) n -> p k n", p=P)
    wihv = wih_t.rearrange("(k p) n -> p k n", p=P)
    ew1v = ew1.rearrange("(k p) n -> p k n", p=P)
    ew2v = ew2.rearrange("(k p) n -> p k n", p=P)
    wgv = wg.rearrange("(k p) n -> p k n", p=P)
    ws1v = ws1.rearrange("(k p) n -> p k n", p=P)
    FW = KF - 1

    def wide(w, a, b, hi, lo, n):
        return [(lambda s: s[:, 0:(b - a) * n].rearrange("p (k n) -> p k n", n=n), w[:, a:b, :])], \
            (b - a) * n, hi[:, a:b, :], lo[:, a:b, :], n

    loads = [wide(w1v, 0, 3, w1_hi, w1_lo, D), wide(w1v, 3, 5, w1_hi, w1_lo, D),
             wide(w2v, 0, 3, w2_hi, w2_lo, D), wide(w2v, 3, 4, w2_hi, w2_lo, D)]
    loads += [wide(wihv, k, k + 1, wih_hi, wih_lo, G3) for k in range(DK)]
    loads += [([
        (lambda s: s[:, 0:DK * F1].rearrange("p (k n) -> p k n", n=F1)[:, :, 0:NE], wgv),
        (lambda s: s[:, 0:DK * F1].rearrange("p (k n) -> p k n", n=F1)[:, :, NE:NE + HE], ew1v),
        (lambda s: s[:, 0:DK * F1].rearrange("p (k n) -> p k n", n=F1)[:, :, NE + HE:F1], ws1v)],
        DK * F1, f1_hi[:, :, :], f1_lo[:, :, :], F1)]
    loads += [([
        (lambda s: s[:, 0:FW * D].rearrange("p (k n) -> p k n", n=D), ew2v),
        (lambda s: s[0:HS, FW * D:KF * D], ws2),
        (lambda s: s[HS:HS + NE, FW * D:KF * D], eb2),
        (lambda s: s[HS + NE:HS + NE + 1, FW * D:KF * D], bs2.rearrange("(o n) -> o n", o=1))],
        KF * D, f2_hi[:, :, :], f2_lo[:, :, :], D)]
    F2_LOAD = len(loads) - 1

    landed = []
    tally = [0, 0]
    for n, ld in enumerate(loads):
        tally[n % 2] += 16 * len(ld[0])
        landed.append(tally[n % 2])
    W1_LOADS, W2_LOADS = 2, 4

    small = [
        (src_i[:, :], src), (dst_i[:, :], dst),
        (b1_col[:, :], b1),
    ]
    wide_rows = [
        (b2_row[:, :], b2), (bn_scale[:, :], gamma), (bn_shift[:, :], beta), (hn_bias[:, :], b_hh[2 * D:G3]),
        (var_row, run_var), (mean_row, run_mean),
        (f1_bias[:, 0:NE], bg), (f1_bias[:, NE:NE + HE], eb1), (f1_bias[:, NE + HE:F1], bs1),
    ]
    SMALL_IN, ROWS_IN = 16 * len(small), 16 * len(wide_rows)

    def bcast(v):
        return v.rearrange("(o n) -> o n", o=1).broadcast_to((R, v.shape[0]))

    with nc.Block() as block:
        @block.sync
        def _(sp):
            for to, of in small:
                sp.dma_start(to, of).then_inc(small_in, 16)
            sp.dma_start(attr[:, :], attr_t[:, 0:SW]).then_inc(attr_in, 16)
            sp.dma_start(all_dst[:, :, :].rearrange("p c r -> p (c r)"),
                         dst_rows.rearrange("(o g) r -> o (g r)", o=1).broadcast_to((R, E))).then_inc(all_dst_in, 16)
            sp.dma_start(row_i[:, :], dst_rows[0:1, :].broadcast_to((R, SW))).then_inc(row_in, 16)
            for n in range(2):
                for to, of in loads[n][0]:
                    sp.dma_start(to(stage[:, n % 2, :]), of).then_inc(staged[n % 2], 16)
            for to, of in wide_rows:
                sp.dma_start(to, bcast(of)).then_inc(rows_in, 16)
            sp.wait_ge(iotas, 8)
            sp.dma_start(slot_of_node.rearrange("(p t) o -> p (t o)", t=NT), node_init[:, :]).then_inc(table_init, 16)
            sp.dma_start(agg.rearrange("(p k) d -> p k d", p=R),
                         zeros.unsqueeze(1).broadcast_to((R, EC + 1, D))).then_inc(table_init, 16)

            def weights(a, b):
                for n in range(a, b):
                    sp.wait_ge(stage_lo, n - 1)
                    sp.wait_ge(stage_hi, n - 1)
                    if n == F2_LOAD:
                        sp.wait_ge(iotas, 9)
                    for to, of in loads[n][0]:
                        sp.dma_start(to(stage[:, n % 2, :]), of).then_inc(staged[n % 2], 16)

            def edge_inputs(g):
                at, gg = (g * SW, g) if isinstance(g, int) else (sp.snap(g * SW), sp.snap(g))
                sp.wait_ge(t_lo, g * (SUP + 1) - SUP)
                sp.dma_start(attr[:, :], attr_t[:, bass.ds(at, SW)]).then_inc(attr_in, 16)
                sp.wait_ge(same_done, SUP * g)
                sp.dma_start(row_i[:, :], dst_rows[bass.ds(gg, 1), :].broadcast_to((R, SW))).then_inc(row_in, 16)

            weights(2, 4)
            edge_inputs(1)
            weights(4, 8)
            edge_inputs(2)
            weights(8, len(loads))
            with sp.Fori(3, NSUP) as g:
                edge_inputs(g)

        @block.gpsimd
        def _(pool):
            pool.memset(zeros, 0.0).then_inc(iotas, 1)
            pool.iota(iota_row[:, :], pattern=[[1, R]], base=0, channel_multiplier=0,
                      allow_small_or_imprecise_dtypes=True).then_inc(iotas, 1)
            pool.iota(tile_base[:, :], pattern=[[R, EC]], base=0, channel_multiplier=0,
                      allow_small_or_imprecise_dtypes=True).then_inc(iotas, 1)
            pool.iota(iota8[:, :], pattern=[[1, NE]], base=0, channel_multiplier=0,
                      allow_small_or_imprecise_dtypes=True).then_inc(iotas, 1)
            pool.memset(minus_half[:, :], -0.5).then_inc(iotas, 1)
            pool.iota(node_init[:, :], pattern=[[0, NT]], base=E, channel_multiplier=1).then_inc(iotas, 1)
            pool.iota(trash[:, :], pattern=[[0, 1]], base=E, channel_multiplier=1,
                      allow_small_or_imprecise_dtypes=True).then_inc(iotas, 1)
            pool.iota(row_no[:, :], pattern=[[0, 1]], base=0, channel_multiplier=1,
                      allow_small_or_imprecise_dtypes=True).then_inc(iotas, 1)
            pool.memset(ones_col[:, :], 1.0)
            pool.memset(ident[:, :], 0.0).then_inc(consts, 1)
            pool.wait_ge(consts, 1)
            pool.affine_select(out=ident[:, :], in_=ident[:, :], compare_op=ALU.not_equal, fill=1.0, base=0,
                               pattern=[[-1, P]], channel_multiplier=1).then_inc(consts, 1)

            def gather_sources(g):
                pool.tensor_copy(src_at[:, :], src_i[:, bass.ds(g * SUP, SUP)]).then_inc(src_ready, 1)
                pool.wait_ge(src_ready, g + 1).then_inc(held["pool"], 1)
                for j in range(SUP):
                    pool.indirect_dma_start(out=xs[:, j, :], out_offset=None, in_=x,
                                            in_offset=bass.IndirectOffsetOnAxis(ap=src_at[:, j:j + 1], axis=0),
                                            ).then_inc(xs_in[j], 16)

            pool.wait_ge(small_in, SMALL_IN)
            gather_sources(0)

            def front(g1):
                pool.wait_ge(var_e, g1 + 1)
                pool.tensor_tensor(rs_e[:, :], ve_e[:, :], minus_half[:, :], ALU.pow).then_inc(rs_ready, 1)
                pool.wait_ge(rs_ready, g1 + 1)
                pool.tensor_tensor(nmr_e[:, :], nm_e[:, :], rs_e[:, :], ALU.mult).then_inc(nmr_ready, 1)

            def enter_slots():
                with pool.Fori(0, NSUP) as g:
                    copied = pool.snap(2 * (g + 1))
                    entered = [pool.snap(16 * (g * SUP + j + 1)) for j in range(SUP)]
                    at = bass.ds(g * SUP, SUP)
                    pool.tensor_copy(dst_at[:, :], dst_i[:, at]).then_inc(index_step, 1)
                    pool.tensor_copy(slot_at4[:, :], slot_i[:, at]).then_inc(index_step, 1)
                    pool.wait_ge(index_step, copied).then_inc(held["pool"], 1)
                    for j in range(SUP):
                        pool.indirect_dma_start(out=slot_of_node, in_=slot_at4[:, j:j + 1], in_offset=None,
                                                out_offset=bass.IndirectOffsetOnAxis(ap=dst_at[:, j:j + 1], axis=0),
                                                ).then_inc(slots_in, 16)
                        pool.wait_ge(slots_in, entered[j]).then_inc(held["pool"], 1)

            def read_slots():
                with pool.Fori(0, NSUP) as g:
                    copied = pool.snap(2 * NSUP + 2 * g + 1)
                    taken = pool.snap(2 * NSUP + 2 * g + 2)
                    got = pool.snap(16 * SUP * (g + 1))
                    at = bass.ds(g * SUP, SUP)
                    pool.tensor_copy(dst_at[:, :], dst_i[:, at]).then_inc(index_step, 1)
                    pool.wait_ge(index_step, copied).then_inc(held["pool"], 1)
                    for j in range(SUP):
                        pool.indirect_dma_start(out=slot_at4[:, j:j + 1], out_offset=None, in_=slot_of_node,
                                                in_offset=bass.IndirectOffsetOnAxis(ap=dst_at[:, j:j + 1], axis=0),
                                                ).then_inc(slots_out, 16)
                    pool.wait_ge(slots_out, got).then_inc(held["pool"], 1)
                    pool.tensor_copy(slot_i[:, at], slot_at4[:, :]).then_inc(index_step, 1)
                    pool.wait_ge(index_step, taken).then_inc(held["pool"], 1)
                done = 4 * NSUP
                pool.tensor_scalar(top_row[:, :], slot_i[:, :], trash[:, 0:1], None, ALU.subtract)\
                    .then_inc(index_step, 1)
                pool.wait_ge(index_step, done + 1)
                pool.tensor_tensor(top_row[:, :], top_row[:, :], is_top[:, :], ALU.mult).then_inc(index_step, 1)
                pool.wait_ge(index_step, done + 2)
                pool.tensor_scalar(add_all[:, :], top_row[:, :], trash[:, 0:1], None, ALU.add).then_inc(index_step, 1)
                pool.wait_ge(index_step, done + 3)

            def chain(g):
                copied = pool.snap(g + 1)
                ready = [pool.snap(g * SUP + j + 1) for j in range(SUP)]
                written = [pool.snap(16 * (g * SUP + j + 1)) for j in range(SUP)]
                pool.tensor_copy(add_at[:, :], add_all[:, bass.ds(g * SUP, SUP)]).then_inc(add_at_ready, 1)
                pool.wait_ge(add_at_ready, copied).then_inc(held["pool"], 1)
                for j in range(SUP):
                    pool.wait_ge(sums_done, ready[j]).then_inc(held["pool"], 1)
                    pool.indirect_dma_start(out=agg, in_=sums[:, j, :], in_offset=None,
                                            out_offset=bass.IndirectOffsetOnAxis(ap=add_at[:, j:j + 1], axis=0),
                                            compute_op=ALU.add).then_inc(scattered, 16)
                    pool.wait_ge(scattered, written[j]).then_inc(held["pool"], 1)

            front(0)

            pool.wait_ge(bn_rows, 1)
            pool.tensor_tensor(var_row, var_row, minus_half[:, 0:1].broadcast_to((R, D)), ALU.pow).then_inc(consts, 1)
            pool.wait_ge(consts, 3)
            pool.tensor_tensor(bn_scale[:, :], bn_scale[:, :], var_row, ALU.mult).then_inc(consts, 1)
            pool.wait_ge(consts, 4)
            pool.tensor_tensor(mean_row, mean_row, bn_scale[:, :], ALU.mult).then_inc(consts, 1)
            pool.wait_ge(consts, 5)
            pool.tensor_tensor(bn_shift[:, :], bn_shift[:, :], mean_row, ALU.subtract).then_inc(consts, 1)
            pool.wait_ge(consts, 6)

            pool.wait_ge(h_e, SUP)
            gather_sources(1)
            front(1)
            pool.wait_ge(h_e, 2 * SUP)
            gather_sources(2)

            pool.wait_ge(table_init, 32)
            pool.wait_ge(top_step, 5)
            enter_slots()
            read_slots()
            chain(0)
            with pool.Fori(1, NSUP - 2) as g:
                front(g + 1)
                pool.wait_ge(h_e, SUP * (g + 2)).then_inc(held["pool"], 1)
                gather_sources(g + 2)
                chain(g)
            front(NSUP - 1)
            chain(NSUP - 2)
            chain(NSUP - 1)

        @block.scalar
        def _(act):
            def split_hi(n):
                act.wait_ge(staged[n % 2], landed[n])
                _, width, hi, _, cols = loads[n]
                act.activation(hi, stage[:, n % 2, 0:width].rearrange("p (k n) -> p k n", n=cols), ACT.Copy)\
                    .then_inc(stage_hi, 1)

            def normalise(g1):
                act.wait_ge(nmr_ready, g1 + 1)
                if not isinstance(g1, int) or g1 > 0:
                    act.wait_ge(t_e, SUP * g1)
                for j in range(SUP):
                    act.activation(hs[:, j, :], xs[:, j, :], ACT.Identity, bias=nmr_e[:, j:j + 1],
                                   scale=rs_e[:, j:j + 1]).then_inc(h_e, 1)

            def transposed_hi(g1):
                if not isinstance(g1, int) or g1 > 0:
                    act.wait_ge(l1, DK * g1)
                act.wait_ge(attr_in, 16 * (g1 + 1))
                act.activation(m_hi_t[:, K1 - 1, :], attr[:, :], ACT.Copy).then_inc(t_hi, 1)
                for j in range(SUP):
                    act.wait_ge(t_e, SUP * g1 + j + 1)
                    act.activation(m_hi_t[:, 0:DK, j * R:(j + 1) * R],
                                   bank[2 + j % 2][:, 0:DK * R].rearrange("p (k r) -> p k r", k=DK),
                                   ACT.Copy).then_inc(t_hi, 1)

            def layer1(g):
                for b in range(DK):
                    act.wait_ge(l1, DK * g + b + 1)
                    wait_from(act, r_lo_done, DK * g + b - 1)
                    act.activation(r32[:, b % 2, :], bank[b % 2][:, 0:SW], ACT.Relu, bias=b1_col[:, b:b + 1])\
                        .then_inc(relu_done, 1)
                    act.wait_ge(relu_done, DK * g + b + 1)
                    if b == 0 and (not isinstance(g, int) or g > 0):
                        act.wait_ge(l2, SUP * g)
                    act.activation(r_hi[:, b, :], r32[:, b % 2, :], ACT.Copy).then_inc(r_hi_done, 1)

            def take_sums(g, j):
                act.wait_ge(summed, SUP * g + j + 1)
                if not isinstance(g, int) or g > 0:
                    act.wait_ge(scattered, 16 * (SUP * g + j - SUP + 1))
                elif j == 1:
                    act.wait_ge(table_init, 32)
                elif j == 2:
                    act.wait_ge(consts, 6)
                act.activation(sums[:, j, :], bank[6 + j % 2][0:R, :], ACT.Copy).then_inc(sums_done, 1)

            def layer2(g):
                for j in range(SUP):
                    act.wait_ge(msg_done, SUP * g + j + 1)
                    wait_from(act, summed, SUP * g + j - 1)
                    act.activation(msg_hi[:, j % 2, :], msg[:, :], ACT.Copy).then_inc(msg_hi_done, 1)
                    if j > 0:
                        take_sums(g, j - 1)
                take_sums(g, SUP - 1)

            for n in range(2):
                split_hi(n)
            normalise(0)
            transposed_hi(0)
            act.wait_ge(top_step, 3)
            split_hi(2)
            split_hi(3)
            normalise(1)
            layer1(0)
            transposed_hi(1)
            layer2(0)
            for n in range(4, 6):
                split_hi(n)
            normalise(2)
            layer1(1)
            transposed_hi(2)
            layer2(1)
            for n in range(6, len(loads)):
                split_hi(n)
            with act.Fori(2, NSUP - 1) as g:
                normalise(g + 1)
                layer1(g)
                transposed_hi(g + 1)
                layer2(g)
            layer1(NSUP - 1)
            layer2(NSUP - 1)

        @block.vector
        def _(dve):
            def split_lo(n):
                dve.wait_ge(stage_hi, n + 1)
                _, width, hi, lo, cols = loads[n]
                dve.tensor_tensor(lo, stage[:, n % 2, 0:width].rearrange("p (k n) -> p k n", n=cols),
                                  hi.bitcast(F32), ALU.subtract).then_inc(stage_lo, 1)
                if n == F2_LOAD - 2:
                    dve.wait_ge(stage_lo, n + 1)
                    dve.memset(stage[:, F2_LOAD % 2, FW * D:KF * D], 0.0).then_inc(iotas, 1)

            def stats(g1):
                if not isinstance(g1, int) or g1 > 0:
                    dve.wait_ge(nmr_ready, g1)
                for j in range(SUP):
                    dve.wait_ge(xs_in[j], 16 * (g1 + 1))
                    dve.bn_stats(st_e[:, j, :], xs[:, j, :]).then_inc(stats_e, 1)
                dve.wait_ge(stats_e, SUP * (g1 + 1)).then_inc(held["dve"], 1)
                for j in range(SUP):
                    dve.bn_aggr(mv_e[:, j, :], st_e[:, j, :]).then_inc(mv_ready, 1)
                dve.wait_ge(mv_ready, SUP * (g1 + 1))
                dve.tensor_scalar(nm_e[:, :], mv_e[:, :, 0], -1.0, None, ALU.mult)
                dve.tensor_scalar(ve_e[:, :], mv_e[:, :, 1], EPS, None, ALU.add).then_inc(var_e, 1)

            def top_rows():
                dve.wait_ge(all_dst_in, 16)
                dve.tensor_tensor(all_same[:, :, :], all_dst[:, :, :],
                                  dst_f[:, :].unsqueeze(2).broadcast_to((R, EC, R)), ALU.is_equal).then_inc(top_step, 1)
                dve.wait_ge(top_step, 1)
                dve.tensor_tensor(all_same[:, :, :], all_same[:, :, :],
                                  iota_row[:, :].unsqueeze(1).broadcast_to((R, EC, R)), ALU.mult).then_inc(top_step, 1)
                dve.wait_ge(top_step, 2)
                dve.tensor_reduce(top_row[:, :], all_same[:, :, :], AX_X, ALU.max).then_inc(top_step, 1)
                dve.wait_ge(top_step, 3)
                dve.tensor_scalar(is_top[:, :], top_row[:, :], row_no[:, 0:1], None, ALU.is_equal).then_inc(top_step, 1)
                dve.tensor_tensor(slot_i[:, :], top_row[:, :], tile_base[:, :], ALU.add).then_inc(top_step, 1)

            def transposed_lo(g1):
                if not isinstance(g1, int) or g1 > 0:
                    dve.wait_ge(l1, DK * g1)
                dve.wait_ge(t_hi, (SUP + 1) * g1 + 1)
                dve.tensor_tensor(m_lo_t[:, K1 - 1, :], attr[:, :], m_hi_t[:, K1 - 1, :].bitcast(F32), ALU.subtract)\
                    .then_inc(t_lo, 1)
                for j in range(SUP):
                    dve.wait_ge(t_hi, (SUP + 1) * g1 + j + 2)
                    dve.tensor_tensor(m_lo_t[:, 0:DK, j * R:(j + 1) * R],
                                      bank[2 + j % 2][:, 0:DK * R].rearrange("p (k r) -> p k r", k=DK),
                                      m_hi_t[:, 0:DK, j * R:(j + 1) * R].bitcast(F32), ALU.subtract)\
                        .then_inc(t_lo, 1)

            def layer1(g):
                for b in range(DK):
                    if b == 0 and (not isinstance(g, int) or g > 0):
                        dve.wait_ge(l2, SUP * g)
                    dve.wait_ge(r_hi_done, DK * g + b + 1)
                    dve.tensor_tensor(r_lo[:, b, :], r32[:, b % 2, :], r_hi[:, b, :].bitcast(F32), ALU.subtract)\
                        .then_inc(r_lo_done, 1)

            def layer2(g):
                for j in range(SUP):
                    dve.wait_ge(l2, SUP * g + j + 1)
                    wait_from(dve, msg_hi_done, SUP * g + j)
                    wait_from(dve, msg_lo_done, SUP * g + j)
                    dve.tensor_tensor(msg[:, :], bank[4 + j % 2][0:R, :], b2_row[:, :], ALU.add).then_inc(msg_done, 1)
                    dve.wait_ge(row_in, 16 * (g + 1))
                    wait_from(dve, summed, SUP * g + j - 1)
                    dve.tensor_scalar(same[:, j % 2, :], row_i[:, j * R:(j + 1) * R],
                                      dst_f[:, bass.ds(SUP * g + j, 1)], None, ALU.is_equal).then_inc(same_done, 1)
                    dve.wait_ge(msg_hi_done, SUP * g + j + 1)
                    wait_from(dve, summed, SUP * g + j)
                    dve.tensor_tensor(msg_lo[:, :], msg[:, :], msg_hi[:, j % 2, :].bitcast(F32), ALU.subtract)\
                        .then_inc(msg_lo_done, 1)

            dve.wait_ge(small_in, SMALL_IN)
            dve.tensor_copy(dst_f[:, :], dst_i[:, :]).then_inc(dst_f_done, 1)
            dve.wait_ge(iotas, 8)
            for n in range(2):
                split_lo(n)
            stats(0)
            dve.wait_ge(dst_f_done, 1)
            top_rows()
            dve.wait_ge(rows_in, ROWS_IN)
            dve.tensor_scalar(var_row, var_row, EPS, None, ALU.add).then_inc(bn_rows, 1)
            transposed_lo(0)
            split_lo(2)
            split_lo(3)
            stats(1)
            layer1(0)
            transposed_lo(1)
            layer2(0)
            for n in range(4, 6):
                split_lo(n)
            stats(2)
            layer1(1)
            transposed_lo(2)
            layer2(1)
            for n in range(6, len(loads)):
                split_lo(n)
            with dve.Fori(2, NSUP - 1) as g:
                stats(g + 1)
                layer1(g)
                transposed_lo(g + 1)
                layer2(g)
            layer1(NSUP - 1)
            layer2(NSUP - 1)

        @block.tensor
        def _(pe):
            def transposes(g1):
                for j in range(SUP):
                    pe.wait_ge(h_e, SUP * g1 + j + 1)
                    if not isinstance(g1, int) or g1 > 0 or j >= 2:
                        pe.wait_ge(t_lo, (SUP + 1) * g1 + j if j >= 2 else (SUP + 1) * g1 + j - 1)
                    for k in range(DK):
                        last = pe.transpose(bank[2 + j % 2][:, k * R:(k + 1) * R], hs[:, j, k * P:(k + 1) * P],
                                            ident[0:R, 0:R])
                    last.then_inc(t_e, 1)

            def layer1(g):
                pe.wait_ge(t_lo, (SUP + 1) * (g + 1))
                for b in range(DK):
                    wait_from(pe, relu_done, DK * g + b - 1)
                    n = 0
                    for k in range(K1):
                        for w, m in ((w1_hi, m_hi_t), (w1_hi, m_lo_t), (w1_lo, m_hi_t)):
                            last = pe.matmul(bank[b % 2][:, 0:SW], w[:, k, b * P:(b + 1) * P], m[:, k, :],
                                             start=n == 0, stop=n == 3 * K1 - 1)
                            n += 1
                    last.then_inc(l1, 1)

            def tile_sums(g, j):
                pe.wait_ge(msg_lo_done, SUP * g + j + 1)
                wait_from(pe, sums_done, SUP * g + j - 1)
                pe.matmul(bank[6 + j % 2][0:R, :], same[:, j % 2, :], msg_hi[:, j % 2, :], start=True, stop=False)
                pe.matmul(bank[6 + j % 2][0:R, :], same[:, j % 2, :], msg_lo[:, :], start=False, stop=True)\
                    .then_inc(summed, 1)

            def layer2(g):
                pe.wait_ge(r_lo_done, DK * (g + 1))
                for j in range(SUP):
                    wait_from(pe, msg_done, SUP * g + j - 1)
                    n = 0
                    for k in range(DK):
                        for r, w in ((r_hi, w2_hi), (r_hi, w2_lo), (r_lo, w2_hi)):
                            last = pe.matmul(bank[4 + j % 2][0:R, :], r[:, k, j * R:(j + 1) * R], w[:, k, :],
                                             start=n == 0, stop=n == 3 * DK - 1)
                            n += 1
                    last.then_inc(l2, 1)
                    if j > 0:
                        tile_sums(g, j - 1)
                tile_sums(g, SUP - 1)

            pe.wait_ge(consts, 2)
            transposes(0)
            pe.wait_ge(stage_lo, W1_LOADS)
            layer1(0)
            transposes(1)
            pe.wait_ge(stage_lo, W2_LOADS)
            layer2(0)
            with pe.Fori(1, NSUP - 1) as g:
                layer1(g)
                transposes(g + 1)
                layer2(g)
            layer1(NSUP - 1)
            layer2(NSUP - 1)

    cursor[0] = region_c
    ig_bias = place("ig_bias", [R, G3])
    ig_bhh = place("ig_bhh", [R, 2 * D])
    agg_in = place("agg_in", [R, 2, D])
    a_hi = place("a_hi", [P, 2, DK * R], F32R)
    a_lo = place("a_lo", [P, 2, DK * R], F32R)
    g_out = place("g_out", [R, 2, G3])
    stage2 = place("stage2", [P, 2, G3])
    assert cursor[0] <= nc.sbuf_usable_end

    bias_in = sem("bias_in")
    bias_done = sem("bias_done")
    staged2 = [sem("staged2_0"), sem("staged2_1")]
    stage2_hi = sem("stage2_hi")
    stage2_lo = sem("stage2_lo")
    agg_loaded = [sem("agg_loaded0"), sem("agg_loaded1")]
    t_a = sem("t_a")
    a_hi_done = sem("a_hi_done")
    a_lo_done = sem("a_lo_done")
    g_prod = sem("g_prod")
    g_added = sem("g_added")
    g_stored = [sem("g_stored0"), sem("g_stored1")]
    bias_stored = sem("bias_stored")

    whhv = whh_t.rearrange("(k p) n -> p k n", p=P)

    with nc.Block() as block:
        @block.sync
        def _(sp):
            def load(c, s):
                sp.dma_start(agg_in[:, s, :], agg[bass.ds(c * R, R), :]).then_inc(agg_loaded[s], 16)

            for c in range(2):
                load(c, c)
            sp.dma_start(ig_bias[:, :], bcast(b_ih)).then_inc(bias_in, 16)
            sp.dma_start(ig_bhh[:, :], bcast(b_hh[0:2 * D])).then_inc(bias_in, 16)
            sp.dma_start(stage2[:, 0, :], whhv[:, 0, :]).then_inc(staged2[0], 16)
            sp.dma_start(stage2[:, 1, :], whhv[:, 1, :]).then_inc(staged2[1], 16)
            sp.wait_ge(bias_done, 1)
            sp.dma_start(gates_in[E:E + R, :], ig_bias[:, :]).then_inc(bias_stored, 16)
            for c in range(2):
                sp.wait_ge(stage2_lo, c + 1)
                sp.dma_start(stage2[:, c, :], whhv[:, 2 + c, :]).then_inc(staged2[c], 16)
            with sp.Fori(1, EC // 2) as i:
                row = [sp.snap((2 * i + s) * R) for s in range(2)]
                past = [sp.snap((2 * i + s - 2) * R) for s in range(2)]
                for s in range(2):
                    sp.wait_ge(t_a, 2 * i + s - 1)
                    sp.dma_start(agg_in[:, s, :], agg[bass.ds(row[s], R), :]).then_inc(agg_loaded[s], 16)
                for s in range(2):
                    sp.wait_ge(g_added, 3 * (2 * i + s - 1))
                    sp.dma_start(gates_in[bass.ds(past[s], R), :], g_out[:, s, :]).then_inc(g_stored[s], 16)
            for s in range(2):
                c = EC - 2 + s
                sp.wait_ge(g_added, 3 * (c + 1))
                sp.dma_start(gates_in[c * R:(c + 1) * R, :], g_out[:, s, :]).then_inc(g_stored[s], 16)
            for s in range(2):
                sp.wait_ge(g_stored[s], 16 * (EC // 2))
            sp.wait_ge(bias_stored, 16)

        @block.scalar
        def _(act):
            def hi(c, s):
                act.wait_ge(t_a, c + 1)
                wait_from(act, g_prod, 3 * (c - 1))
                act.activation(a_hi[:, s, :], bank[6 + s][:, 0:DK * R], ACT.Copy).then_inc(a_hi_done, 1)

            hi(0, 0)
            for k in range(2):
                act.wait_ge(staged2[k], 16)
                act.activation(whh_hi[:, k, :], stage2[:, k, :], ACT.Copy).then_inc(stage2_hi, 1)
            hi(1, 1)
            for k in range(2, 4):
                act.wait_ge(staged2[k % 2], 32)
                act.activation(whh_hi[:, k, :], stage2[:, k % 2, :], ACT.Copy).then_inc(stage2_hi, 1)
            with act.Fori(1, EC // 2) as i:
                for s in range(2):
                    hi(2 * i + s, s)

        @block.vector
        def _(dve):
            def lo(c, s):
                dve.wait_ge(a_hi_done, c + 1)
                dve.tensor_tensor(a_lo[:, s, :], bank[6 + s][:, 0:DK * R], a_hi[:, s, :].bitcast(F32), ALU.subtract)\
                    .then_inc(a_lo_done, 1)

            def add_bias(c, s, i):
                if not isinstance(i, int) or i > 0:
                    dve.wait_ge(g_stored[s], 16 * i)
                for q in range(3):
                    dve.wait_ge(g_prod, 3 * c + q + 1)
                    dve.tensor_tensor(g_out[:, s, q * D:(q + 1) * D], bank[3 * s + q][0:R, :],
                                      ig_bias[:, q * D:(q + 1) * D], ALU.add).then_inc(g_added, 1)

            def split(k):
                dve.wait_ge(stage2_hi, k + 1)
                dve.tensor_tensor(whh_lo[:, k, :], stage2[:, k % 2, :], whh_hi[:, k, :].bitcast(F32), ALU.subtract)\
                    .then_inc(stage2_lo, 1)

            lo(0, 0)
            dve.wait_ge(bias_in, 32)
            dve.tensor_tensor(ig_bias[:, 0:2 * D], ig_bias[:, 0:2 * D], ig_bhh[:, :], ALU.add).then_inc(bias_done, 1)
            dve.wait_ge(bias_done, 1)
            split(0)
            split(1)
            lo(1, 1)
            add_bias(0, 0, 0)
            split(2)
            split(3)

            def pair(i):
                lo(2 * i, 0)
                add_bias(2 * i - 1, 1, i - 1)
                lo(2 * i + 1, 1)
                add_bias(2 * i, 0, i)

            pair(1)
            with dve.Fori(2, EC // 2) as i:
                pair(i)
            add_bias(EC - 1, 1, EC // 2 - 1)

        @block.tensor
        def _(pe):
            def transposes(c, s, i):
                pe.wait_ge(agg_loaded[s], 16 * (i + 1))
                wait_from(pe, a_lo_done, c - 1)
                for k in range(DK):
                    last = pe.transpose(bank[6 + s][:, k * R:(k + 1) * R], agg_in[:, s, k * P:(k + 1) * P],
                                        ident[0:R, 0:R])
                last.then_inc(t_a, 1)

            def product(c, s):
                pe.wait_ge(a_lo_done, c + 1)
                for q in range(3):
                    wait_from(pe, g_added, 3 * (c - 2) + q + 1)
                    n = 0
                    for k in range(DK):
                        for a, w in ((a_hi, wih_hi), (a_hi, wih_lo), (a_lo, wih_hi)):
                            last = pe.matmul(bank[3 * s + q][0:R, :], a[:, s, k * R:(k + 1) * R],
                                             w[:, k, q * D:(q + 1) * D], start=n == 0, stop=n == 3 * DK - 1)
                            n += 1
                    last.then_inc(g_prod, 1)

            transposes(0, 0, 0)
            transposes(1, 1, 0)
            product(0, 0)

            def pair(i):
                transposes(2 * i, 0, i)
                product(2 * i - 1, 1)
                transposes(2 * i + 1, 1, i)
                product(2 * i, 0)

            pair(1)
            with pe.Fori(2, EC // 2) as i:
                pair(i)
            product(EC - 1, 1)

    cursor[0] = region_b
    node_slot = place("node_slot", [R, NT], I32)
    slot_at = place("slot_at", [R, 2], I32)
    xt = place("xt", [R, 2, D])
    h = place("h", [R, 2, D])
    x_h = place("x_h", [R, 2, D])
    x_h_b = place("x_h_b", [R, 2, D])
    h_hi = place("h_hi", [P, 2, DK * R], F32R)
    h_lo = place("h_lo", [P, 2, DK * R], F32R)
    gates = place("gates", [R, 2, G3])
    hn_raw = place("hn_raw", [R, 2, D])
    hn = place("hn", [R, 2, D])
    r_pre = place("r_pre", [R, D])
    r_gate = place("r_gate", [R, D])
    z_pre = place("z_pre", [R, D])
    z_gate = place("z_gate", [R, D])
    r_hn = place("r_hn", [R, D])
    n_pre = place("n_pre", [R, D])
    n_gate = place("n_gate", [R, 2, D])
    h_n = place("h_n", [R, D])
    z_h_n = place("z_h_n", [R, D])
    h_new = place("h_new", [R, D])
    scaled = place("scaled", [R, D])
    x1 = place("x1", [R, 2, D])
    h2 = place("h2", [R, 2, D])
    h2_hi = place("h2_hi", [P, DK * R], F32R)
    h2_lo = place("h2_lo", [P, DK * R], F32R)
    f1 = place("f1", [R, F1])
    hid = place("hid", [R, 2, KF * P])
    hid_hi = place("hid_hi", [P, KF * R], F32R)
    hid_lo = place("hid_lo", [P, KF * R], F32R)
    y = place("y", [R, 2, D])
    st = {k: place(f"st{k}", [R, 6]) for k in (1, 2)}
    mv = {k: place(f"mv{k}", [R, 2]) for k in (1, 2)}
    var_eps = {k: place(f"var_eps{k}", [R, 1]) for k in (1, 2)}
    neg_mean = {k: place(f"neg_mean{k}", [R, 1]) for k in (1, 2)}
    rstd = {k: place(f"rstd{k}", [R, 2]) for k in (1, 2)}
    shift = {k: place(f"shift{k}", [R, 2]) for k in (1, 2)}
    one_rstd = place("one_rstd", [R, 2])
    top = place("top", [R, 8])
    top_i = place("top_i", [R, 8], U32)
    top_f = place("top_f", [R, 2])
    gap = place("gap", [R, 1])
    weight = place("weight", [R, 2])
    comb1 = place("comb1", [R, NE])
    comb2 = place("comb2", [R, NE])
    assert cursor[0] <= nc.sbuf_usable_end, (cursor[0], nc.sbuf_usable_end)

    b_r, b_z, b_n, b_th, b_th2, b_thid, b_f1, b_f2 = bank

    table_in = sem("table_in")
    hid_set = sem("hid_set")
    x_in = [sem("x_in0"), sem("x_in1")]
    slot_copied = sem("slot_copied")
    gates_loaded = [sem("gates_loaded0"), sem("gates_loaded1")]
    st_done = {k: sem(f"st_done{k}") for k in (1, 2)}
    mv_done = {k: sem(f"mv_done{k}") for k in (1, 2)}
    var_done = {k: sem(f"var_done{k}") for k in (1, 2)}
    rstd_done = {k: sem(f"rstd_done{k}") for k in (1, 2)}
    shift_done = {k: sem(f"shift_done{k}") for k in (1, 2)}
    h_done = sem("h_done")
    x_h_done = sem("x_h_done")
    x_h_b_done = sem("x_h_b_done")
    h_turned = sem("h_turned")
    h_hi_done = sem("h_hi_done")
    h_lo_done = sem("h_lo_done")
    n_prod = sem("n_prod")
    r_prod = sem("r_prod")
    z_prod = sem("z_prod")
    hn_raw_done = sem("hn_raw_done")
    hn_done = sem("hn_done")
    r_pre_done = sem("r_pre_done")
    r_done = sem("r_done")
    z_pre_done = sem("z_pre_done")
    z_done = sem("z_done")
    r_hn_done = sem("r_hn_done")
    n_pre_done = sem("n_pre_done")
    n_done = sem("n_done")
    h_n_done = sem("h_n_done")
    z_h_n_done = sem("z_h_n_done")
    h_new_done = sem("h_new_done")
    scaled_done = sem("scaled_done")
    x1_done = sem("x1_done")
    h2_done = sem("h2_done")
    h2_turned = sem("h2_turned")
    h2_hi_done = sem("h2_hi_done")
    h2_lo_done = sem("h2_lo_done")
    f1_prod = sem("f1_prod")
    f1_done = sem("f1_done")
    top_done = sem("top_done")
    top_i_done = sem("top_i_done")
    gap_done = sem("gap_done")
    weight_done = sem("weight_done")
    comb1_done = sem("comb1_done")
    comb2_done = sem("comb2_done")
    comb_done = sem("comb_done")
    hid_done = sem("hid_done")
    hid_turned = sem("hid_turned")
    hid_hi_done = sem("hid_hi_done")
    hid_lo_done = sem("hid_lo_done")
    f2_prod = sem("f2_prod")
    y_done = sem("y_done")
    y_stored = [sem("y_stored0"), sem("y_stored1")]

    x_tiles = x.rearrange("(p t) d -> p t d", t=NT)
    out_tiles = out.rearrange("(p t) d -> p t d", t=NT)

    FIRST = 4
    LOOPS = (NT - 2 - FIRST) // 2

    class Period:
        def __init__(self, i, j):
            self.i, self.j = i, j
            self.t = FIRST + 2 * i + j

        def has(self, k):
            return not isinstance(self.i, int) or 0 <= self.t + k < NT

        def slot(self, k):
            return (self.j + k) % 2

        def turn(self, k):
            return self.i + (FIRST + self.j + k - self.slot(k)) // 2

    def periods(eng, body):
        for j in range(-FIRST - 2, 0):
            body(Period(0, j))
        with eng.Fori(0, LOOPS) as i:
            for j in range(2):
                body(Period(i, j))
        for j in range(4):
            body(Period(LOOPS, j))

    with nc.Block() as block:
        @block.sync
        def _(sp):
            sp.dma_start(node_slot[:, :], slot_of_node.rearrange("(p t) o -> p (t o)", t=NT)).then_inc(table_in, 16)

            def body(p):
                t = p.t
                if not isinstance(p.i, int):
                    tile_x, tile_y = sp.snap(t + 2), sp.snap(t - 2)
                else:
                    tile_x, tile_y = t + 2, t - 2
                if p.has(2):
                    s = p.slot(2)
                    wait_from(sp, x_h_done, t + 1)
                    sp.dma_start(xt[:, s, :], x_tiles[:, bass.ds(tile_x, 1), :].rearrange("p o d -> p (o d)"))\
                        .then_inc(x_in[s], 16)
                if p.has(-2):
                    s = p.slot(-2)
                    sp.wait_ge(y_done, t - 1)
                    sp.dma_start(out_tiles[:, bass.ds(tile_y, 1), :].rearrange("p o d -> p (o d)"), y[:, s, :])\
                        .then_inc(y_stored[s], 16)

            periods(sp, body)
            for s in range(2):
                sp.wait_ge(y_stored[s], 16 * (NT // 2))

        @block.gpsimd
        def _(pool):
            for s in range(2):
                pool.memset(hid[:, s, F1:KF * P], 0.0).then_inc(hid_set, 1)
            pool.wait_ge(hid_set, 2)
            for s in range(2):
                pool.memset(hid[:, s, F1:F1 + 1], 0.5).then_inc(hid_set, 1)
            pool.wait_ge(table_in, 16)

            def gather(p, k):
                s, t = p.slot(k), p.t
                pool.tensor_copy(slot_at[:, s:s + 1], node_slot[:, bass.ds(t + k, 1)]).then_inc(slot_copied, 1)
                pool.wait_ge(slot_copied, t + k + 1).then_inc(held["pool"], 1)
                pool.indirect_dma_start(out=gates[:, s, :], out_offset=None, in_=gates_in,
                                        in_offset=bass.IndirectOffsetOnAxis(ap=slot_at[:, s:s + 1], axis=0),
                                        ).then_inc(gates_loaded[s], 16)

            def norm(p, k, which):
                s = p.slot(k)
                pool.wait_ge(var_done[which], p.t + k + 1)
                pool.tensor_tensor(rstd[which][:, s:s + 1], var_eps[which][:, :], minus_half[:, 0:1], ALU.pow)\
                    .then_inc(rstd_done[which], 1)
                pool.wait_ge(rstd_done[which], p.t + k + 1)
                pool.tensor_tensor(shift[which][:, s:s + 1], neg_mean[which][:, :], rstd[which][:, s:s + 1], ALU.mult)\
                    .then_inc(shift_done[which], 1)
                if which == 1:
                    pool.tensor_tensor(one_rstd[:, s:s + 1], rstd[1][:, s:s + 1], ones_col[:, 0:1], ALU.add)\
                        .then_inc(shift_done[which], 1)

            def body(p):
                t = p.t
                if p.has(-1):
                    norm(p, -1, 2)
                if p.has(0):
                    s = p.slot(0)
                    pool.wait_ge(hn_raw_done, t + 1)
                    wait_from(pool, r_hn_done, t - 1)
                    pool.tensor_tensor(hn[:, s, :], hn_raw[:, s, :], hn_bias[:, :], ALU.add).then_inc(hn_done, 1)
                if p.has(1):
                    s = p.slot(1)
                    pool.wait_ge(x_h_done, t + 2)
                    wait_from(pool, x1_done, t)
                    pool.tensor_tensor(x_h_b[:, s, :], x_h[:, s, :], bn_shift[:, :], ALU.add).then_inc(x_h_b_done, 1)
                if p.has(0):
                    s = p.slot(0)
                    pool.wait_ge(r_done, t + 1)
                    pool.wait_ge(hn_done, t + 1)
                    pool.tensor_tensor(r_hn[:, :], r_gate[:, :], hn[:, s, :], ALU.mult).then_inc(r_hn_done, 1)
                    wait_from(pool, n_done, t)
                    pool.wait_ge(gates_loaded[s], 16 * (p.turn(0) + 1))
                    pool.wait_ge(r_hn_done, t + 1)
                    pool.tensor_tensor(n_pre[:, :], r_hn[:, :], gates[:, s, 2 * D:G3], ALU.add).then_inc(n_pre_done, 1)
                if p.has(2):
                    if p.has(0):
                        pool.wait_ge(n_pre_done, t + 1)
                        pool.wait_ge(r_pre_done, t + 1)
                        pool.wait_ge(z_pre_done, t + 1).then_inc(held["pool"], 1)
                    gather(p, 2)
                    norm(p, 2, 1)
                if p.has(0):
                    s = p.slot(0)
                    pool.wait_ge(n_done, t + 1)
                    wait_from(pool, z_h_n_done, t)
                    pool.tensor_tensor(h_n[:, :], h[:, s, :], n_gate[:, s, :], ALU.subtract).then_inc(h_n_done, 1)

            periods(pool, body)

        @block.scalar
        def _(act):
            def body(p):
                t = p.t
                if p.has(1):
                    s = p.slot(1)
                    act.wait_ge(shift_done[1], 2 * (t + 2))
                    wait_from(act, h_n_done, t)
                    act.activation(h[:, s, :], xt[:, s, :], ACT.Identity, bias=shift[1][:, s:s + 1],
                                   scale=rstd[1][:, s:s + 1]).then_inc(h_done, 1)
                    wait_from(act, x_h_b_done, t)
                    act.activation(x_h[:, s, :], xt[:, s, :], ACT.Identity, bias=shift[1][:, s:s + 1],
                                   scale=one_rstd[:, s:s + 1]).then_inc(x_h_done, 1)
                if p.has(0):
                    s = p.slot(0)
                    act.wait_ge(n_prod, t + 1)
                    wait_from(act, hn_done, t - 1)
                    act.activation(hn_raw[:, s, :], b_n[0:R, :], ACT.Copy).then_inc(hn_raw_done, 1)
                if p.has(-1):
                    s = p.slot(-1)
                    act.wait_ge(shift_done[2], t)
                    wait_from(act, h2_turned, t - 2)
                    act.activation(h2[:, s, :], x1[:, s, :], ACT.Identity, bias=shift[2][:, s:s + 1],
                                   scale=rstd[2][:, s:s + 1]).then_inc(h2_done, 1)
                if p.has(0):
                    act.wait_ge(r_pre_done, t + 1)
                    wait_from(act, r_hn_done, t)
                    act.activation(r_gate[:, :], r_pre[:, :], ACT.Sigmoid).then_inc(r_done, 1)
                if p.has(-2):
                    act.wait_ge(hid_turned, t - 1)
                    wait_from(act, f2_prod, t - 2)
                    act.activation(hid_hi[:, :], b_thid[:, 0:KF * R], ACT.Copy).then_inc(hid_hi_done, 1)
                if p.has(-1):
                    act.wait_ge(h2_turned, t)
                    wait_from(act, f1_prod, t - 1)
                    act.activation(h2_hi[:, :], b_th2[:, 0:DK * R], ACT.Copy).then_inc(h2_hi_done, 1)
                if p.has(1):
                    s = p.slot(1)
                    act.wait_ge(h_turned, t + 2)
                    wait_from(act, z_prod, t)
                    act.activation(h_hi[:, s, :], b_th[:, 0:DK * R], ACT.Copy).then_inc(h_hi_done, 1)
                if p.has(0):
                    s = p.slot(0)
                    act.wait_ge(n_pre_done, t + 1)
                    wait_from(act, h_new_done, t - 1)
                    act.activation(n_gate[:, s, :], n_pre[:, :], ACT.Tanh).then_inc(n_done, 1)
                    act.wait_ge(z_pre_done, t + 1)
                    wait_from(act, z_h_n_done, t)
                    act.activation(z_gate[:, :], z_pre[:, :], ACT.Sigmoid).then_inc(z_done, 1)
                if p.has(-1):
                    act.wait_ge(gap_done, t)
                    wait_from(act, comb2_done, t - 1)
                    act.activation(weight[:, 0:1], gap[:, :], ACT.Sigmoid).then_inc(weight_done, 1)
                    act.activation(weight[:, 1:2], gap[:, :], ACT.Sigmoid, scale=-1.0).then_inc(weight_done, 1)

            periods(act, body)

        @block.vector
        def _(dve):
            dve.wait_ge(hid_set, 4)

            def norm_stats(p, k, which, rows_of):
                t = p.t
                dve.bn_stats(st[which][:, :], rows_of).then_inc(st_done[which], 1)
                dve.wait_ge(st_done[which], t + k + 1).then_inc(held["dve"], 1)
                dve.bn_aggr(mv[which][:, :], st[which][:, :]).then_inc(mv_done[which], 1)
                dve.wait_ge(mv_done[which], t + k + 1)
                wait_from(dve, shift_done[which], (3 - which) * (t + k))
                dve.tensor_scalar(neg_mean[which][:, :], mv[which][:, 0:1], -1.0, None, ALU.mult)
                dve.tensor_scalar(var_eps[which][:, :], mv[which][:, 1:2], EPS, None, ALU.add)\
                    .then_inc(var_done[which], 1)

            def body(p):
                t = p.t
                if p.has(0):
                    s = p.slot(0)
                    dve.wait_ge(r_prod, t + 1)
                    dve.wait_ge(gates_loaded[s], 16 * (p.turn(0) + 1))
                    wait_from(dve, r_done, t)
                    dve.tensor_tensor(r_pre[:, :], b_r[0:R, :], gates[:, s, 0:D], ALU.add).then_inc(r_pre_done, 1)
                if p.has(-2):
                    dve.wait_ge(hid_hi_done, t - 1)
                    dve.tensor_tensor(hid_lo[:, :], b_thid[:, 0:KF * R], hid_hi[:, :].bitcast(F32), ALU.subtract)\
                        .then_inc(hid_lo_done, 1)
                if p.has(-1):
                    dve.wait_ge(h2_hi_done, t)
                    dve.tensor_tensor(h2_lo[:, :], b_th2[:, 0:DK * R], h2_hi[:, :].bitcast(F32), ALU.subtract)\
                        .then_inc(h2_lo_done, 1)
                if p.has(1):
                    s = p.slot(1)
                    dve.wait_ge(h_hi_done, t + 2)
                    dve.tensor_tensor(h_lo[:, s, :], b_th[:, 0:DK * R], h_hi[:, s, :].bitcast(F32), ALU.subtract)\
                        .then_inc(h_lo_done, 1)
                if p.has(0):
                    s = p.slot(0)
                    dve.wait_ge(z_prod, t + 1)
                    wait_from(dve, z_done, t)
                    dve.tensor_tensor(z_pre[:, :], b_z[0:R, :], gates[:, s, D:2 * D], ALU.add).then_inc(z_pre_done, 1)
                if p.has(2):
                    s = p.slot(2)
                    dve.wait_ge(x_in[s], 16 * (p.turn(2) + 1))
                    norm_stats(p, 2, 1, xt[:, s, :])
                if p.has(-2):
                    s = p.slot(-2)
                    dve.wait_ge(f2_prod, t - 1)
                    wait_from(dve, y_stored[s], 16 * p.turn(-2))
                    dve.tensor_tensor(y[:, s, :], b_f2[0:R, :], x1[:, s, :], ALU.add).then_inc(y_done, 1)
                if p.has(0):
                    s = p.slot(0)
                    dve.wait_ge(z_done, t + 1)
                    dve.wait_ge(h_n_done, t + 1)
                    dve.tensor_tensor(z_h_n[:, :], z_gate[:, :], h_n[:, :], ALU.mult).then_inc(z_h_n_done, 1)
                    dve.wait_ge(z_h_n_done, t + 1)
                    dve.tensor_tensor(h_new[:, :], z_h_n[:, :], n_gate[:, s, :], ALU.add).then_inc(h_new_done, 1)
                    dve.wait_ge(h_new_done, t + 1)
                    dve.tensor_tensor(scaled[:, :], h_new[:, :], bn_scale[:, :], ALU.mult).then_inc(scaled_done, 1)
                    dve.wait_ge(scaled_done, t + 1)
                    dve.wait_ge(x_h_b_done, t + 1)
                    dve.tensor_tensor(x1[:, s, :], scaled[:, :], x_h_b[:, s, :], ALU.add).then_inc(x1_done, 1)
                    dve.wait_ge(x1_done, t + 1)
                    norm_stats(p, 0, 2, x1[:, s, :])
                if p.has(-1):
                    s = p.slot(-1)
                    dve.wait_ge(f1_prod, t)
                    dve.tensor_tensor(f1[:, :], b_f1[0:R, 0:F1], f1_bias[:, :], ALU.add).then_inc(f1_done, 1)
                    dve.wait_ge(f1_done, t).then_inc(held["dve"], 1)
                    dve.max(top[:, :], f1[:, 0:NE]).then_inc(top_done, 1)
                    dve.wait_ge(top_done, t)
                    wait_from(dve, weight_done, 2 * (t - 1))
                    dve.tensor_tensor(gap[:, :], top[:, 0:1], top[:, 1:2], ALU.subtract).then_inc(gap_done, 1)
                    dve.max_index(top_i[:, :], top[:, :], f1[:, 0:NE]).then_inc(top_i_done, 1)
                    dve.wait_ge(top_i_done, t)
                    dve.tensor_copy(top_f[:, :], top_i[:, 0:2]).then_inc(comb1_done, 1)
                    dve.wait_ge(weight_done, 2 * t)
                    dve.wait_ge(comb1_done, 2 * t - 1)
                    dve.tensor_scalar(comb1[:, :], iota8[:, :], top_f[:, 0:1], weight[:, 0:1], ALU.is_equal, ALU.mult)\
                        .then_inc(comb1_done, 1)
                    dve.tensor_scalar(comb2[:, :], iota8[:, :], top_f[:, 1:2], weight[:, 1:2], ALU.is_equal, ALU.mult)\
                        .then_inc(comb2_done, 1)
                    dve.wait_ge(comb1_done, 2 * t)
                    dve.wait_ge(comb2_done, t)
                    wait_from(dve, hid_turned, t - 2)
                    dve.tensor_tensor(hid[:, s, HE + HS:F1], comb1[:, :], comb2[:, :], ALU.add).then_inc(comb_done, 1)
                    dve.tensor_scalar(hid[:, s, HE:HE + HS], f1[:, NE + HE:F1], 0.0, 0.5, ALU.max, ALU.mult)
                    dve.wait_ge(comb_done, t)
                    dve.scalar_tensor_tensor(
                        hid[:, s, 0:HE].rearrange("p (e f) -> p e f", e=NE),
                        f1[:, NE:NE + HE].rearrange("p (e f) -> p e f", e=NE), 0.0,
                        hid[:, s, HE + HS:F1].unsqueeze(2).broadcast_to((R, NE, HF)), ALU.max, ALU.mult)\
                        .then_inc(hid_done, 1)

            periods(dve, body)

        @block.tensor
        def _(pe):
            pe.wait_ge(hid_set, 4)

            def gate(s, to, q):
                n = 0
                for k in range(DK):
                    for a, w in ((h_hi, whh_hi), (h_hi, whh_lo), (h_lo, whh_hi)):
                        last = pe.matmul(to[0:R, :], a[:, s, k * R:(k + 1) * R], w[:, k, q * D:(q + 1) * D],
                                         start=n == 0, stop=n == 3 * DK - 1)
                        n += 1
                return last

            def turn(to, rows_of, chunks):
                for k in range(chunks):
                    last = pe.transpose(to[:, k * R:(k + 1) * R], rows_of[:, k * P:(k + 1) * P], ident[0:R, 0:R])
                return last

            def body(p):
                t = p.t
                if p.has(0):
                    s = p.slot(0)
                    pe.wait_ge(h_lo_done, t + 1)
                    wait_from(pe, hn_raw_done, t)
                    gate(s, b_n, 2).then_inc(n_prod, 1)
                    wait_from(pe, r_pre_done, t)
                    gate(s, b_r, 0).then_inc(r_prod, 1)
                if p.has(-2):
                    pe.wait_ge(hid_done, t - 1)
                    wait_from(pe, hid_lo_done, t - 2)
                    turn(b_thid, hid[:, p.slot(-2), :], KF).then_inc(hid_turned, 1)
                if p.has(-1):
                    pe.wait_ge(h2_done, t)
                    wait_from(pe, h2_lo_done, t - 1)
                    turn(b_th2, h2[:, p.slot(-1), :], DK).then_inc(h2_turned, 1)
                if p.has(1):
                    pe.wait_ge(h_done, t + 2)
                    wait_from(pe, h_lo_done, t + 1)
                    turn(b_th, h[:, p.slot(1), :], DK).then_inc(h_turned, 1)
                if p.has(0):
                    wait_from(pe, z_pre_done, t)
                    gate(p.slot(0), b_z, 1).then_inc(z_prod, 1)
                if p.has(-2):
                    pe.wait_ge(hid_lo_done, t - 1)
                    wait_from(pe, y_done, t - 2)
                    n = 0
                    for k in range(KF):
                        for a, w in ((hid_hi, f2_hi), (hid_hi, f2_lo), (hid_lo, f2_hi)):
                            last = pe.matmul(b_f2[0:R, :], a[:, k * R:(k + 1) * R], w[:, k, :],
                                             start=n == 0, stop=n == 3 * KF - 1)
                            n += 1
                    last.then_inc(f2_prod, 1)
                if p.has(-1):
                    pe.wait_ge(h2_lo_done, t)
                    wait_from(pe, f1_done, t - 1)
                    n = 0
                    for k in range(DK):
                        for a, w in ((h2_hi, f1_hi), (h2_hi, f1_lo), (h2_lo, f1_hi)):
                            last = pe.matmul(b_f1[0:R, 0:F1], a[:, k * R:(k + 1) * R], w[:, k, :],
                                             start=n == 0, stop=n == 3 * DK - 1)
                            n += 1
                    last.then_inc(f1_prod, 1)

            periods(pe, body)


def kernel(x, src, dst, edge_attr_128, L0_gnn_W1, L0_gnn_b1, L0_gnn_W2, L0_gnn_b2, L0_gnn_W_ih, L0_gnn_W_hh,
           L0_gnn_b_ih, L0_gnn_b_hh, L0_gnn_gamma, L0_gnn_beta, L0_gnn_run_mean, L0_gnn_run_var, L0_ffn_Wg,
           L0_ffn_bg, L0_ffn_W1, L0_ffn_b1, L0_ffn_W2, L0_ffn_b2, L0_ffn_Ws1, L0_ffn_bs1, L0_ffn_Ws2, L0_ffn_bs2):
    import numpy as np
    import concourse.bacc as bacc
    from concourse.bass_utils import run_bass_kernel_spmd

    rows, edge_tiles, sup = 125, 20, 4
    src, dst, attr = np.asarray(src), np.asarray(dst), np.asarray(edge_attr_128)
    w1, w2 = np.asarray(L0_ffn_W1), np.asarray(L0_ffn_W2)
    by_row = dst.reshape(rows, edge_tiles)
    arrays = dict(
        x=x, src=src.reshape(rows, edge_tiles), dst=by_row,
        dst_rows=by_row.T.reshape(edge_tiles // sup, sup * rows),
        attr_t=attr.reshape(rows, edge_tiles, -1).transpose(2, 1, 0).reshape(attr.shape[1], -1),
        w1t=np.asarray(L0_gnn_W1).T, b1=np.asarray(L0_gnn_b1).reshape(-1, 128).T, w2t=np.asarray(L0_gnn_W2).T, b2=L0_gnn_b2,
        wih_t=np.asarray(L0_gnn_W_ih).T, whh_t=np.asarray(L0_gnn_W_hh).T, b_ih=L0_gnn_b_ih, b_hh=L0_gnn_b_hh,
        gamma=L0_gnn_gamma, beta=L0_gnn_beta, run_mean=L0_gnn_run_mean, run_var=L0_gnn_run_var,
        wg=L0_ffn_Wg, bg=L0_ffn_bg, ew1=w1.transpose(1, 0, 2).reshape(w1.shape[1], -1),
        eb1=np.asarray(L0_ffn_b1).reshape(-1), ew2=w2.reshape(-1, w2.shape[2]), eb2=L0_ffn_b2,
        ws1=L0_ffn_Ws1, bs1=L0_ffn_bs1, ws2=L0_ffn_Ws2, bs2=L0_ffn_bs2)
    arrays = {f"in_{k}": np.ascontiguousarray(v) for k, v in arrays.items()}
    nc = bacc.Bacc("TRN2", target_bir_lowering=False, num_devices=1)
    args = [nc.dram_tensor(k, v.shape, mybir.dt.from_np(v.dtype), kind="ExternalInput").ap()
            for k, v in arrays.items()]
    out = nc.dram_tensor("out", tuple(np.asarray(x).shape), F32, kind="ExternalOutput").ap()
    gnn_ffn(nc, *args, out)
    result = run_bass_kernel_spmd(nc, [arrays], core_ids=[0])
    return result.results[0]["out"]
```

```python
import concourse.bass as bass
from concourse import mybir

F32 = mybir.dt.float32
F32R = mybir.dt.float32r
I32 = mybir.dt.int32
U32 = mybir.dt.uint32
ALU = mybir.AluOpType
ACT = mybir.ActivationFunctionType
AX_X = mybir.AxisListType.X

P = 128
EPS = 1e-5


def gnn_ffn(nc, x, src, dst, dst_rows, attr_t, w1t, b1, w2t, b2, wih_t, whh_t, b_ih, b_hh, gamma, beta,
            run_mean, run_var, wg, bg, ew1, eb1, ew2, eb2, ws1, bs1, ws2, bs2, out):
    N, D = x.shape
    R, EC = src.shape
    NT = N // R
    E = R * EC
    DK = D // P
    K1 = w1t.shape[0] // P
    G3 = 3 * D
    NE = wg.shape[1]
    HE = ew1.shape[1]
    HS = ws1.shape[1]
    HF = HE // NE
    F1 = NE + HE + HS
    KF = 3
    SUP = 4
    NSUP = EC // SUP
    SW = SUP * R
    GE = (EC + 7) // 8
    assert N == R * NT and EC == SUP * NSUP and HE == 2 * P and NT % 2 == 0

    agg = nc.dram_tensor("agg", (E + R, D), F32, kind="Internal").ap()
    gates_in = nc.dram_tensor("gates_in", (E + R, G3), F32, kind="Internal").ap()
    bn_rows = nc.dram_tensor("bn_rows", (2, D), F32, kind="Internal").ap()
    slot_of_node = nc.dram_tensor("slot_of_node", (N, 1), I32, kind="Internal").ap()

    cursor = [(nc.sbuf_base + 63) // 64 * 64]

    def place(name, shape, dt=F32):
        size = 4
        for n in shape[1:]:
            size *= n
        at = cursor[0]
        cursor[0] = (at + size + 31) // 32 * 32
        return nc.alloc_sbuf_tensor_at(name, list(shape), dt, offset=at)

    ident = place("ident", [P, P])
    f1_hi = place("f1_hi", [P, DK, F1], F32R)
    f1_lo = place("f1_lo", [P, DK, F1], F32R)
    f2_hi = place("f2_hi", [P, KF, D], F32R)
    f2_lo = place("f2_lo", [P, KF, D], F32R)
    bn_scale = place("bn_scale", [R, D])
    bn_shift = place("bn_shift", [R, D])
    hn_bias = place("hn_bias", [R, D])
    f1_bias = place("f1_bias", [R, F1])
    minus_half = place("minus_half", [P, SUP])
    ones_col = place("ones_col", [R, SUP])
    iota8 = place("iota8", [R, NE])
    region_a = cursor[0]
    whh_hi = place("whh_hi", [P, DK, G3], F32R)
    whh_lo = place("whh_lo", [P, DK, G3], F32R)
    region_b = cursor[0]

    bank = [nc.alloc_psum_tensor(f"bank{k}", [P, 512], F32) for k in range(8)]

    def sem(name):
        return nc.alloc_semaphore(name)

    def wait_from(eng, s, n):
        if not isinstance(n, int) or n > 0:
            eng.wait_ge(s, n)

    held = {e: sem(f"held_{e}") for e in ("pool", "dve")}

    cursor[0] = region_a
    w1_hi = place("w1_hi", [P, K1, D], F32R)
    w1_lo = place("w1_lo", [P, K1, D], F32R)
    w2_hi = place("w2_hi", [P, DK, D], F32R)
    w2_lo = place("w2_lo", [P, DK, D], F32R)
    hs = place("hs", [R, SUP, D])
    msg = place("msg", [R, D])
    b2_row = place("b2_row", [R, D])
    cursor[0] = max(cursor[0], region_b)
    wih_hi = place("wih_hi", [P, DK, G3], F32R)
    wih_lo = place("wih_lo", [P, DK, G3], F32R)
    dst_i = place("dst_i", [R, EC], I32)
    slot_i = place("slot_i", [R, EC], I32)
    region_c = cursor[0]
    src_i = place("src_i", [R, EC], I32)
    dst_f = place("dst_f", [R, GE * 8])
    row_i = place("row_i", [R, SUP * R], I32)
    iota_row = place("iota_row", [R, R])
    node_init = place("node_init", [R, NT], I32)
    bn_cols = place("bn_cols", [P, 4, DK])
    b1_col = place("b1_col", [P, DK])
    src_at = place("src_at", [R, SUP], I32)
    stage = place("stage", [P, 2, G3])
    xs = place("xs", [R, SUP, D])
    st_e = place("st_e", [R, SUP, 6])
    mv_e = place("mv_e", [R, SUP, 2])
    ve_e = place("ve_e", [R, SUP])
    nm_e = place("nm_e", [R, SUP])
    rs_e = place("rs_e", [R, SUP])
    nmr_e = place("nmr_e", [R, SUP])
    attr = place("attr", [P, SW])
    m_hi_t = place("m_hi_t", [P, K1, SW], F32R)
    m_lo_t = place("m_lo_t", [P, K1, SW], F32R)
    r32 = place("r32", [P, 2, SW])
    r_hi = place("r_hi", [P, DK, SW], F32R)
    r_lo = place("r_lo", [P, DK, SW], F32R)
    msg_hi = place("msg_hi", [R, 2, D], F32R)
    msg_lo = place("msg_lo", [R, D], F32R)
    same = place("same", [R, 2, R], F32R)
    trash = place("trash", [R, 1])
    row_no = place("row_no", [R, 1])
    sums = place("sums", [R, SUP, D])
    top_row = place("top_row", [R, EC])
    is_top = place("is_top", [R, EC])
    found = place("found", [R, GE * 8], U32)
    found_f = place("found_f", [R, GE * 8])
    paired = place("paired", [R, GE, 8, 8])
    first = place("first", [R, GE * 8])
    slot_f = place("slot_f", [R, EC])
    add_all = place("add_all", [R, EC], I32)
    add_at = place("add_at", [R, SUP], I32)
    assert cursor[0] <= nc.sbuf_usable_end, (cursor[0], nc.sbuf_usable_end)
    all_size = (4 * E + 31) // 32 * 32
    assert 2 * all_size + 4 * D <= 4 * DK * G3
    all_same = nc.alloc_sbuf_tensor_at("all_same", [R, EC, R], F32, offset=region_b)
    all_dst_i = nc.alloc_sbuf_tensor_at("all_dst_i", [R, E], I32, offset=region_b)
    all_dst = nc.alloc_sbuf_tensor_at("all_dst", [R, EC, R], F32, offset=region_b + all_size)
    zeros = nc.alloc_sbuf_tensor_at("zeros", [R, D], F32, offset=region_b + 2 * all_size)

    small_in = sem("small_in")
    b1_in = sem("b1_in")
    b2_in = sem("b2_in")
    dst_in = sem("dst_in")
    agg_init = sem("agg_init")
    all_used = sem("all_used")
    iotas = sem("iotas")
    consts = sem("consts")
    bn_in = sem("bn_in")
    bn_step = sem("bn_step")
    bn_out = sem("bn_out")
    bn_back = sem("bn_back")
    staged = [sem("staged0"), sem("staged1")]
    stage_hi = sem("stage_hi")
    stage_lo = sem("stage_lo")
    attr_in = sem("attr_in")
    row_in = sem("row_in")
    dst_f_done = sem("dst_f_done")
    table_init = sem("table_init")
    src_ready = sem("src_ready")
    xs_in = [sem(f"xs_in{j}") for j in range(SUP)]
    stats_e = sem("stats_e")
    mv_ready = sem("mv_ready")
    var_e = sem("var_e")
    rs_ready = sem("rs_ready")
    nmr_ready = sem("nmr_ready")
    h_e = sem("h_e")
    t_e = sem("t_e")
    t_hi = sem("t_hi")
    t_lo = sem("t_lo")
    l1 = sem("l1")
    relu_done = sem("relu_done")
    r_hi_done = sem("r_hi_done")
    r_lo_done = sem("r_lo_done")
    l2 = sem("l2")
    msg_done = sem("msg_done")
    msg_hi_done = sem("msg_hi_done")
    msg_lo_done = sem("msg_lo_done")
    same_done = sem("same_done")
    summed = sem("summed")
    sums_done = sem("sums_done")
    all_dst_in = sem("all_dst_in")
    top_step = sem("top_step")
    add_all_ready = sem("add_all_ready")
    add_at_ready = sem("add_at_ready")
    scattered = sem("scattered")

    w1v = w1t.rearrange("(k p) n -> p k n", p=P)
    w2v = w2t.rearrange("(k p) n -> p k n", p=P)
    wihv = wih_t.rearrange("(k p) n -> p k n", p=P)
    ew1v = ew1.rearrange("(k p) n -> p k n", p=P)
    ew2v = ew2.rearrange("(k p) n -> p k n", p=P)
    wgv = wg.rearrange("(k p) n -> p k n", p=P)
    ws1v = ws1.rearrange("(k p) n -> p k n", p=P)
    FW = KF - 1

    def wide(w, a, b, hi, lo, n):
        return [(lambda s: s[:, 0:(b - a) * n].rearrange("p (k n) -> p k n", n=n), w[:, a:b, :])], \
            (b - a) * n, hi[:, a:b, :], lo[:, a:b, :], n

    loads = [wide(w1v, 0, 3, w1_hi, w1_lo, D), wide(w1v, 3, 5, w1_hi, w1_lo, D),
             wide(w2v, 0, 3, w2_hi, w2_lo, D), wide(w2v, 3, 4, w2_hi, w2_lo, D)]
    loads += [wide(wihv, k, k + 1, wih_hi, wih_lo, G3) for k in range(DK)]
    loads += [([
        (lambda s: s[:, 0:DK * F1].rearrange("p (k n) -> p k n", n=F1)[:, :, 0:NE], wgv),
        (lambda s: s[:, 0:DK * F1].rearrange("p (k n) -> p k n", n=F1)[:, :, NE:NE + HE], ew1v),
        (lambda s: s[:, 0:DK * F1].rearrange("p (k n) -> p k n", n=F1)[:, :, NE + HE:F1], ws1v)],
        DK * F1, f1_hi[:, :, :], f1_lo[:, :, :], F1)]
    loads += [([
        (lambda s: s[:, 0:FW * D].rearrange("p (k n) -> p k n", n=D), ew2v),
        (lambda s: s[0:HS, FW * D:KF * D], ws2),
        (lambda s: s[HS:HS + NE, FW * D:KF * D], eb2),
        (lambda s: s[HS + NE:HS + NE + 1, FW * D:KF * D], bs2.rearrange("(o n) -> o n", o=1))],
        KF * D, f2_hi[:, :, :], f2_lo[:, :, :], D)]
    F2_LOAD = len(loads) - 1

    landed = []
    tally = [0, 0]
    for n, ld in enumerate(loads):
        tally[n % 2] += 16 * len(ld[0])
        landed.append(tally[n % 2])
    W1_LOADS, W2_LOADS = 2, 4

    rows_of_biases = [
        (hn_bias[:, :], b_hh[2 * D:G3]),
        (f1_bias[:, 0:NE], bg), (f1_bias[:, NE:NE + HE], eb1), (f1_bias[:, NE + HE:F1], bs1),
    ]

    def bcast(v):
        return v.rearrange("(o n) -> o n", o=1).broadcast_to((R, v.shape[0]))

    with nc.Block() as block:
        @block.sync
        def _(sp):
            sp.dma_start(src_i[:, :], src).then_inc(small_in, 16)
            for n in range(2):
                for to, of in loads[n][0]:
                    sp.dma_start(to(stage[:, n % 2, :]), of).then_inc(staged[n % 2], 16)
                if n == 0:
                    sp.dma_start(attr[:, :], attr_t[:, 0:SW]).then_inc(attr_in, 16)
            sp.dma_start(b1_col[:, :], b1).then_inc(b1_in, 16)
            sp.dma_start(dst_i[:, :], dst).then_inc(dst_in, 16)
            sp.dma_start(all_dst_i[:, :],
                         dst_rows.rearrange("(o g) r -> o (g r)", o=1).broadcast_to((R, E))).then_inc(all_dst_in, 16)
            sp.dma_start(row_i[:, :], dst_rows[0:1, :].broadcast_to((R, SW))).then_inc(row_in, 16)
            sp.dma_start(b2_row[:, :], bcast(b2)).then_inc(b2_in, 16)
            for n, of in enumerate((gamma, beta, run_mean, run_var)):
                sp.dma_start(bn_cols[:, n, :], of.rearrange("(p k) -> p k", p=P)).then_inc(bn_in, 16)

            def weights(a, b):
                for n in range(a, b):
                    sp.wait_ge(stage_lo, n - 1)
                    sp.wait_ge(stage_hi, n - 1)
                    if n == F2_LOAD:
                        sp.wait_ge(iotas, 8)
                    for to, of in loads[n][0]:
                        sp.dma_start(to(stage[:, n % 2, :]), of).then_inc(staged[n % 2], 16)

            def edge_inputs(g):
                at, gg = (g * SW, g) if isinstance(g, int) else (sp.snap(g * SW), sp.snap(g))
                sp.wait_ge(t_lo, g * (SUP + 1) - SUP)
                sp.dma_start(attr[:, :], attr_t[:, bass.ds(at, SW)]).then_inc(attr_in, 16)
                sp.wait_ge(same_done, SUP * g)
                sp.dma_start(row_i[:, :], dst_rows[bass.ds(gg, 1), :].broadcast_to((R, SW))).then_inc(row_in, 16)

            weights(2, 4)
            sp.wait_ge(iotas, 7)
            sp.dma_start(agg.rearrange("(p k) d -> p k d", p=R),
                         zeros[:, :].unsqueeze(1).broadcast_to((R, EC + 1, D))).then_inc(agg_init, 16)
            edge_inputs(1)
            sp.dma_start(slot_of_node.rearrange("(p t) o -> p (t o)", t=NT), node_init[:, :]).then_inc(table_init, 16)
            sp.wait_ge(bn_step, 5)
            sp.dma_start(bn_rows.rearrange("n (p k) -> p n k", p=P), bn_cols[:, 0:2, :]).then_inc(bn_out, 16)
            sp.wait_ge(bn_out, 16)
            for n, to in enumerate((bn_scale, bn_shift)):
                sp.dma_start(to[:, :], bn_rows[n:n + 1, :].broadcast_to((R, D))).then_inc(bn_back, 16)
            for to, of in rows_of_biases:
                sp.dma_start(to, bcast(of)).then_inc(bn_back, 16)
            sp.wait_ge(all_used, 1)
            sp.wait_ge(agg_init, 16)
            weights(4, 8)
            edge_inputs(2)
            weights(8, len(loads))
            with sp.Fori(3, NSUP) as g:
                edge_inputs(g)
            sp.wait_ge(table_init, 16)
            sp.wait_ge(bn_back, 16 * (2 + len(rows_of_biases)))

        @block.gpsimd
        def _(pool):
            pool.memset(zeros[:, :], 0.0).then_inc(iotas, 1)
            pool.iota(iota_row[:, :], pattern=[[1, R]], base=0, channel_multiplier=0,
                      allow_small_or_imprecise_dtypes=True).then_inc(iotas, 1)
            pool.iota(iota8[:, :], pattern=[[1, NE]], base=0, channel_multiplier=0,
                      allow_small_or_imprecise_dtypes=True).then_inc(iotas, 1)
            pool.memset(minus_half[:, :], -0.5).then_inc(iotas, 1)
            pool.iota(node_init[:, :], pattern=[[0, NT]], base=E, channel_multiplier=1).then_inc(iotas, 1)
            pool.iota(trash[:, :], pattern=[[0, 1]], base=E, channel_multiplier=1,
                      allow_small_or_imprecise_dtypes=True).then_inc(iotas, 1)
            pool.iota(row_no[:, :], pattern=[[0, 1]], base=0, channel_multiplier=1,
                      allow_small_or_imprecise_dtypes=True).then_inc(iotas, 1)
            pool.memset(ones_col[:, :], 1.0)
            pool.memset(ident[:, :], 0.0).then_inc(consts, 1)
            pool.wait_ge(consts, 1)
            pool.affine_select(out=ident[:, :], in_=ident[:, :], compare_op=ALU.not_equal, fill=1.0, base=0,
                               pattern=[[-1, P]], channel_multiplier=1).then_inc(consts, 1)

            def gather_sources(g):
                pool.tensor_copy(src_at[:, :], src_i[:, bass.ds(g * SUP, SUP)]).then_inc(src_ready, 1)
                pool.wait_ge(src_ready, g + 1).then_inc(held["pool"], 1)
                for j in range(SUP):
                    pool.indirect_dma_start(out=xs[:, j, :], out_offset=None, in_=x,
                                            in_offset=bass.IndirectOffsetOnAxis(ap=src_at[:, j:j + 1], axis=0),
                                            ).then_inc(xs_in[j], 16)

            pool.wait_ge(small_in, 16)
            gather_sources(0)

            def front(g1):
                pool.wait_ge(var_e, g1 + 1)
                pool.tensor_tensor(rs_e[:, :], ve_e[:, :], minus_half[0:R, :], ALU.pow).then_inc(rs_ready, 1)
                pool.wait_ge(rs_ready, g1 + 1)
                pool.tensor_tensor(nmr_e[:, :], nm_e[:, :], rs_e[:, :], ALU.mult).then_inc(nmr_ready, 1)

            def add(g, first, last):
                ready = [pool.snap(g * SUP + j + 1) for j in range(first, last)]
                written = [pool.snap(16 * (g * SUP + j + 1)) for j in range(first, last)]
                if first == 0:
                    copied = pool.snap(g + 1)
                    pool.tensor_copy(add_at[:, :], add_all[:, bass.ds(g * SUP, SUP)]).then_inc(add_at_ready, 1)
                    pool.wait_ge(add_at_ready, copied).then_inc(held["pool"], 1)
                for j in range(first, last):
                    pool.wait_ge(sums_done, ready[j - first]).then_inc(held["pool"], 1)
                    pool.indirect_dma_start(out=agg, in_=sums[:, j, :], in_offset=None,
                                            out_offset=bass.IndirectOffsetOnAxis(ap=add_at[:, j:j + 1], axis=0),
                                            compute_op=ALU.add).then_inc(scattered, 16)
                    pool.wait_ge(scattered, written[j - first]).then_inc(held["pool"], 1)

            front(0)
            pool.wait_ge(h_e, SUP)
            gather_sources(1)

            bn_gamma, bn_beta, bn_mean, bn_var = (bn_cols[:, n, :] for n in range(4))
            pool.wait_ge(bn_step, 1)
            pool.tensor_tensor(bn_var, bn_var, minus_half[:, :], ALU.pow).then_inc(bn_step, 1)
            pool.wait_ge(bn_step, 2)
            pool.tensor_tensor(bn_gamma, bn_gamma, bn_var, ALU.mult).then_inc(bn_step, 1)
            pool.wait_ge(bn_step, 3)
            pool.tensor_tensor(bn_mean, bn_mean, bn_gamma, ALU.mult).then_inc(bn_step, 1)
            pool.wait_ge(bn_step, 4)
            pool.tensor_tensor(bn_beta, bn_beta, bn_mean, ALU.subtract).then_inc(bn_step, 1)

            front(1)
            pool.wait_ge(h_e, 2 * SUP)
            gather_sources(2)
            pool.wait_ge(agg_init, 16)
            pool.wait_ge(add_all_ready, 3)
            add(0, 0, SUP - 1)
            with pool.Fori(1, NSUP - 2) as g:
                front(g + 1)
                pool.wait_ge(h_e, SUP * (g + 2)).then_inc(held["pool"], 1)
                gather_sources(g + 2)
                add(g - 1, SUP - 1, SUP)
                add(g, 0, SUP - 1)
            front(NSUP - 1)
            for g in (NSUP - 2, NSUP - 1):
                add(g - 1, SUP - 1, SUP)
                add(g, 0, SUP - 1)
            add(NSUP - 1, SUP - 1, SUP)

        @block.scalar
        def _(act):
            def split_hi(n):
                act.wait_ge(staged[n % 2], landed[n])
                _, width, hi, _, cols = loads[n]
                act.activation(hi, stage[:, n % 2, 0:width].rearrange("p (k n) -> p k n", n=cols), ACT.Copy)\
                    .then_inc(stage_hi, 1)

            def normalise(g1):
                act.wait_ge(nmr_ready, g1 + 1)
                if not isinstance(g1, int) or g1 > 0:
                    act.wait_ge(t_e, SUP * g1)
                for j in range(SUP):
                    act.activation(hs[:, j, :], xs[:, j, :], ACT.Identity, bias=nmr_e[:, j:j + 1],
                                   scale=rs_e[:, j:j + 1]).then_inc(h_e, 1)

            def attributes_hi(g1):
                wait_from(act, l1, DK * g1)
                act.wait_ge(attr_in, 16 * (g1 + 1))
                act.activation(m_hi_t[:, K1 - 1, :], attr[:, :], ACT.Copy).then_inc(t_hi, 1)

            def transposed_hi(g1, j):
                act.wait_ge(t_e, SUP * g1 + j + 1)
                act.activation(m_hi_t[:, 0:DK, j * R:(j + 1) * R],
                               bank[2 + j % 2][:, 0:DK * R].rearrange("p (k r) -> p k r", k=DK),
                               ACT.Copy).then_inc(t_hi, 1)

            def layer1(g, b):
                act.wait_ge(l1, DK * g + b + 1)
                wait_from(act, r_lo_done, DK * g + b - 1)
                act.activation(r32[:, b % 2, :], bank[b % 2][:, 0:SW], ACT.Relu, bias=b1_col[:, b:b + 1])\
                    .then_inc(relu_done, 1)
                act.wait_ge(relu_done, DK * g + b + 1)
                if b == 0:
                    wait_from(act, l2, SUP * g)
                act.activation(r_hi[:, b, :], r32[:, b % 2, :], ACT.Copy).then_inc(r_hi_done, 1)

            def take_sums(g, j):
                act.wait_ge(summed, SUP * g + j + 1)
                wait_from(act, scattered, 16 * (SUP * g + j - SUP + 1))
                act.activation(sums[:, j, :], bank[6 + j % 2][0:R, :], ACT.Copy).then_inc(sums_done, 1)

            def supertile(g, first, last, more):
                layer1(g, 0)
                if not first:
                    take_sums(g - 1, SUP - 1)
                layer1(g, 1)
                if not last:
                    normalise(g + 1)
                layer1(g, 2)
                layer1(g, 3)
                if not last:
                    attributes_hi(g + 1)
                    transposed_hi(g + 1, 0)
                    transposed_hi(g + 1, 1)
                for j in range(SUP):
                    act.wait_ge(msg_done, SUP * g + j + 1)
                    wait_from(act, summed, SUP * g + j - 1)
                    act.activation(msg_hi[:, j % 2, :], msg[:, :], ACT.Copy).then_inc(msg_hi_done, 1)
                    if j < 2 and not last:
                        transposed_hi(g + 1, j + 2)
                    if j > 0:
                        take_sums(g, j - 1)
                for n in more:
                    split_hi(n)

            for n in range(2):
                split_hi(n)
            normalise(0)
            attributes_hi(0)
            for j in range(SUP):
                transposed_hi(0, j)
            split_hi(2)
            split_hi(3)
            act.wait_ge(b1_in, 16)
            supertile(0, True, False, range(4, 6))
            supertile(1, False, False, range(6, len(loads)))
            with act.Fori(2, NSUP - 1) as g:
                supertile(g, False, False, ())
            supertile(NSUP - 1, False, True, ())
            take_sums(NSUP - 1, SUP - 1)

        @block.vector
        def _(dve):
            def split_lo(n):
                dve.wait_ge(stage_hi, n + 1)
                _, width, hi, lo, cols = loads[n]
                dve.tensor_tensor(lo, stage[:, n % 2, 0:width].rearrange("p (k n) -> p k n", n=cols),
                                  hi.bitcast(F32), ALU.subtract).then_inc(stage_lo, 1)
                if n == F2_LOAD - 2:
                    dve.wait_ge(stage_lo, n + 1)
                    dve.memset(stage[:, F2_LOAD % 2, FW * D:KF * D], 0.0).then_inc(iotas, 1)

            def stats(g1):
                if not isinstance(g1, int) or g1 > 0:
                    dve.wait_ge(nmr_ready, g1)
                for j in range(SUP):
                    dve.wait_ge(xs_in[j], 16 * (g1 + 1))
                    dve.bn_stats(st_e[:, j, :], xs[:, j, :]).then_inc(stats_e, 1)
                dve.wait_ge(stats_e, SUP * (g1 + 1)).then_inc(held["dve"], 1)
                for j in range(SUP):
                    dve.bn_aggr(mv_e[:, j, :], st_e[:, j, :]).then_inc(mv_ready, 1)
                dve.wait_ge(mv_ready, SUP * (g1 + 1))
                dve.tensor_scalar(nm_e[:, :], mv_e[:, :, 0], -1.0, None, ALU.mult)
                dve.tensor_scalar(ve_e[:, :], mv_e[:, :, 1], EPS, None, ALU.add).then_inc(var_e, 1)

            def slots():
                dve.wait_ge(all_dst_in, 16)
                dve.tensor_copy(all_dst[:, :, :], all_dst_i[:, :].rearrange("p (c r) -> p c r", r=R)).then_inc(top_step, 1)
                dve.wait_ge(top_step, 1)
                dve.tensor_tensor(all_same[:, :, :], all_dst[:, :, :],
                                  dst_f[:, 0:EC].unsqueeze(2).broadcast_to((R, EC, R)), ALU.is_equal).then_inc(top_step, 1)
                dve.wait_ge(top_step, 2)
                dve.tensor_tensor(all_same[:, :, :], all_same[:, :, :],
                                  iota_row[:, :].unsqueeze(1).broadcast_to((R, EC, R)), ALU.mult).then_inc(top_step, 1)
                dve.wait_ge(top_step, 3)
                dve.tensor_reduce(top_row[:, :], all_same[:, :, :], AX_X, ALU.max).then_inc(top_step, 1)
                for q in range(GE):
                    dve.max_index(found[:, 8 * q:8 * q + 8], dst_f[:, 8 * q:8 * q + 8],
                                  all_dst[:, :, :].rearrange("p c r -> p (c r)")).then_inc(top_step, 1)
                dve.wait_ge(top_step, 4 + GE)
                dve.tensor_scalar(is_top[:, :], top_row[:, :], row_no[:, 0:1], None, ALU.is_equal).then_inc(all_used, 1)
                dve.tensor_copy(found_f[:, :], found[:, :]).then_inc(top_step, 1)
                dve.wait_ge(top_step, 5 + GE)
                dve.tensor_scalar(found_f[:, :], found_f[:, :], -1.0, float(E), ALU.mult, ALU.add).then_inc(top_step, 1)
                groups = dst_f[:, :].rearrange("p (q i) -> p q i", i=8)
                dve.tensor_tensor(paired[:, :, :, :], groups.unsqueeze(3).broadcast_to((R, GE, 8, 8)),
                                  groups.unsqueeze(2).broadcast_to((R, GE, 8, 8)), ALU.is_equal).then_inc(top_step, 1)
                dve.wait_ge(top_step, 7 + GE)
                dve.tensor_tensor(paired[:, :, :, :], paired[:, :, :, :],
                                  found_f[:, :].rearrange("p (q i) -> p q i", i=8).unsqueeze(2)
                                  .broadcast_to((R, GE, 8, 8)), ALU.mult).then_inc(top_step, 1)
                dve.wait_ge(top_step, 8 + GE)
                dve.tensor_reduce(first[:, :].rearrange("p (q i) -> p q i", i=8), paired[:, :, :, :], AX_X, ALU.max)\
                    .then_inc(top_step, 1)
                dve.wait_ge(top_step, 9 + GE)
                dve.tensor_scalar(slot_f[:, :], first[:, 0:EC], -1.0, float(E), ALU.mult, ALU.add).then_inc(top_step, 1)
                dve.wait_ge(top_step, 10 + GE)
                dve.tensor_copy(slot_i[:, :], slot_f[:, :]).then_inc(top_step, 1)
                dve.tensor_scalar(slot_f[:, :], slot_f[:, :], trash[:, 0:1], None, ALU.subtract).then_inc(add_all_ready, 1)
                dve.wait_ge(all_used, 1)
                dve.wait_ge(add_all_ready, 1)
                dve.tensor_tensor(slot_f[:, :], slot_f[:, :], is_top[:, :], ALU.mult).then_inc(add_all_ready, 1)
                dve.wait_ge(add_all_ready, 2)
                dve.tensor_scalar(add_all[:, :], slot_f[:, :], trash[:, 0:1], None, ALU.add).then_inc(add_all_ready, 1)

            def attributes_lo(g1):
                wait_from(dve, l1, DK * g1)
                dve.wait_ge(t_hi, (SUP + 1) * g1 + 1)
                dve.tensor_tensor(m_lo_t[:, K1 - 1, :], attr[:, :], m_hi_t[:, K1 - 1, :].bitcast(F32), ALU.subtract)\
                    .then_inc(t_lo, 1)

            def transposed_lo(g1, j):
                dve.wait_ge(t_hi, (SUP + 1) * g1 + j + 2)
                dve.tensor_tensor(m_lo_t[:, 0:DK, j * R:(j + 1) * R],
                                  bank[2 + j % 2][:, 0:DK * R].rearrange("p (k r) -> p k r", k=DK),
                                  m_hi_t[:, 0:DK, j * R:(j + 1) * R].bitcast(F32), ALU.subtract).then_inc(t_lo, 1)

            def layer1(g, b):
                if b == 0:
                    wait_from(dve, l2, SUP * g)
                dve.wait_ge(r_hi_done, DK * g + b + 1)
                dve.tensor_tensor(r_lo[:, b, :], r32[:, b % 2, :], r_hi[:, b, :].bitcast(F32), ALU.subtract)\
                    .then_inc(r_lo_done, 1)

            def supertile(g, last, more):
                for b in range(DK):
                    layer1(g, b)
                if not last:
                    attributes_lo(g + 1)
                    transposed_lo(g + 1, 0)
                    transposed_lo(g + 1, 1)
                for j in range(SUP):
                    dve.wait_ge(l2, SUP * g + j + 1)
                    wait_from(dve, msg_hi_done, SUP * g + j)
                    wait_from(dve, msg_lo_done, SUP * g + j)
                    dve.tensor_tensor(msg[:, :], bank[4 + j % 2][0:R, :], b2_row[:, :], ALU.add).then_inc(msg_done, 1)
                    dve.wait_ge(row_in, 16 * (g + 1))
                    wait_from(dve, summed, SUP * g + j - 1)
                    dve.tensor_scalar(same[:, j % 2, :], row_i[:, j * R:(j + 1) * R],
                                      dst_f[:, bass.ds(SUP * g + j, 1)], None, ALU.is_equal).then_inc(same_done, 1)
                    dve.wait_ge(msg_hi_done, SUP * g + j + 1)
                    wait_from(dve, summed, SUP * g + j)
                    dve.tensor_tensor(msg_lo[:, :], msg[:, :], msg_hi[:, j % 2, :].bitcast(F32), ALU.subtract)\
                        .then_inc(msg_lo_done, 1)
                    if j < 2 and not last:
                        transposed_lo(g + 1, j + 2)
                for n in more:
                    split_lo(n)

            dve.memset(dst_f[:, :], -1.0).then_inc(dst_f_done, 1)
            for n in range(2):
                split_lo(n)
            stats(0)
            attributes_lo(0)
            for j in range(SUP):
                transposed_lo(0, j)
            split_lo(2)
            split_lo(3)
            dve.wait_ge(bn_in, 64)
            dve.tensor_scalar(bn_cols[:, 3, :], bn_cols[:, 3, :], EPS, None, ALU.add).then_inc(bn_step, 1)
            dve.wait_ge(dst_in, 16)
            dve.wait_ge(dst_f_done, 1)
            dve.tensor_copy(dst_f[:, 0:EC], dst_i[:, :]).then_inc(dst_f_done, 1)
            dve.wait_ge(iotas, 7)
            dve.wait_ge(dst_f_done, 2)
            stats(1)
            slots()
            dve.wait_ge(b2_in, 16)
            supertile(0, False, range(4, 6))
            stats(2)
            supertile(1, False, range(6, len(loads)))
            with dve.Fori(2, NSUP - 1) as g:
                stats(g + 1)
                supertile(g, False, ())
            supertile(NSUP - 1, True, ())

        @block.tensor
        def _(pe):
            def transposes(g1, j):
                pe.wait_ge(h_e, SUP * g1 + j + 1)
                wait_from(pe, t_lo, (SUP + 1) * g1 + j if j >= 2 else (SUP + 1) * g1 + j - 1)
                for k in range(DK):
                    last = pe.transpose(bank[2 + j % 2][:, k * R:(k + 1) * R], hs[:, j, k * P:(k + 1) * P],
                                        ident[0:R, 0:R])
                last.then_inc(t_e, 1)

            def layer1(g, b):
                if b == 0:
                    pe.wait_ge(t_lo, (SUP + 1) * (g + 1))
                wait_from(pe, relu_done, DK * g + b - 1)
                n = 0
                for k in range(K1):
                    for w, m in ((w1_hi, m_hi_t), (w1_hi, m_lo_t), (w1_lo, m_hi_t)):
                        last = pe.matmul(bank[b % 2][:, 0:SW], w[:, k, b * P:(b + 1) * P], m[:, k, :],
                                         start=n == 0, stop=n == 3 * K1 - 1)
                        n += 1
                last.then_inc(l1, 1)

            def tile_sums(g, j):
                pe.wait_ge(msg_lo_done, SUP * g + j + 1)
                wait_from(pe, sums_done, SUP * g + j - 1)
                pe.matmul(bank[6 + j % 2][0:R, :], same[:, j % 2, :], msg_hi[:, j % 2, :], start=True, stop=False)
                pe.matmul(bank[6 + j % 2][0:R, :], same[:, j % 2, :], msg_lo[:, :], start=False, stop=True)\
                    .then_inc(summed, 1)

            def layer2(g, j):
                wait_from(pe, msg_done, SUP * g + j - 1)
                n = 0
                for k in range(DK):
                    if j == 0:
                        pe.wait_ge(r_lo_done, DK * g + k + 1)
                    for r, w in ((r_hi, w2_hi), (r_hi, w2_lo), (r_lo, w2_hi)):
                        last = pe.matmul(bank[4 + j % 2][0:R, :], r[:, k, j * R:(j + 1) * R], w[:, k, :],
                                         start=n == 0, stop=n == 3 * DK - 1)
                        n += 1
                last.then_inc(l2, 1)

            def supertile(g, first, last):
                for b in range(DK):
                    layer1(g, b)
                    if b == 0 and not first:
                        tile_sums(g - 1, SUP - 1)
                if not last:
                    transposes(g + 1, 0)
                    transposes(g + 1, 1)
                if first:
                    pe.wait_ge(stage_lo, W2_LOADS)
                for j in range(SUP):
                    layer2(g, j)
                    if j < 2 and not last:
                        transposes(g + 1, j + 2)
                    if j > 0:
                        tile_sums(g, j - 1)

            pe.wait_ge(consts, 2)
            for j in range(SUP):
                transposes(0, j)
            pe.wait_ge(stage_lo, W1_LOADS)
            supertile(0, True, False)
            with pe.Fori(1, NSUP - 1) as g:
                supertile(g, False, False)
            supertile(NSUP - 1, False, True)
            tile_sums(NSUP - 1, SUP - 1)

    cursor[0] = region_c
    ig_bias = place("ig_bias", [R, G3])
    ig_bhh = place("ig_bhh", [R, 2 * D])
    agg_in = place("agg_in", [R, 2, D])
    a_hi = place("a_hi", [P, 2, DK * R], F32R)
    a_lo = place("a_lo", [P, 2, DK * R], F32R)
    g_out = place("g_out", [R, 2, G3])
    stage2 = place("stage2", [P, 2, G3])
    dst_at = place("dst_at", [R, SUP], I32)
    slot_at4 = place("slot_at4", [R, SUP], I32)
    assert cursor[0] <= nc.sbuf_usable_end

    index_copied = sem("index_copied")
    slots_in = sem("slots_in")
    bias_in = sem("bias_in")
    bias_done = sem("bias_done")
    staged2 = [sem("staged2_0"), sem("staged2_1")]
    stage2_hi = sem("stage2_hi")
    stage2_lo = sem("stage2_lo")
    agg_loaded = [sem("agg_loaded0"), sem("agg_loaded1")]
    t_a = sem("t_a")
    a_hi_done = sem("a_hi_done")
    a_lo_done = sem("a_lo_done")
    g_prod = sem("g_prod")
    g_added = sem("g_added")
    g_stored = [sem("g_stored0"), sem("g_stored1")]
    bias_stored = sem("bias_stored")

    whhv = whh_t.rearrange("(k p) n -> p k n", p=P)

    with nc.Block() as block:
        @block.sync
        def _(sp):
            def load(c, s):
                sp.dma_start(agg_in[:, s, :], agg[bass.ds(c * R, R), :]).then_inc(agg_loaded[s], 16)

            for c in range(2):
                load(c, c)
            sp.dma_start(ig_bias[:, :], bcast(b_ih)).then_inc(bias_in, 16)
            sp.dma_start(ig_bhh[:, :], bcast(b_hh[0:2 * D])).then_inc(bias_in, 16)
            sp.dma_start(stage2[:, 0, :], whhv[:, 0, :]).then_inc(staged2[0], 16)
            sp.dma_start(stage2[:, 1, :], whhv[:, 1, :]).then_inc(staged2[1], 16)
            sp.wait_ge(bias_done, 1)
            sp.dma_start(gates_in[E:E + R, :], ig_bias[:, :]).then_inc(bias_stored, 16)
            for c in range(2):
                sp.wait_ge(stage2_lo, c + 1)
                sp.dma_start(stage2[:, c, :], whhv[:, 2 + c, :]).then_inc(staged2[c], 16)
            with sp.Fori(1, EC // 2) as i:
                row = [sp.snap((2 * i + s) * R) for s in range(2)]
                past = [sp.snap((2 * i + s - 2) * R) for s in range(2)]
                for s in range(2):
                    sp.wait_ge(t_a, 2 * i + s - 1)
                    sp.dma_start(agg_in[:, s, :], agg[bass.ds(row[s], R), :]).then_inc(agg_loaded[s], 16)
                for s in range(2):
                    sp.wait_ge(g_added, 3 * (2 * i + s - 1))
                    sp.dma_start(gates_in[bass.ds(past[s], R), :], g_out[:, s, :]).then_inc(g_stored[s], 16)
            for s in range(2):
                c = EC - 2 + s
                sp.wait_ge(g_added, 3 * (c + 1))
                sp.dma_start(gates_in[c * R:(c + 1) * R, :], g_out[:, s, :]).then_inc(g_stored[s], 16)
            for s in range(2):
                sp.wait_ge(g_stored[s], 16 * (EC // 2))
            sp.wait_ge(bias_stored, 16)

        @block.gpsimd
        def _(pool):
            with pool.Fori(0, NSUP) as g:
                copied = pool.snap(2 * (g + 1))
                entered = [pool.snap(16 * (g * SUP + j + 1)) for j in range(SUP)]
                at = bass.ds(g * SUP, SUP)
                pool.tensor_copy(dst_at[:, :], dst_i[:, at]).then_inc(index_copied, 1)
                pool.tensor_copy(slot_at4[:, :], slot_i[:, at]).then_inc(index_copied, 1)
                pool.wait_ge(index_copied, copied).then_inc(held["pool"], 1)
                for j in range(SUP):
                    pool.indirect_dma_start(out=slot_of_node, in_=slot_at4[:, j:j + 1], in_offset=None,
                                            out_offset=bass.IndirectOffsetOnAxis(ap=dst_at[:, j:j + 1], axis=0),
                                            ).then_inc(slots_in, 16)
                    pool.wait_ge(slots_in, entered[j]).then_inc(held["pool"], 1)

        @block.scalar
        def _(act):
            def hi(c, s):
                act.wait_ge(t_a, c + 1)
                wait_from(act, g_prod, 3 * (c - 1))
                act.activation(a_hi[:, s, :], bank[6 + s][:, 0:DK * R], ACT.Copy).then_inc(a_hi_done, 1)

            hi(0, 0)
            for k in range(2):
                act.wait_ge(staged2[k], 16)
                act.activation(whh_hi[:, k, :], stage2[:, k, :], ACT.Copy).then_inc(stage2_hi, 1)
            hi(1, 1)
            for k in range(2, 4):
                act.wait_ge(staged2[k % 2], 32)
                act.activation(whh_hi[:, k, :], stage2[:, k % 2, :], ACT.Copy).then_inc(stage2_hi, 1)
            with act.Fori(1, EC // 2) as i:
                for s in range(2):
                    hi(2 * i + s, s)

        @block.vector
        def _(dve):
            def lo(c, s):
                dve.wait_ge(a_hi_done, c + 1)
                dve.tensor_tensor(a_lo[:, s, :], bank[6 + s][:, 0:DK * R], a_hi[:, s, :].bitcast(F32), ALU.subtract)\
                    .then_inc(a_lo_done, 1)

            def add_bias(c, s, i):
                if not isinstance(i, int) or i > 0:
                    dve.wait_ge(g_stored[s], 16 * i)
                for q in range(3):
                    dve.wait_ge(g_prod, 3 * c + q + 1)
                    dve.tensor_tensor(g_out[:, s, q * D:(q + 1) * D], bank[3 * s + q][0:R, :],
                                      ig_bias[:, q * D:(q + 1) * D], ALU.add).then_inc(g_added, 1)

            def split(k):
                dve.wait_ge(stage2_hi, k + 1)
                dve.tensor_tensor(whh_lo[:, k, :], stage2[:, k % 2, :], whh_hi[:, k, :].bitcast(F32), ALU.subtract)\
                    .then_inc(stage2_lo, 1)

            lo(0, 0)
            dve.wait_ge(bias_in, 32)
            dve.tensor_tensor(ig_bias[:, 0:2 * D], ig_bias[:, 0:2 * D], ig_bhh[:, :], ALU.add).then_inc(bias_done, 1)
            dve.wait_ge(bias_done, 1)
            split(0)
            split(1)
            lo(1, 1)
            add_bias(0, 0, 0)
            split(2)
            split(3)

            def pair(i):
                lo(2 * i, 0)
                add_bias(2 * i - 1, 1, i - 1)
                lo(2 * i + 1, 1)
                add_bias(2 * i, 0, i)

            pair(1)
            with dve.Fori(2, EC // 2) as i:
                pair(i)
            add_bias(EC - 1, 1, EC // 2 - 1)

        @block.tensor
        def _(pe):
            def transposes(c, s, i):
                pe.wait_ge(agg_loaded[s], 16 * (i + 1))
                wait_from(pe, a_lo_done, c - 1)
                for k in range(DK):
                    last = pe.transpose(bank[6 + s][:, k * R:(k + 1) * R], agg_in[:, s, k * P:(k + 1) * P],
                                        ident[0:R, 0:R])
                last.then_inc(t_a, 1)

            def product(c, s):
                pe.wait_ge(a_lo_done, c + 1)
                for q in range(3):
                    wait_from(pe, g_added, 3 * (c - 2) + q + 1)
                    n = 0
                    for k in range(DK):
                        for a, w in ((a_hi, wih_hi), (a_hi, wih_lo), (a_lo, wih_hi)):
                            last = pe.matmul(bank[3 * s + q][0:R, :], a[:, s, k * R:(k + 1) * R],
                                             w[:, k, q * D:(q + 1) * D], start=n == 0, stop=n == 3 * DK - 1)
                            n += 1
                    last.then_inc(g_prod, 1)

            transposes(0, 0, 0)
            transposes(1, 1, 0)
            product(0, 0)

            def pair(i):
                transposes(2 * i, 0, i)
                product(2 * i - 1, 1)
                transposes(2 * i + 1, 1, i)
                product(2 * i, 0)

            pair(1)
            with pe.Fori(2, EC // 2) as i:
                pair(i)
            product(EC - 1, 1)

    cursor[0] = region_b
    node_slot = place("node_slot", [R, NT], I32)
    slot_at = place("slot_at", [R, 2], I32)
    xt = place("xt", [R, 2, D])
    h = place("h", [R, 2, D])
    x_h = place("x_h", [R, 2, D])
    x_h_b = place("x_h_b", [R, 2, D])
    h_hi = place("h_hi", [P, 2, DK * R], F32R)
    h_lo = place("h_lo", [P, 2, DK * R], F32R)
    gates = place("gates", [R, 2, G3])
    hn_raw = place("hn_raw", [R, 2, D])
    hn = place("hn", [R, 2, D])
    r_pre = place("r_pre", [R, D])
    r_gate = place("r_gate", [R, D])
    z_pre = place("z_pre", [R, D])
    z_gate = place("z_gate", [R, D])
    r_hn = place("r_hn", [R, D])
    n_pre = place("n_pre", [R, D])
    n_gate = place("n_gate", [R, 2, D])
    h_n = place("h_n", [R, D])
    z_h_n = place("z_h_n", [R, D])
    h_new = place("h_new", [R, D])
    scaled = place("scaled", [R, D])
    x1 = place("x1", [R, 2, D])
    h2 = place("h2", [R, 2, D])
    h2_hi = place("h2_hi", [P, DK * R], F32R)
    h2_lo = place("h2_lo", [P, DK * R], F32R)
    f1 = place("f1", [R, F1])
    hid = place("hid", [R, 2, KF * P])
    hid_hi = place("hid_hi", [P, KF * R], F32R)
    hid_lo = place("hid_lo", [P, KF * R], F32R)
    y = place("y", [R, 2, D])
    st = {k: place(f"st{k}", [R, 6]) for k in (1, 2)}
    mv = {k: place(f"mv{k}", [R, 2]) for k in (1, 2)}
    var_eps = {k: place(f"var_eps{k}", [R, 1]) for k in (1, 2)}
    neg_mean = {k: place(f"neg_mean{k}", [R, 1]) for k in (1, 2)}
    rstd = {k: place(f"rstd{k}", [R, 2]) for k in (1, 2)}
    shift = {k: place(f"shift{k}", [R, 2]) for k in (1, 2)}
    one_rstd = place("one_rstd", [R, 2])
    top = place("top", [R, 8])
    top_i = place("top_i", [R, 8], U32)
    top_f = place("top_f", [R, 2])
    gap = place("gap", [R, 1])
    weight = place("weight", [R, 2])
    comb1 = place("comb1", [R, NE])
    comb2 = place("comb2", [R, NE])
    assert cursor[0] <= nc.sbuf_usable_end, (cursor[0], nc.sbuf_usable_end)

    b_r, b_z, b_n, b_th, b_th2, b_thid, b_f1, b_f2 = bank

    table_in = sem("table_in")
    hid_set = sem("hid_set")
    x_in = [sem("x_in0"), sem("x_in1")]
    slot_copied = sem("slot_copied")
    gates_loaded = [sem("gates_loaded0"), sem("gates_loaded1")]
    st_done = {k: sem(f"st_done{k}") for k in (1, 2)}
    mv_done = {k: sem(f"mv_done{k}") for k in (1, 2)}
    var_done = {k: sem(f"var_done{k}") for k in (1, 2)}
    rstd_done = {k: sem(f"rstd_done{k}") for k in (1, 2)}
    shift_done = {k: sem(f"shift_done{k}") for k in (1, 2)}
    h_done = sem("h_done")
    x_h_done = sem("x_h_done")
    x_h_b_done = sem("x_h_b_done")
    h_turned = sem("h_turned")
    h_hi_done = sem("h_hi_done")
    h_lo_done = sem("h_lo_done")
    n_prod = sem("n_prod")
    r_prod = sem("r_prod")
    z_prod = sem("z_prod")
    hn_raw_done = sem("hn_raw_done")
    hn_done = sem("hn_done")
    r_pre_done = sem("r_pre_done")
    r_done = sem("r_done")
    z_pre_done = sem("z_pre_done")
    z_done = sem("z_done")
    r_hn_done = sem("r_hn_done")
    n_pre_done = sem("n_pre_done")
    n_done = sem("n_done")
    h_n_done = sem("h_n_done")
    z_h_n_done = sem("z_h_n_done")
    h_new_done = sem("h_new_done")
    scaled_done = sem("scaled_done")
    x1_done = sem("x1_done")
    h2_done = sem("h2_done")
    h2_turned = sem("h2_turned")
    h2_hi_done = sem("h2_hi_done")
    h2_lo_done = sem("h2_lo_done")
    f1_prod = sem("f1_prod")
    f1_done = sem("f1_done")
    top_done = sem("top_done")
    top_i_done = sem("top_i_done")
    gap_done = sem("gap_done")
    weight_done = sem("weight_done")
    comb1_done = sem("comb1_done")
    comb2_done = sem("comb2_done")
    comb_done = sem("comb_done")
    hid_done = sem("hid_done")
    hid_turned = sem("hid_turned")
    hid_hi_done = sem("hid_hi_done")
    hid_lo_done = sem("hid_lo_done")
    f2_prod = sem("f2_prod")
    y_done = sem("y_done")
    y_stored = [sem("y_stored0"), sem("y_stored1")]

    x_tiles = x.rearrange("(p t) d -> p t d", t=NT)
    out_tiles = out.rearrange("(p t) d -> p t d", t=NT)

    FIRST = 4
    LOOPS = (NT - 2 - FIRST) // 2

    class Period:
        def __init__(self, i, j):
            self.i, self.j = i, j
            self.t = FIRST + 2 * i + j

        def has(self, k):
            return not isinstance(self.i, int) or 0 <= self.t + k < NT

        def slot(self, k):
            return (self.j + k) % 2

        def turn(self, k):
            return self.i + (FIRST + self.j + k - self.slot(k)) // 2

    def periods(eng, body):
        for j in range(-FIRST - 2, 0):
            body(Period(0, j))
        with eng.Fori(0, LOOPS) as i:
            for j in range(2):
                body(Period(i, j))
        for j in range(4):
            body(Period(LOOPS, j))

    with nc.Block() as block:
        @block.sync
        def _(sp):
            sp.dma_start(node_slot[:, :], slot_of_node.rearrange("(p t) o -> p (t o)", t=NT)).then_inc(table_in, 16)

            def body(p):
                t = p.t
                if not isinstance(p.i, int):
                    tile_x, tile_y = sp.snap(t + 2), sp.snap(t - 2)
                else:
                    tile_x, tile_y = t + 2, t - 2
                if p.has(2):
                    s = p.slot(2)
                    wait_from(sp, x_h_done, t + 1)
                    sp.dma_start(xt[:, s, :], x_tiles[:, bass.ds(tile_x, 1), :].rearrange("p o d -> p (o d)"))\
                        .then_inc(x_in[s], 16)
                if p.has(-2):
                    s = p.slot(-2)
                    sp.wait_ge(y_done, t - 1)
                    sp.dma_start(out_tiles[:, bass.ds(tile_y, 1), :].rearrange("p o d -> p (o d)"), y[:, s, :])\
                        .then_inc(y_stored[s], 16)

            periods(sp, body)
            for s in range(2):
                sp.wait_ge(y_stored[s], 16 * (NT // 2))

        @block.gpsimd
        def _(pool):
            for s in range(2):
                pool.memset(hid[:, s, F1:KF * P], 0.0).then_inc(hid_set, 1)
            pool.wait_ge(hid_set, 2)
            for s in range(2):
                pool.memset(hid[:, s, F1:F1 + 1], 0.5).then_inc(hid_set, 1)
            pool.wait_ge(table_in, 16)

            def gather(p, k):
                s, t = p.slot(k), p.t
                pool.tensor_copy(slot_at[:, s:s + 1], node_slot[:, bass.ds(t + k, 1)]).then_inc(slot_copied, 1)
                pool.wait_ge(slot_copied, t + k + 1).then_inc(held["pool"], 1)
                pool.indirect_dma_start(out=gates[:, s, :], out_offset=None, in_=gates_in,
                                        in_offset=bass.IndirectOffsetOnAxis(ap=slot_at[:, s:s + 1], axis=0),
                                        ).then_inc(gates_loaded[s], 16)

            def norm(p, k, which):
                s = p.slot(k)
                pool.wait_ge(var_done[which], p.t + k + 1)
                pool.tensor_tensor(rstd[which][:, s:s + 1], var_eps[which][:, :], minus_half[0:R, 0:1], ALU.pow)\
                    .then_inc(rstd_done[which], 1)
                pool.wait_ge(rstd_done[which], p.t + k + 1)
                pool.tensor_tensor(shift[which][:, s:s + 1], neg_mean[which][:, :], rstd[which][:, s:s + 1], ALU.mult)\
                    .then_inc(shift_done[which], 1)
                if which == 1:
                    pool.tensor_tensor(one_rstd[:, s:s + 1], rstd[1][:, s:s + 1], ones_col[:, 0:1], ALU.add)\
                        .then_inc(shift_done[which], 1)

            def body(p):
                t = p.t
                if p.has(-1):
                    norm(p, -1, 2)
                if p.has(0):
                    s = p.slot(0)
                    pool.wait_ge(hn_raw_done, t + 1)
                    wait_from(pool, r_hn_done, t - 1)
                    pool.tensor_tensor(hn[:, s, :], hn_raw[:, s, :], hn_bias[:, :], ALU.add).then_inc(hn_done, 1)
                if p.has(1):
                    s = p.slot(1)
                    pool.wait_ge(x_h_done, t + 2)
                    wait_from(pool, x1_done, t)
                    pool.tensor_tensor(x_h_b[:, s, :], x_h[:, s, :], bn_shift[:, :], ALU.add).then_inc(x_h_b_done, 1)
                if p.has(0):
                    s = p.slot(0)
                    pool.wait_ge(r_done, t + 1)
                    pool.wait_ge(hn_done, t + 1)
                    pool.tensor_tensor(r_hn[:, :], r_gate[:, :], hn[:, s, :], ALU.mult).then_inc(r_hn_done, 1)
                    wait_from(pool, n_done, t)
                    pool.wait_ge(gates_loaded[s], 16 * (p.turn(0) + 1))
                    pool.wait_ge(r_hn_done, t + 1)
                    pool.tensor_tensor(n_pre[:, :], r_hn[:, :], gates[:, s, 2 * D:G3], ALU.add).then_inc(n_pre_done, 1)
                if p.has(0):
                    s = p.slot(0)
                    pool.wait_ge(n_done, t + 1)
                    wait_from(pool, z_h_n_done, t)
                    pool.tensor_tensor(h_n[:, :], h[:, s, :], n_gate[:, s, :], ALU.subtract).then_inc(h_n_done, 1)

                if p.has(2):
                    if p.has(0):
                        pool.wait_ge(n_pre_done, t + 1)
                        pool.wait_ge(r_pre_done, t + 1)
                        pool.wait_ge(z_pre_done, t + 1).then_inc(held["pool"], 1)
                    gather(p, 2)
                    norm(p, 2, 1)

            periods(pool, body)

        @block.scalar
        def _(act):
            def body(p):
                t = p.t
                if p.has(1):
                    s = p.slot(1)
                    act.wait_ge(shift_done[1], 2 * (t + 2))
                    wait_from(act, h_n_done, t)
                    act.activation(h[:, s, :], xt[:, s, :], ACT.Identity, bias=shift[1][:, s:s + 1],
                                   scale=rstd[1][:, s:s + 1]).then_inc(h_done, 1)
                    wait_from(act, x_h_b_done, t)
                    act.activation(x_h[:, s, :], xt[:, s, :], ACT.Identity, bias=shift[1][:, s:s + 1],
                                   scale=one_rstd[:, s:s + 1]).then_inc(x_h_done, 1)
                if p.has(0):
                    s = p.slot(0)
                    act.wait_ge(n_prod, t + 1)
                    wait_from(act, hn_done, t - 1)
                    act.activation(hn_raw[:, s, :], b_n[0:R, :], ACT.Copy).then_inc(hn_raw_done, 1)
                if p.has(-1):
                    s = p.slot(-1)
                    act.wait_ge(shift_done[2], t)
                    wait_from(act, h2_turned, t - 2)
                    act.activation(h2[:, s, :], x1[:, s, :], ACT.Identity, bias=shift[2][:, s:s + 1],
                                   scale=rstd[2][:, s:s + 1]).then_inc(h2_done, 1)
                if p.has(-2):
                    act.wait_ge(gap_done, t - 1)
                    wait_from(act, comb2_done, t - 2)
                    act.activation(weight[:, 0:1], gap[:, :], ACT.Sigmoid).then_inc(weight_done, 1)
                    act.activation(weight[:, 1:2], gap[:, :], ACT.Sigmoid, scale=-1.0).then_inc(weight_done, 1)
                if p.has(1):
                    s = p.slot(1)
                    act.wait_ge(h_turned, t + 2)
                    wait_from(act, z_prod, t)
                    act.activation(h_hi[:, s, :], b_th[:, 0:DK * R], ACT.Copy).then_inc(h_hi_done, 1)
                if p.has(0):
                    act.wait_ge(r_pre_done, t + 1)
                    wait_from(act, r_hn_done, t)
                    act.activation(r_gate[:, :], r_pre[:, :], ACT.Sigmoid).then_inc(r_done, 1)
                if p.has(-2):
                    act.wait_ge(hid_turned, t - 1)
                    wait_from(act, f2_prod, t - 2)
                    act.activation(hid_hi[:, :], b_thid[:, 0:KF * R], ACT.Copy).then_inc(hid_hi_done, 1)
                if p.has(-1):
                    act.wait_ge(h2_turned, t)
                    wait_from(act, f1_prod, t - 1)
                    act.activation(h2_hi[:, :], b_th2[:, 0:DK * R], ACT.Copy).then_inc(h2_hi_done, 1)
                if p.has(0):
                    s = p.slot(0)
                    act.wait_ge(n_pre_done, t + 1)
                    wait_from(act, h_new_done, t - 1)
                    act.activation(n_gate[:, s, :], n_pre[:, :], ACT.Tanh).then_inc(n_done, 1)
                    act.wait_ge(z_pre_done, t + 1)
                    wait_from(act, z_h_n_done, t)
                    act.activation(z_gate[:, :], z_pre[:, :], ACT.Sigmoid).then_inc(z_done, 1)
            periods(act, body)

        @block.vector
        def _(dve):
            dve.wait_ge(hid_set, 4)

            def norm_stats(p, k, which, rows_of):
                t = p.t
                dve.bn_stats(st[which][:, :], rows_of).then_inc(st_done[which], 1)
                dve.wait_ge(st_done[which], t + k + 1).then_inc(held["dve"], 1)
                dve.bn_aggr(mv[which][:, :], st[which][:, :]).then_inc(mv_done[which], 1)
                dve.wait_ge(mv_done[which], t + k + 1)
                wait_from(dve, shift_done[which], (3 - which) * (t + k))
                dve.tensor_scalar(neg_mean[which][:, :], mv[which][:, 0:1], -1.0, None, ALU.mult)
                dve.tensor_scalar(var_eps[which][:, :], mv[which][:, 1:2], EPS, None, ALU.add)\
                    .then_inc(var_done[which], 1)

            def body(p):
                t = p.t
                if p.has(0):
                    s = p.slot(0)
                    dve.wait_ge(r_prod, t + 1)
                    dve.wait_ge(gates_loaded[s], 16 * (p.turn(0) + 1))
                    wait_from(dve, r_done, t)
                    dve.tensor_tensor(r_pre[:, :], b_r[0:R, :], gates[:, s, 0:D], ALU.add).then_inc(r_pre_done, 1)
                if p.has(-2):
                    s = p.slot(-2)
                    dve.wait_ge(weight_done, 2 * (t - 1))
                    dve.wait_ge(comb1_done, 2 * t - 3)
                    dve.tensor_scalar(comb1[:, :], iota8[:, :], top_f[:, 0:1], weight[:, 0:1], ALU.is_equal, ALU.mult)\
                        .then_inc(comb1_done, 1)
                    dve.tensor_scalar(comb2[:, :], iota8[:, :], top_f[:, 1:2], weight[:, 1:2], ALU.is_equal, ALU.mult)\
                        .then_inc(comb2_done, 1)
                    dve.wait_ge(comb1_done, 2 * t - 2)
                    dve.wait_ge(comb2_done, t - 1)
                    wait_from(dve, hid_turned, t - 3)
                    dve.tensor_tensor(hid[:, s, HE + HS:F1], comb1[:, :], comb2[:, :], ALU.add).then_inc(comb_done, 1)
                    dve.tensor_scalar(hid[:, s, HE:HE + HS], f1[:, NE + HE:F1], 0.0, 0.5, ALU.max, ALU.mult)
                    dve.wait_ge(comb_done, t - 1)
                    dve.scalar_tensor_tensor(
                        hid[:, s, 0:HE].rearrange("p (e f) -> p e f", e=NE),
                        f1[:, NE:NE + HE].rearrange("p (e f) -> p e f", e=NE), 0.0,
                        hid[:, s, HE + HS:F1].unsqueeze(2).broadcast_to((R, NE, HF)), ALU.max, ALU.mult)\
                        .then_inc(hid_done, 1)
                if p.has(1):
                    s = p.slot(1)
                    dve.wait_ge(h_hi_done, t + 2)
                    dve.tensor_tensor(h_lo[:, s, :], b_th[:, 0:DK * R], h_hi[:, s, :].bitcast(F32), ALU.subtract)\
                        .then_inc(h_lo_done, 1)
                if p.has(-2):
                    dve.wait_ge(hid_hi_done, t - 1)
                    dve.tensor_tensor(hid_lo[:, :], b_thid[:, 0:KF * R], hid_hi[:, :].bitcast(F32), ALU.subtract)\
                        .then_inc(hid_lo_done, 1)
                if p.has(-1):
                    dve.wait_ge(h2_hi_done, t)
                    dve.tensor_tensor(h2_lo[:, :], b_th2[:, 0:DK * R], h2_hi[:, :].bitcast(F32), ALU.subtract)\
                        .then_inc(h2_lo_done, 1)
                if p.has(0):
                    s = p.slot(0)
                    dve.wait_ge(z_prod, t + 1)
                    wait_from(dve, z_done, t)
                    dve.tensor_tensor(z_pre[:, :], b_z[0:R, :], gates[:, s, D:2 * D], ALU.add).then_inc(z_pre_done, 1)
                if p.has(2):
                    s = p.slot(2)
                    dve.wait_ge(x_in[s], 16 * (p.turn(2) + 1))
                    norm_stats(p, 2, 1, xt[:, s, :])
                if p.has(-2):
                    s = p.slot(-2)
                    dve.wait_ge(f2_prod, t - 1)
                    wait_from(dve, y_stored[s], 16 * p.turn(-2))
                    dve.tensor_tensor(y[:, s, :], b_f2[0:R, :], x1[:, s, :], ALU.add).then_inc(y_done, 1)
                if p.has(0):
                    s = p.slot(0)
                    dve.wait_ge(z_done, t + 1)
                    dve.wait_ge(h_n_done, t + 1)
                    dve.tensor_tensor(z_h_n[:, :], z_gate[:, :], h_n[:, :], ALU.mult).then_inc(z_h_n_done, 1)
                    dve.wait_ge(z_h_n_done, t + 1)
                    dve.tensor_tensor(h_new[:, :], z_h_n[:, :], n_gate[:, s, :], ALU.add).then_inc(h_new_done, 1)
                    dve.wait_ge(h_new_done, t + 1)
                    dve.tensor_tensor(scaled[:, :], h_new[:, :], bn_scale[:, :], ALU.mult).then_inc(scaled_done, 1)
                    dve.wait_ge(scaled_done, t + 1)
                    dve.wait_ge(x_h_b_done, t + 1)
                    dve.tensor_tensor(x1[:, s, :], scaled[:, :], x_h_b[:, s, :], ALU.add).then_inc(x1_done, 1)
                    dve.wait_ge(x1_done, t + 1)
                    norm_stats(p, 0, 2, x1[:, s, :])
                if p.has(-1):
                    s = p.slot(-1)
                    dve.wait_ge(f1_prod, t)
                    dve.tensor_tensor(f1[:, :], b_f1[0:R, 0:F1], f1_bias[:, :], ALU.add).then_inc(f1_done, 1)
                    dve.wait_ge(f1_done, t).then_inc(held["dve"], 1)
                    dve.max(top[:, :], f1[:, 0:NE]).then_inc(top_done, 1)
                    dve.wait_ge(top_done, t)
                    wait_from(dve, weight_done, 2 * (t - 1))
                    dve.tensor_tensor(gap[:, :], top[:, 0:1], top[:, 1:2], ALU.subtract).then_inc(gap_done, 1)
                    dve.max_index(top_i[:, :], top[:, :], f1[:, 0:NE]).then_inc(top_i_done, 1)
                    dve.wait_ge(top_i_done, t)
                    dve.tensor_copy(top_f[:, :], top_i[:, 0:2]).then_inc(comb1_done, 1)

            periods(dve, body)

        @block.tensor
        def _(pe):
            pe.wait_ge(hid_set, 4)

            def gate(s, to, q, k0=0, k1=DK):
                n = 3 * k0
                for k in range(k0, k1):
                    for a, w in ((h_hi, whh_hi), (h_hi, whh_lo), (h_lo, whh_hi)):
                        last = pe.matmul(to[0:R, :], a[:, s, k * R:(k + 1) * R], w[:, k, q * D:(q + 1) * D],
                                         start=n == 0, stop=n == 3 * DK - 1)
                        n += 1
                return last

            def turn(to, rows_of, chunks):
                for k in range(chunks):
                    last = pe.transpose(to[:, k * R:(k + 1) * R], rows_of[:, k * P:(k + 1) * P], ident[0:R, 0:R])
                return last

            def body(p):
                t = p.t
                if p.has(0):
                    s = p.slot(0)
                    pe.wait_ge(h_lo_done, t + 1)
                    wait_from(pe, hn_raw_done, t)
                    gate(s, b_n, 2).then_inc(n_prod, 1)
                    wait_from(pe, r_pre_done, t)
                    gate(s, b_r, 0).then_inc(r_prod, 1)
                if p.has(1):
                    pe.wait_ge(h_done, t + 2)
                    wait_from(pe, h_lo_done, t + 1)
                    turn(b_th, h[:, p.slot(1), :], DK).then_inc(h_turned, 1)
                if p.has(-1):
                    pe.wait_ge(h2_done, t)
                    wait_from(pe, h2_lo_done, t - 1)
                    turn(b_th2, h2[:, p.slot(-1), :], DK).then_inc(h2_turned, 1)
                if p.has(0):
                    wait_from(pe, z_pre_done, t)
                    gate(p.slot(0), b_z, 1, 0, DK // 2)
                if p.has(-2):
                    pe.wait_ge(hid_done, t - 1)
                    wait_from(pe, hid_lo_done, t - 2)
                    turn(b_thid, hid[:, p.slot(-2), :], KF).then_inc(hid_turned, 1)
                if p.has(0):
                    gate(p.slot(0), b_z, 1, DK // 2, DK).then_inc(z_prod, 1)
                if p.has(-2):
                    pe.wait_ge(hid_lo_done, t - 1)
                    wait_from(pe, y_done, t - 2)
                    n = 0
                    for k in range(KF):
                        for a, w in ((hid_hi, f2_hi), (hid_hi, f2_lo), (hid_lo, f2_hi)):
                            last = pe.matmul(b_f2[0:R, :], a[:, k * R:(k + 1) * R], w[:, k, :],
                                             start=n == 0, stop=n == 3 * KF - 1)
                            n += 1
                    last.then_inc(f2_prod, 1)
                if p.has(-1):
                    pe.wait_ge(h2_lo_done, t)
                    wait_from(pe, f1_done, t - 1)
                    n = 0
                    for k in range(DK):
                        for a, w in ((h2_hi, f1_hi), (h2_hi, f1_lo), (h2_lo, f1_hi)):
                            last = pe.matmul(b_f1[0:R, 0:F1], a[:, k * R:(k + 1) * R], w[:, k, :],
                                             start=n == 0, stop=n == 3 * DK - 1)
                            n += 1
                    last.then_inc(f1_prod, 1)

            periods(pe, body)


def kernel(x, src, dst, edge_attr_128, L0_gnn_W1, L0_gnn_b1, L0_gnn_W2, L0_gnn_b2, L0_gnn_W_ih, L0_gnn_W_hh,
           L0_gnn_b_ih, L0_gnn_b_hh, L0_gnn_gamma, L0_gnn_beta, L0_gnn_run_mean, L0_gnn_run_var, L0_ffn_Wg,
           L0_ffn_bg, L0_ffn_W1, L0_ffn_b1, L0_ffn_W2, L0_ffn_b2, L0_ffn_Ws1, L0_ffn_bs1, L0_ffn_Ws2, L0_ffn_bs2):
    import numpy as np
    import concourse.bacc as bacc
    from concourse.bass_utils import run_bass_kernel_spmd

    rows, edge_tiles, sup = 125, 20, 4
    src, dst, attr = np.asarray(src), np.asarray(dst), np.asarray(edge_attr_128)
    w1, w2 = np.asarray(L0_ffn_W1), np.asarray(L0_ffn_W2)
    by_row = dst.reshape(rows, edge_tiles)
    arrays = dict(
        x=x, src=src.reshape(rows, edge_tiles), dst=by_row,
        dst_rows=by_row.T.reshape(edge_tiles // sup, sup * rows),
        attr_t=attr.reshape(rows, edge_tiles, -1).transpose(2, 1, 0).reshape(attr.shape[1], -1),
        w1t=np.asarray(L0_gnn_W1).T, b1=np.asarray(L0_gnn_b1).reshape(-1, 128).T, w2t=np.asarray(L0_gnn_W2).T, b2=L0_gnn_b2,
        wih_t=np.asarray(L0_gnn_W_ih).T, whh_t=np.asarray(L0_gnn_W_hh).T, b_ih=L0_gnn_b_ih, b_hh=L0_gnn_b_hh,
        gamma=L0_gnn_gamma, beta=L0_gnn_beta, run_mean=L0_gnn_run_mean, run_var=L0_gnn_run_var,
        wg=L0_ffn_Wg, bg=L0_ffn_bg, ew1=w1.transpose(1, 0, 2).reshape(w1.shape[1], -1),
        eb1=np.asarray(L0_ffn_b1).reshape(-1), ew2=w2.reshape(-1, w2.shape[2]), eb2=L0_ffn_b2,
        ws1=L0_ffn_Ws1, bs1=L0_ffn_bs1, ws2=L0_ffn_Ws2, bs2=L0_ffn_bs2)
    arrays = {f"in_{k}": np.ascontiguousarray(v) for k, v in arrays.items()}
    nc = bacc.Bacc("TRN2", target_bir_lowering=False, num_devices=1)
    args = [nc.dram_tensor(k, v.shape, mybir.dt.from_np(v.dtype), kind="ExternalInput").ap()
            for k, v in arrays.items()]
    out = nc.dram_tensor("out", tuple(np.asarray(x).shape), F32, kind="ExternalOutput").ap()
    gnn_ffn(nc, *args, out)
    result = run_bass_kernel_spmd(nc, [arrays], core_ids=[0])
    return result.results[0]["out"]
```

```python
import concourse.bass as bass
from concourse import mybir

F32 = mybir.dt.float32
F32R = mybir.dt.float32r
I32 = mybir.dt.int32
U32 = mybir.dt.uint32
ALU = mybir.AluOpType
ACT = mybir.ActivationFunctionType
AX_X = mybir.AxisListType.X

P = 128
EPS = 1e-5


def gnn_ffn(nc, x, src, dst, dst_rows, attr_t, w1t, b1, w2t, b2, wih_t, whh_t, b_ih, b_hh, gamma, beta,
            run_mean, run_var, wg, bg, ew1, eb1, ew2, eb2, ws1, bs1, ws2, bs2, out):
    N, D = x.shape
    R, EC = src.shape
    NT = N // R
    E = R * EC
    DK = D // P
    K1 = w1t.shape[0] // P
    G3 = 3 * D
    NE = wg.shape[1]
    HE = ew1.shape[1]
    HS = ws1.shape[1]
    HF = HE // NE
    F1 = NE + HE + HS
    KF = 3
    V = HS + NE + 1
    SUP = 4
    NSUP = EC // SUP
    SW = SUP * R
    GE = (EC + 7) // 8
    assert N == R * NT and EC == SUP * NSUP and HE == (KF - 1) * P and 3 * V <= P and NT % 2 == 0

    agg = nc.dram_tensor("agg", (E + R, D), F32, kind="Internal").ap()
    gates_in = nc.dram_tensor("gates_in", (E + R, G3), F32, kind="Internal").ap()
    bn_rows = nc.dram_tensor("bn_rows", (2, D), F32, kind="Internal").ap()
    slot_of_node = nc.dram_tensor("slot_of_node", (N, 1), I32, kind="Internal").ap()

    cursor = [(nc.sbuf_base + 63) // 64 * 64]

    def place(name, shape, dt=F32):
        size = 4
        for n in shape[1:]:
            size *= n
        at = cursor[0]
        cursor[0] = (at + size + 31) // 32 * 32
        return nc.alloc_sbuf_tensor_at(name, list(shape), dt, offset=at)

    ident = place("ident", [P, P])
    f1_hi = place("f1_hi", [P, DK, F1], F32R)
    f1_lo = place("f1_lo", [P, DK, F1], F32R)
    f2_hi = place("f2_hi", [P, KF, D], F32R)
    f2_lo = place("f2_lo", [P, KF - 1, D], F32R)
    bn_scale = place("bn_scale", [R, D])
    bn_shift = place("bn_shift", [R, D])
    hn_bias = place("hn_bias", [R, D])
    f1_bias = place("f1_bias", [R, F1])
    minus_half = place("minus_half", [P, SUP])
    ones_col = place("ones_col", [R, SUP])
    iota8 = place("iota8", [R, NE])
    region_a = cursor[0]
    whh_hi = place("whh_hi", [P, DK, G3], F32R)
    whh_lo = place("whh_lo", [P, DK, G3], F32R)
    region_b = cursor[0]

    bank = [nc.alloc_psum_tensor(f"bank{k}", [P, 512], F32) for k in range(8)]

    def sem(name):
        return nc.alloc_semaphore(name)

    def wait_from(eng, s, n):
        if not isinstance(n, int) or n > 0:
            eng.wait_ge(s, n)

    held = {e: sem(f"held_{e}") for e in ("pool", "dve")}

    cursor[0] = region_a
    w1_hi = place("w1_hi", [P, K1, D], F32R)
    w1_lo = place("w1_lo", [P, K1, D], F32R)
    w2_hi = place("w2_hi", [P, DK, D], F32R)
    w2_lo = place("w2_lo", [P, DK, D], F32R)
    hs = place("hs", [R, SUP, D])
    msg = place("msg", [R, D])
    b2_row = place("b2_row", [R, D])
    cursor[0] = max(cursor[0], region_b)
    wih_hi = place("wih_hi", [P, DK, G3], F32R)
    wih_lo = place("wih_lo", [P, DK, G3], F32R)
    dst_i = place("dst_i", [R, EC], I32)
    slot_i = place("slot_i", [R, EC], I32)
    region_c = cursor[0]
    src_i = place("src_i", [R, EC], I32)
    dst_f = place("dst_f", [R, GE * 8])
    row_i = place("row_i", [R, SUP * R], I32)
    iota_row = place("iota_row", [R, R])
    node_init = place("node_init", [R, NT], I32)
    bn_cols = place("bn_cols", [P, 4, DK])
    b1_col = place("b1_col", [P, DK])
    is_lo = place("is_lo", [P, 2])
    src_at = place("src_at", [R, SUP], I32)
    stage = place("stage", [P, 2, G3])
    xs = place("xs", [R, SUP, D])
    st_e = place("st_e", [R, SUP, 6])
    mv_e = place("mv_e", [R, SUP, 2])
    ve_e = place("ve_e", [R, SUP])
    nm_e = place("nm_e", [R, SUP])
    rs_e = place("rs_e", [R, SUP])
    nmr_e = place("nmr_e", [R, SUP])
    attr = place("attr", [P, SW])
    m_hi_t = place("m_hi_t", [P, K1, SW], F32R)
    m_lo_t = place("m_lo_t", [P, K1, SW], F32R)
    r32 = place("r32", [P, 2, SW])
    r_hi = place("r_hi", [P, DK, SW], F32R)
    r_lo = place("r_lo", [P, DK, SW], F32R)
    msg_hi = place("msg_hi", [R, 2, D], F32R)
    msg_lo = place("msg_lo", [R, D], F32R)
    same = place("same", [R, 2, R], F32R)
    trash = place("trash", [R, 1])
    row_no = place("row_no", [R, 1])
    sums = place("sums", [R, SUP, D])
    top_row = place("top_row", [R, EC])
    is_top = place("is_top", [R, EC])
    found = place("found", [R, GE * 8], U32)
    found_f = place("found_f", [R, GE * 8])
    add_scratch = cursor[0]
    paired = place("paired", [P, max(GE * 8 * 8, D)])
    paired = paired[0:R, 0:GE * 8 * 8].rearrange("p (q i j) -> p q i j", i=8, j=8)
    first_place = place("first_place", [R, GE * 8])
    slot_f = place("slot_f", [R, EC])
    add_all = place("add_all", [R, EC], I32)
    add_at = place("add_at", [R, SUP], I32)
    assert cursor[0] <= nc.sbuf_usable_end, (cursor[0], nc.sbuf_usable_end)
    all_size = (4 * E + 31) // 32 * 32
    assert 2 * all_size + 4 * D <= 4 * DK * G3
    all_same = nc.alloc_sbuf_tensor_at("all_same", [R, EC, R], F32, offset=region_b)
    all_dst_i = nc.alloc_sbuf_tensor_at("all_dst_i", [R, E], I32, offset=region_b)
    all_dst = nc.alloc_sbuf_tensor_at("all_dst", [R, EC, R], F32, offset=region_b + all_size)
    f2_last_hi = nc.alloc_sbuf_tensor_at("f2_last_hi", [P, D], F32R, offset=add_scratch)
    zeros = nc.alloc_sbuf_tensor_at("zeros", [R, D], F32, offset=region_b + 2 * all_size)

    small_in = sem("small_in")
    b1_in = sem("b1_in")
    b2_in = sem("b2_in")
    dst_in = sem("dst_in")
    agg_init = sem("agg_init")
    is_top_done = sem("is_top_done")
    iotas = sem("iotas")
    consts = sem("consts")
    bn_in = sem("bn_in")
    bn_step = sem("bn_step")
    bn_out = sem("bn_out")
    bn_back = sem("bn_back")
    staged = [sem("staged0"), sem("staged1")]
    stage_hi = sem("stage_hi")
    stage_lo = sem("stage_lo")
    attr_in = sem("attr_in")
    row_in = sem("row_in")
    dst_f_done = sem("dst_f_done")
    table_init = sem("table_init")
    src_ready = sem("src_ready")
    xs_in = [sem(f"xs_in{j}") for j in range(SUP)]
    stats_e = sem("stats_e")
    mv_ready = sem("mv_ready")
    var_e = sem("var_e")
    rs_ready = sem("rs_ready")
    nmr_ready = sem("nmr_ready")
    h_e = sem("h_e")
    t_e = sem("t_e")
    t_hi = sem("t_hi")
    t_lo = sem("t_lo")
    l1 = sem("l1")
    relu_done = sem("relu_done")
    r_hi_done = sem("r_hi_done")
    r_lo_done = sem("r_lo_done")
    l2 = sem("l2")
    msg_done = sem("msg_done")
    msg_hi_done = sem("msg_hi_done")
    msg_lo_done = sem("msg_lo_done")
    same_done = sem("same_done")
    summed = sem("summed")
    sums_done = sem("sums_done")
    all_dst_in = sem("all_dst_in")
    all_dst_ready = sem("all_dst_ready")
    all_compared = sem("all_compared")
    all_weighed = sem("all_weighed")
    top_step = sem("top_step")
    add_all_ready = sem("add_all_ready")
    f2_step = sem("f2_step")
    is_lo_step = sem("is_lo_step")
    add_at_ready = sem("add_at_ready")
    scattered = sem("scattered")

    w1v = w1t.rearrange("(k p) n -> p k n", p=P)
    w2v = w2t.rearrange("(k p) n -> p k n", p=P)
    wihv = wih_t.rearrange("(k p) n -> p k n", p=P)
    ew1v = ew1.rearrange("(k p) n -> p k n", p=P)
    ew2v = ew2.rearrange("(k p) n -> p k n", p=P)
    wgv = wg.rearrange("(k p) n -> p k n", p=P)
    ws1v = ws1.rearrange("(k p) n -> p k n", p=P)
    FW = KF - 1

    def wide(w, a, b, hi, lo, n):
        return [(lambda s: s[:, 0:(b - a) * n].rearrange("p (k n) -> p k n", n=n), w[:, a:b, :])], \
            (b - a) * n, hi[:, a:b, :], lo[:, a:b, :], n

    loads = [wide(w1v, 0, 3, w1_hi, w1_lo, D), wide(w1v, 3, 5, w1_hi, w1_lo, D),
             wide(w2v, 0, 3, w2_hi, w2_lo, D), wide(w2v, 3, 4, w2_hi, w2_lo, D)]
    loads += [wide(wihv, k, k + 1, wih_hi, wih_lo, G3) for k in range(DK)]
    loads += [([
        (lambda s: s[:, 0:DK * F1].rearrange("p (k n) -> p k n", n=F1)[:, :, 0:NE], wgv),
        (lambda s: s[:, 0:DK * F1].rearrange("p (k n) -> p k n", n=F1)[:, :, NE:NE + HE], ew1v),
        (lambda s: s[:, 0:DK * F1].rearrange("p (k n) -> p k n", n=F1)[:, :, NE + HE:F1], ws1v)],
        DK * F1, f1_hi[:, :, :], f1_lo[:, :, :], F1)]
    loads += [([
        (lambda s: s[:, 0:FW * D].rearrange("p (k n) -> p k n", n=D), ew2v),
        *[(lambda s, at=q * V + at, n=of.shape[0]: s[at:at + n, FW * D:KF * D], of) for q in range(3)
          for at, of in ((0, ws2), (HS, eb2), (HS + NE, bs2.rearrange("(o n) -> o n", o=1)))]],
        KF * D, f2_hi[:, :, :], f2_lo[:, :, :], D)]
    F2_LOAD = len(loads) - 1

    landed = []
    tally = [0, 0]
    for n, ld in enumerate(loads):
        tally[n % 2] += 16 * len(ld[0])
        landed.append(tally[n % 2])
    SPLITS = ({6: (4,), 7: (5,)}, {1: (6,), 2: (7,), 6: (8,), 7: (9,)})
    assert len(loads) == 10
    W1_LOADS, W2_LOADS = 2, 4

    rows_of_biases = [
        (hn_bias[:, :], b_hh[2 * D:G3]),
        (f1_bias[:, 0:NE], bg), (f1_bias[:, NE:NE + HE], eb1), (f1_bias[:, NE + HE:F1], bs1),
    ]

    def bcast(v):
        return v.rearrange("(o n) -> o n", o=1).broadcast_to((R, v.shape[0]))

    with nc.Block() as block:
        @block.sync
        def _(sp):
            sp.dma_start(src_i[:, :], src).then_inc(small_in, 16)
            for n in range(2):
                for to, of in loads[n][0]:
                    sp.dma_start(to(stage[:, n % 2, :]), of).then_inc(staged[n % 2], 16)
                if n == 0:
                    sp.dma_start(attr[:, :], attr_t[:, 0:SW]).then_inc(attr_in, 16)
            sp.wait_ge(xs_in[SUP - 1], 16)
            sp.dma_start(b1_col[:, :], b1).then_inc(b1_in, 16)
            sp.dma_start(dst_i[:, :], dst).then_inc(dst_in, 16)
            sp.dma_start(all_dst_i[:, :],
                         dst_rows.rearrange("(o g) r -> o (g r)", o=1).broadcast_to((R, E))).then_inc(all_dst_in, 16)
            sp.dma_start(row_i[:, :], dst_rows[0:1, :].broadcast_to((R, SW))).then_inc(row_in, 16)
            sp.dma_start(b2_row[:, :], bcast(b2)).then_inc(b2_in, 16)
            for n, of in enumerate((gamma, beta, run_mean, run_var)):
                sp.dma_start(bn_cols[:, n, :], of.rearrange("(p k) -> p k", p=P)).then_inc(bn_in, 16)

            def weights(a, b):
                for n in range(a, b):
                    sp.wait_ge(stage_lo, n - 1)
                    sp.wait_ge(stage_hi, n - 1)
                    if n == F2_LOAD:
                        sp.wait_ge(iotas, 8)
                    for to, of in loads[n][0]:
                        sp.dma_start(to(stage[:, n % 2, :]), of).then_inc(staged[n % 2], 16)

            def attributes(g):
                at = g * SW if isinstance(g, int) else sp.snap(g * SW)
                sp.wait_ge(t_lo, g * (SUP + 1) - SUP)
                sp.dma_start(attr[:, :], attr_t[:, bass.ds(at, SW)]).then_inc(attr_in, 16)

            def destinations(g):
                gg = g if isinstance(g, int) else sp.snap(g)
                sp.wait_ge(same_done, SUP * g)
                sp.dma_start(row_i[:, :], dst_rows[bass.ds(gg, 1), :].broadcast_to((R, SW))).then_inc(row_in, 16)

            weights(2, 4)
            attributes(1)
            sp.wait_ge(xs_in[SUP - 1], 32)
            sp.wait_ge(iotas, 7)
            sp.dma_start(agg.rearrange("(p k) d -> p k d", p=R),
                         zeros[:, :].unsqueeze(1).broadcast_to((R, EC + 1, D))).then_inc(agg_init, 16)
            sp.dma_start(slot_of_node.rearrange("(p t) o -> p (t o)", t=NT), node_init[:, :]).then_inc(table_init, 16)
            sp.wait_ge(bn_step, 5)
            sp.dma_start(bn_rows.rearrange("n (p k) -> p n k", p=P), bn_cols[:, 0:2, :]).then_inc(bn_out, 16)
            weights(4, 6)
            destinations(1)
            weights(6, 8)
            attributes(2)
            weights(8, len(loads))
            destinations(2)
            sp.wait_ge(bn_out, 16)
            for n, to in enumerate((bn_scale, bn_shift)):
                sp.dma_start(to[:, :], bn_rows[n:n + 1, :].broadcast_to((R, D))).then_inc(bn_back, 16)
            for to, of in rows_of_biases:
                sp.dma_start(to, bcast(of)).then_inc(bn_back, 16)
            with sp.Fori(3, NSUP) as g:
                attributes(g)
                destinations(g)
            sp.wait_ge(table_init, 16)
            sp.wait_ge(bn_back, 16 * (2 + len(rows_of_biases)))

        @block.gpsimd
        def _(pool):
            pool.memset(zeros[:, :], 0.0).then_inc(iotas, 1)
            pool.iota(iota_row[:, :], pattern=[[1, R]], base=0, channel_multiplier=0,
                      allow_small_or_imprecise_dtypes=True).then_inc(iotas, 1)
            pool.iota(iota8[:, :], pattern=[[1, NE]], base=0, channel_multiplier=0,
                      allow_small_or_imprecise_dtypes=True).then_inc(iotas, 1)
            pool.memset(minus_half[:, :], -0.5).then_inc(iotas, 1)
            pool.iota(node_init[:, :], pattern=[[0, NT]], base=E, channel_multiplier=1).then_inc(iotas, 1)
            pool.iota(trash[:, :], pattern=[[0, 1]], base=E, channel_multiplier=1,
                      allow_small_or_imprecise_dtypes=True).then_inc(iotas, 1)
            pool.iota(row_no[:, :], pattern=[[0, 1]], base=0, channel_multiplier=1,
                      allow_small_or_imprecise_dtypes=True).then_inc(iotas, 1)
            pool.memset(ones_col[:, :], 1.0)
            pool.memset(ident[:, :], 0.0).then_inc(consts, 1)
            pool.wait_ge(consts, 1)
            pool.affine_select(out=ident[:, :], in_=ident[:, :], compare_op=ALU.not_equal, fill=1.0, base=0,
                               pattern=[[-1, P]], channel_multiplier=1).then_inc(consts, 1)

            pool.iota(is_lo[:, :], pattern=[[0, 2]], base=0, channel_multiplier=1,
                      allow_small_or_imprecise_dtypes=True).then_inc(is_lo_step, 1)

            def gather_sources(g):
                pool.tensor_copy(src_at[:, :], src_i[:, bass.ds(g * SUP, SUP)]).then_inc(src_ready, 1)
                pool.wait_ge(src_ready, g + 1).then_inc(held["pool"], 1)
                for j in range(SUP):
                    pool.indirect_dma_start(out=xs[:, j, :], out_offset=None, in_=x,
                                            in_offset=bass.IndirectOffsetOnAxis(ap=src_at[:, j:j + 1], axis=0),
                                            ).then_inc(xs_in[j], 16)

            pool.wait_ge(small_in, 16)
            gather_sources(0)

            def front(g1):
                pool.wait_ge(var_e, g1 + 1)
                pool.tensor_tensor(rs_e[:, :], ve_e[:, :], minus_half[0:R, :], ALU.pow).then_inc(rs_ready, 1)
                pool.wait_ge(rs_ready, g1 + 1)
                pool.tensor_tensor(nmr_e[:, :], nm_e[:, :], rs_e[:, :], ALU.mult).then_inc(nmr_ready, 1)

            def add(g, first, last):
                ready = [pool.snap(g * SUP + j + 1) for j in range(first, last)]
                written = [pool.snap(16 * (g * SUP + j + 1)) for j in range(first, last)]
                if first == 0:
                    copied = pool.snap(g + 1)
                    pool.tensor_copy(add_at[:, :], add_all[:, bass.ds(g * SUP, SUP)]).then_inc(add_at_ready, 1)
                    pool.wait_ge(add_at_ready, copied).then_inc(held["pool"], 1)
                for j in range(first, last):
                    pool.wait_ge(sums_done, ready[j - first]).then_inc(held["pool"], 1)
                    pool.indirect_dma_start(out=agg, in_=sums[:, j, :], in_offset=None,
                                            out_offset=bass.IndirectOffsetOnAxis(ap=add_at[:, j:j + 1], axis=0),
                                            compute_op=ALU.add).then_inc(scattered, 16)
                    pool.wait_ge(scattered, written[j - first]).then_inc(held["pool"], 1)

            front(0)
            pool.wait_ge(h_e, SUP)
            gather_sources(1)

            bn_gamma, bn_beta, bn_mean, bn_var = (bn_cols[:, n, :] for n in range(4))
            pool.wait_ge(bn_step, 1)
            pool.tensor_tensor(bn_var, bn_var, minus_half[:, :], ALU.pow).then_inc(bn_step, 1)
            pool.wait_ge(bn_step, 2)
            pool.tensor_tensor(bn_gamma, bn_gamma, bn_var, ALU.mult).then_inc(bn_step, 1)
            pool.wait_ge(bn_step, 3)
            pool.tensor_tensor(bn_mean, bn_mean, bn_gamma, ALU.mult).then_inc(bn_step, 1)
            pool.wait_ge(bn_step, 4)
            pool.tensor_tensor(bn_beta, bn_beta, bn_mean, ALU.subtract).then_inc(bn_step, 1)

            front(1)
            pool.wait_ge(h_e, 2 * SUP)
            gather_sources(2)
            pool.wait_ge(all_compared, 1)
            pool.tensor_tensor(all_same[:, :, :], all_same[:, :, :],
                               iota_row[:, :].unsqueeze(1).broadcast_to((R, EC, R)), ALU.mult).then_inc(all_weighed, 1)
            pool.wait_ge(agg_init, 16)
            pool.wait_ge(add_all_ready, 3)
            add(0, 0, SUP - 1)
            with pool.Fori(1, NSUP - 2) as g:
                front(g + 1)
                pool.wait_ge(h_e, SUP * (g + 2)).then_inc(held["pool"], 1)
                gather_sources(g + 2)
                add(g - 1, SUP - 1, SUP)
                add(g, 0, SUP - 1)
            front(NSUP - 1)
            for g in (NSUP - 2, NSUP - 1):
                add(g - 1, SUP - 1, SUP)
                add(g, 0, SUP - 1)
            add(NSUP - 1, SUP - 1, SUP)

        @block.scalar
        def _(act):
            def split_hi(n):
                act.wait_ge(staged[n % 2], landed[n])
                if n == W2_LOADS:
                    act.wait_ge(top_step, 1 + GE)
                    act.wait_ge(agg_init, 16)
                _, width, hi, _, cols = loads[n]
                if n == F2_LOAD:
                    width, hi = FW * D, f2_hi[:, 0:FW, :]
                act.activation(hi, stage[:, n % 2, 0:width].rearrange("p (k n) -> p k n", n=cols), ACT.Copy)\
                    .then_inc(stage_hi, 1)

            def normalise(g1):
                act.wait_ge(nmr_ready, g1 + 1)
                if not isinstance(g1, int) or g1 > 0:
                    act.wait_ge(t_e, SUP * g1)
                for j in range(SUP):
                    act.activation(hs[:, j, :], xs[:, j, :], ACT.Identity, bias=nmr_e[:, j:j + 1],
                                   scale=rs_e[:, j:j + 1]).then_inc(h_e, 1)

            def attributes_hi(g1):
                wait_from(act, l1, DK * g1)
                act.wait_ge(attr_in, 16 * (g1 + 1))
                act.activation(m_hi_t[:, K1 - 1, :], attr[:, :], ACT.Copy).then_inc(t_hi, 1)

            def transposed_hi(g1, j):
                act.wait_ge(t_e, SUP * g1 + j + 1)
                act.activation(m_hi_t[:, 0:DK, j * R:(j + 1) * R],
                               bank[2 + j % 2][:, 0:DK * R].rearrange("p (k r) -> p k r", k=DK),
                               ACT.Copy).then_inc(t_hi, 1)

            def layer1(g, b):
                act.wait_ge(l1, DK * g + b + 1)
                wait_from(act, r_lo_done, DK * g + b - 1)
                act.activation(r32[:, b % 2, :], bank[b % 2][:, 0:SW], ACT.Relu, bias=b1_col[:, b:b + 1])\
                    .then_inc(relu_done, 1)
                act.wait_ge(relu_done, DK * g + b + 1)
                if b == 0:
                    wait_from(act, l2, SUP * g)
                act.activation(r_hi[:, b, :], r32[:, b % 2, :], ACT.Copy).then_inc(r_hi_done, 1)

            def take_sums(g, j):
                act.wait_ge(summed, SUP * g + j + 1)
                wait_from(act, scattered, 16 * (SUP * g + j - SUP + 1))
                act.activation(sums[:, j, :], bank[6 + j % 2][0:R, :], ACT.Copy).then_inc(sums_done, 1)

            def split_hi_of(splits, place):
                for n in splits.get(place, ()):
                    split_hi(n)

            def supertile(g, first, last, splits):
                layer1(g, 0)
                if not first:
                    take_sums(g - 1, SUP - 1)
                layer1(g, 1)
                if not last:
                    normalise(g + 1)
                split_hi_of(splits, 1)
                layer1(g, 2)
                split_hi_of(splits, 2)
                layer1(g, 3)
                if not last:
                    attributes_hi(g + 1)
                    transposed_hi(g + 1, 0)
                    transposed_hi(g + 1, 1)
                for j in range(SUP):
                    act.wait_ge(msg_done, SUP * g + j + 1)
                    wait_from(act, summed, SUP * g + j - 1)
                    act.activation(msg_hi[:, j % 2, :], msg[:, :], ACT.Copy).then_inc(msg_hi_done, 1)
                    if j < 2 and not last:
                        transposed_hi(g + 1, j + 2)
                    if j > 0:
                        take_sums(g, j - 1)
                    split_hi_of(splits, 4 + j)

            for n in range(2):
                split_hi(n)
            normalise(0)
            attributes_hi(0)
            for j in range(SUP):
                transposed_hi(0, j)
            split_hi(2)
            split_hi(3)
            act.wait_ge(b1_in, 16)
            supertile(0, True, False, SPLITS[0])
            supertile(1, False, False, SPLITS[1])
            with act.Fori(2, NSUP - 1) as g:
                supertile(g, False, False, {})
            supertile(NSUP - 1, False, True, {})
            take_sums(NSUP - 1, SUP - 1)

        @block.vector
        def _(dve):
            def split_lo(n):
                dve.wait_ge(stage_hi, n + 1)
                _, width, hi, lo, cols = loads[n]
                if n == F2_LOAD:
                    dve.wait_ge(staged[n % 2], landed[n])
                    last = stage[:, n % 2, FW * D:KF * D]
                    dve.tensor_copy(f2_last_hi[:, :], last).then_inc(f2_step, 1)
                    dve.wait_ge(f2_step, 1)
                    dve.tensor_tensor(last, last, f2_last_hi[:, :].bitcast(F32), ALU.subtract).then_inc(f2_step, 1)
                    dve.wait_ge(f2_step, 2)
                    dve.tensor_scalar(last, last, is_lo[:, 0:1], None, ALU.mult).then_inc(f2_step, 1)
                    dve.wait_ge(f2_step, 3)
                    dve.scalar_tensor_tensor(f2_hi[:, FW, :], f2_last_hi[:, :].bitcast(F32), is_lo[:, 1:2], last,
                                             ALU.mult, ALU.add).then_inc(f2_step, 1)
                    dve.wait_ge(f2_step, 4)
                    width, hi = FW * D, f2_hi[:, 0:FW, :]
                dve.tensor_tensor(lo, stage[:, n % 2, 0:width].rearrange("p (k n) -> p k n", n=cols),
                                  hi.bitcast(F32), ALU.subtract).then_inc(stage_lo, 1)
                if n == F2_LOAD - 2:
                    dve.wait_ge(stage_lo, n + 1)
                    dve.memset(stage[:, F2_LOAD % 2, FW * D:KF * D], 0.0).then_inc(iotas, 1)

            def stats(g1):
                if not isinstance(g1, int) or g1 > 0:
                    dve.wait_ge(nmr_ready, g1)
                for j in range(SUP):
                    dve.wait_ge(xs_in[j], 16 * (g1 + 1))
                    dve.bn_stats(st_e[:, j, :], xs[:, j, :]).then_inc(stats_e, 1)
                dve.wait_ge(stats_e, SUP * (g1 + 1)).then_inc(held["dve"], 1)
                for j in range(SUP):
                    dve.bn_aggr(mv_e[:, j, :], st_e[:, j, :]).then_inc(mv_ready, 1)
                dve.wait_ge(mv_ready, SUP * (g1 + 1))
                dve.tensor_scalar(nm_e[:, :], mv_e[:, :, 0], -1.0, None, ALU.mult)
                dve.tensor_scalar(ve_e[:, :], mv_e[:, :, 1], EPS, None, ALU.add).then_inc(var_e, 1)

            def take_destinations():
                dve.wait_ge(all_dst_in, 16)
                dve.tensor_copy(all_dst[:, :, :], all_dst_i[:, :].rearrange("p (c r) -> p c r", r=R)).then_inc(all_dst_ready, 1)

            def compare():
                dve.wait_ge(all_dst_ready, 1)
                dve.tensor_tensor(all_same[:, :, :], all_dst[:, :, :],
                                  dst_f[:, 0:EC].unsqueeze(2).broadcast_to((R, EC, R)), ALU.is_equal)\
                    .then_inc(all_compared, 1)

            def top_rows():
                dve.wait_ge(all_weighed, 1)
                dve.tensor_reduce(top_row[:, :], all_same[:, :, :], AX_X, ALU.max).then_inc(top_step, 1)

            def find(q):
                dve.max_index(found[:, 8 * q:8 * q + 8], dst_f[:, 8 * q:8 * q + 8],
                              all_dst[:, :, :].rearrange("p c r -> p (c r)")).then_inc(top_step, 1)

            def slots():
                dve.wait_ge(top_step, 1 + GE)
                dve.tensor_scalar(is_top[:, :], top_row[:, :], row_no[:, 0:1], None, ALU.is_equal).then_inc(is_top_done, 1)
                dve.tensor_copy(found_f[:, :], found[:, :]).then_inc(top_step, 1)
                dve.wait_ge(top_step, 2 + GE)
                dve.tensor_scalar(found_f[:, :], found_f[:, :], -1.0, float(E), ALU.mult, ALU.add).then_inc(top_step, 1)
                groups = dst_f[:, :].rearrange("p (q i) -> p q i", i=8)
                dve.tensor_tensor(paired[:, :, :, :], groups.unsqueeze(3).broadcast_to((R, GE, 8, 8)),
                                  groups.unsqueeze(2).broadcast_to((R, GE, 8, 8)), ALU.is_equal).then_inc(top_step, 1)
                dve.wait_ge(top_step, 4 + GE)
                dve.tensor_tensor(paired[:, :, :, :], paired[:, :, :, :],
                                  found_f[:, :].rearrange("p (q i) -> p q i", i=8).unsqueeze(2)
                                  .broadcast_to((R, GE, 8, 8)), ALU.mult).then_inc(top_step, 1)
                dve.wait_ge(top_step, 5 + GE)
                dve.tensor_reduce(first_place[:, :].rearrange("p (q i) -> p q i", i=8), paired[:, :, :, :], AX_X, ALU.max)\
                    .then_inc(top_step, 1)
                dve.wait_ge(top_step, 6 + GE)
                dve.tensor_scalar(slot_f[:, :], first_place[:, 0:EC], -1.0, float(E), ALU.mult, ALU.add).then_inc(top_step, 1)
                dve.wait_ge(top_step, 7 + GE)
                dve.tensor_copy(slot_i[:, :], slot_f[:, :]).then_inc(top_step, 1)
                dve.tensor_scalar(slot_f[:, :], slot_f[:, :], trash[:, 0:1], None, ALU.subtract).then_inc(add_all_ready, 1)
                dve.wait_ge(is_top_done, 1)
                dve.wait_ge(add_all_ready, 1)
                dve.tensor_tensor(slot_f[:, :], slot_f[:, :], is_top[:, :], ALU.mult).then_inc(add_all_ready, 1)
                dve.wait_ge(add_all_ready, 2)
                dve.tensor_scalar(add_all[:, :], slot_f[:, :], trash[:, 0:1], None, ALU.add).then_inc(add_all_ready, 1)

            def attributes_lo(g1):
                wait_from(dve, l1, DK * g1)
                dve.wait_ge(t_hi, (SUP + 1) * g1 + 1)
                dve.tensor_tensor(m_lo_t[:, K1 - 1, :], attr[:, :], m_hi_t[:, K1 - 1, :].bitcast(F32), ALU.subtract)\
                    .then_inc(t_lo, 1)

            def transposed_lo(g1, j):
                dve.wait_ge(t_hi, (SUP + 1) * g1 + j + 2)
                dve.tensor_tensor(m_lo_t[:, 0:DK, j * R:(j + 1) * R],
                                  bank[2 + j % 2][:, 0:DK * R].rearrange("p (k r) -> p k r", k=DK),
                                  m_hi_t[:, 0:DK, j * R:(j + 1) * R].bitcast(F32), ALU.subtract).then_inc(t_lo, 1)

            def layer1(g, b):
                if b == 0:
                    wait_from(dve, l2, SUP * g)
                dve.wait_ge(r_hi_done, DK * g + b + 1)
                dve.tensor_tensor(r_lo[:, b, :], r32[:, b % 2, :], r_hi[:, b, :].bitcast(F32), ALU.subtract)\
                    .then_inc(r_lo_done, 1)

            def supertile(g, first, last, splits):
                for b in range(DK):
                    layer1(g, b)
                    if first and b == 0:
                        compare()
                    elif first:
                        find(b - 1)
                    for n in splits.get(b, ()):
                        split_lo(n)
                if not last:
                    attributes_lo(g + 1)
                    transposed_lo(g + 1, 0)
                    transposed_lo(g + 1, 1)
                for j in range(SUP):
                    dve.wait_ge(l2, SUP * g + j + 1)
                    wait_from(dve, msg_hi_done, SUP * g + j)
                    wait_from(dve, msg_lo_done, SUP * g + j)
                    dve.tensor_tensor(msg[:, :], bank[4 + j % 2][0:R, :], b2_row[:, :], ALU.add).then_inc(msg_done, 1)
                    dve.wait_ge(row_in, 16 * (g + 1))
                    wait_from(dve, summed, SUP * g + j - 1)
                    dve.tensor_scalar(same[:, j % 2, :], row_i[:, j * R:(j + 1) * R],
                                      dst_f[:, bass.ds(SUP * g + j, 1)], None, ALU.is_equal).then_inc(same_done, 1)
                    dve.wait_ge(msg_hi_done, SUP * g + j + 1)
                    wait_from(dve, summed, SUP * g + j)
                    dve.tensor_tensor(msg_lo[:, :], msg[:, :], msg_hi[:, j % 2, :].bitcast(F32), ALU.subtract)\
                        .then_inc(msg_lo_done, 1)
                    if j < 2 and not last:
                        transposed_lo(g + 1, j + 2)
                    if first and j == 0:
                        top_rows()
                    elif first and j == 1:
                        slots()
                    for n in splits.get(4 + j, ()):
                        split_lo(n)

            dve.memset(dst_f[:, :], -1.0).then_inc(dst_f_done, 1)
            for n in range(2):
                split_lo(n)
            stats(0)
            attributes_lo(0)
            for j in range(SUP):
                transposed_lo(0, j)
            split_lo(2)
            split_lo(3)
            dve.wait_ge(is_lo_step, 1)
            dve.tensor_scalar(is_lo[:, 1:2], is_lo[:, 0:1], float(V), None, ALU.is_ge).then_inc(is_lo_step, 1)
            dve.tensor_scalar(is_lo[:, 0:1], is_lo[:, 0:1], float(2 * V), None, ALU.is_lt).then_inc(is_lo_step, 1)
            dve.wait_ge(is_lo_step, 3)
            dve.tensor_tensor(is_lo[:, 0:1], is_lo[:, 0:1], is_lo[:, 1:2], ALU.mult).then_inc(is_lo_step, 1)
            dve.wait_ge(is_lo_step, 4)
            dve.tensor_scalar(is_lo[:, 1:2], is_lo[:, 0:1], -1.0, 1.0, ALU.mult, ALU.add).then_inc(is_lo_step, 1)
            dve.wait_ge(is_lo_step, 5)
            dve.wait_ge(bn_in, 64)
            dve.tensor_scalar(bn_cols[:, 3, :], bn_cols[:, 3, :], EPS, None, ALU.add).then_inc(bn_step, 1)
            dve.wait_ge(dst_in, 16)
            dve.wait_ge(dst_f_done, 1)
            dve.tensor_copy(dst_f[:, 0:EC], dst_i[:, :]).then_inc(dst_f_done, 1)
            dve.wait_ge(iotas, 7)
            dve.wait_ge(dst_f_done, 2)
            stats(1)
            assert GE == SUP - 1
            take_destinations()
            dve.wait_ge(b2_in, 16)
            supertile(0, True, False, SPLITS[0])
            stats(2)
            supertile(1, False, False, SPLITS[1])
            with dve.Fori(2, NSUP - 1) as g:
                stats(g + 1)
                supertile(g, False, False, {})
            supertile(NSUP - 1, False, True, {})

        @block.tensor
        def _(pe):
            def transposes(g1, j):
                pe.wait_ge(h_e, SUP * g1 + j + 1)
                wait_from(pe, t_lo, (SUP + 1) * g1 + j if j >= 2 else (SUP + 1) * g1 + j - 1)
                for k in range(DK):
                    last = pe.transpose(bank[2 + j % 2][:, k * R:(k + 1) * R], hs[:, j, k * P:(k + 1) * P],
                                        ident[0:R, 0:R])
                last.then_inc(t_e, 1)

            def layer1(g, b):
                if b == 0:
                    pe.wait_ge(t_lo, (SUP + 1) * (g + 1))
                wait_from(pe, relu_done, DK * g + b - 1)
                n = 0
                for k in range(K1):
                    for w, m in ((w1_hi, m_hi_t), (w1_hi, m_lo_t), (w1_lo, m_hi_t)):
                        last = pe.matmul(bank[b % 2][:, 0:SW], w[:, k, b * P:(b + 1) * P], m[:, k, :],
                                         start=n == 0, stop=n == 3 * K1 - 1)
                        n += 1
                last.then_inc(l1, 1)

            def tile_sums(g, j):
                pe.wait_ge(msg_lo_done, SUP * g + j + 1)
                wait_from(pe, sums_done, SUP * g + j - 1)
                pe.matmul(bank[6 + j % 2][0:R, :], same[:, j % 2, :], msg_hi[:, j % 2, :], start=True, stop=False)
                pe.matmul(bank[6 + j % 2][0:R, :], same[:, j % 2, :], msg_lo[:, :], start=False, stop=True)\
                    .then_inc(summed, 1)

            def layer2(g, j):
                wait_from(pe, msg_done, SUP * g + j - 1)
                n = 0
                for k in range(DK):
                    if j == 0:
                        pe.wait_ge(r_lo_done, DK * g + k + 1)
                    for r, w in ((r_hi, w2_hi), (r_hi, w2_lo), (r_lo, w2_hi)):
                        last = pe.matmul(bank[4 + j % 2][0:R, :], r[:, k, j * R:(j + 1) * R], w[:, k, :],
                                         start=n == 0, stop=n == 3 * DK - 1)
                        n += 1
                last.then_inc(l2, 1)

            def supertile(g, first, last):
                for b in range(DK):
                    layer1(g, b)
                    if b == 0 and not first:
                        tile_sums(g - 1, SUP - 1)
                if not last:
                    transposes(g + 1, 0)
                    transposes(g + 1, 1)
                if first:
                    pe.wait_ge(stage_lo, W2_LOADS)
                for j in range(SUP):
                    layer2(g, j)
                    if j < 2 and not last:
                        transposes(g + 1, j + 2)
                    if j > 0:
                        tile_sums(g, j - 1)

            pe.wait_ge(consts, 2)
            for j in range(SUP):
                transposes(0, j)
            pe.wait_ge(stage_lo, W1_LOADS)
            supertile(0, True, False)
            with pe.Fori(1, NSUP - 1) as g:
                supertile(g, False, False)
            supertile(NSUP - 1, False, True)
            tile_sums(NSUP - 1, SUP - 1)

    cursor[0] = region_c
    ig_bias = place("ig_bias", [R, G3])
    ig_bhh = place("ig_bhh", [R, 2 * D])
    agg_in = place("agg_in", [R, 2, D])
    a_hi = place("a_hi", [P, 2, DK * R], F32R)
    a_lo = place("a_lo", [P, 2, DK * R], F32R)
    g_out = place("g_out", [R, 2, G3])
    stage2 = place("stage2", [P, 2, G3])
    dst_at = place("dst_at", [R, SUP], I32)
    slot_at4 = place("slot_at4", [R, SUP], I32)
    assert cursor[0] <= nc.sbuf_usable_end

    index_copied = sem("index_copied")
    slots_in = sem("slots_in")
    bias_in = sem("bias_in")
    bias_done = sem("bias_done")
    staged2 = [sem("staged2_0"), sem("staged2_1")]
    stage2_hi = sem("stage2_hi")
    stage2_lo = sem("stage2_lo")
    agg_loaded = [sem("agg_loaded0"), sem("agg_loaded1")]
    t_a = sem("t_a")
    a_hi_done = sem("a_hi_done")
    a_lo_done = sem("a_lo_done")
    g_prod = sem("g_prod")
    g_added = sem("g_added")
    g_stored = [sem("g_stored0"), sem("g_stored1")]
    bias_stored = sem("bias_stored")

    whhv = whh_t.rearrange("(k p) n -> p k n", p=P)

    FIRST, UNROLL = 4, 4
    assert FIRST % UNROLL == 0
    early_nodes = cursor[0]
    node_slot = place("node_slot", [R, NT], I32)
    slot_at = place("slot_at", [R, 2], I32)
    xt = place("xt", [R, 2, D])
    h = place("h", [R, 2, D])
    x_h = place("x_h", [R, 2, D])
    x_h_b = place("x_h_b", [R, 2, D])
    h_hi = place("h_hi", [P, 2, DK * R], F32R)
    h_lo = place("h_lo", [P, 2, DK * R], F32R)
    gates = place("gates", [R, 2, G3])
    st = {k: place(f"st{k}", [R, 6]) for k in (1, 2)}
    mv = {k: place(f"mv{k}", [R, 2]) for k in (1, 2)}
    var_eps = {k: place(f"var_eps{k}", [R, 1]) for k in (1, 2)}
    neg_mean = {k: place(f"neg_mean{k}", [R, 1]) for k in (1, 2)}
    rstd = {k: place(f"rstd{k}", [R, 2]) for k in (1, 2)}
    shift = {k: place(f"shift{k}", [R, 2]) for k in (1, 2)}
    one_rstd = place("one_rstd", [R, 2])
    assert cursor[0] <= nc.sbuf_usable_end, (cursor[0], nc.sbuf_usable_end)
    cursor[0] = region_b
    hn_raw = place("hn_raw", [R, 2, D])
    hn = place("hn", [R, 2, D])
    r_pre = place("r_pre", [R, D])
    r_gate = place("r_gate", [R, D])
    z_pre = place("z_pre", [R, D])
    z_gate = place("z_gate", [R, D])
    r_hn = place("r_hn", [R, D])
    n_pre = place("n_pre", [R, D])
    n_gate = place("n_gate", [R, 2, D])
    h_n = place("h_n", [R, D])
    z_h_n = place("z_h_n", [R, D])
    h_new = place("h_new", [R, D])
    scaled = place("scaled", [R, D])
    x1 = place("x1", [R, UNROLL, D])
    h2 = place("h2", [R, 2, D])
    h2_hi = place("h2_hi", [P, DK * R], F32R)
    h2_lo = place("h2_lo", [P, DK * R], F32R)
    f1 = place("f1", [R, F1])
    hid = place("hid", [R, 2, KF * P])
    extra = place("extra", [R, V])
    extra_hi = place("extra_hi", [R, V], F32R)
    hid_hi = place("hid_hi", [P, KF * R], F32R)
    hid_lo = place("hid_lo", [P, (KF - 1) * R], F32R)
    y = place("y", [R, 2, D])
    top = place("top", [R, 8])
    top_i = place("top_i", [R, 8], U32)
    top_f = place("top_f", [R, 2])
    gap = place("gap", [R, 1])
    weight = place("weight", [R, 2])
    comb1 = place("comb1", [R, NE])
    comb2 = place("comb2", [R, NE])
    assert cursor[0] <= early_nodes

    b_r, b_z, b_n, b_th2, b_f1, b_f2, b_th, b_thid = bank

    table_in = sem("table_in")
    hid_set = sem("hid_set")
    x_in = [sem("x_in0"), sem("x_in1")]
    slot_copied = sem("slot_copied")
    gates_loaded = [sem("gates_loaded0"), sem("gates_loaded1")]
    st_done = {k: sem(f"st_done{k}") for k in (1, 2)}
    mv_done = {k: sem(f"mv_done{k}") for k in (1, 2)}
    var_done = {k: sem(f"var_done{k}") for k in (1, 2)}
    rstd_done = {k: sem(f"rstd_done{k}") for k in (1, 2)}
    shift_done = {k: sem(f"shift_done{k}") for k in (1, 2)}
    h_done = sem("h_done")
    x_h_done = sem("x_h_done")
    x_h_b_done = sem("x_h_b_done")
    h_turned = sem("h_turned")
    h_hi_done = sem("h_hi_done")
    h_lo_done = sem("h_lo_done")
    n_prod = sem("n_prod")
    r_prod = sem("r_prod")
    z_prod = sem("z_prod")
    hn_raw_done = sem("hn_raw_done")
    hn_done = sem("hn_done")
    r_pre_done = sem("r_pre_done")
    r_done = sem("r_done")
    z_pre_done = sem("z_pre_done")
    z_done = sem("z_done")
    r_hn_done = sem("r_hn_done")
    n_pre_done = sem("n_pre_done")
    n_done = sem("n_done")
    h_n_done = sem("h_n_done")
    z_h_n_done = sem("z_h_n_done")
    h_new_done = sem("h_new_done")
    scaled_done = sem("scaled_done")
    x1_done = sem("x1_done")
    h2_done = sem("h2_done")
    h2_turned = sem("h2_turned")
    h2_hi_done = sem("h2_hi_done")
    h2_lo_done = sem("h2_lo_done")
    f1_prod = sem("f1_prod")
    f1_done = sem("f1_done")
    top_done = sem("top_done")
    top_i_done = sem("top_i_done")
    gap_done = sem("gap_done")
    weight_done = sem("weight_done")
    comb1_done = sem("comb1_done")
    comb2_done = sem("comb2_done")
    comb_done = sem("comb_done")
    shared_done = sem("shared_done")
    extra_hi_done = sem("extra_hi_done")
    hid_done = sem("hid_done")
    hid_turned = sem("hid_turned")
    hid_hi_done = sem("hid_hi_done")
    hid_lo_done = sem("hid_lo_done")
    f2_prod = sem("f2_prod")
    y_done = sem("y_done")
    y_stored = [sem("y_stored0"), sem("y_stored1")]

    x_tiles = x.rearrange("(p t) d -> p t d", t=NT)
    out_tiles = out.rearrange("(p t) d -> p t d", t=NT)

    LOOPS = (NT - 2 - FIRST) // UNROLL

    class Period:
        def __init__(self, i, j):
            self.i, self.j = i, j
            self.t = FIRST + UNROLL * i + j

        def has(self, k):
            return not isinstance(self.i, int) or 0 <= self.t + k < NT

        def first(self, k):
            return isinstance(self.i, int) and self.t + k == 0

        def early(self, k):
            return isinstance(self.i, int) and self.t + k < 2

        def slot(self, k):
            return (self.j + k) % 2

        def slot4(self, k):
            return (self.j + k) % 4

        def turn(self, k):
            return UNROLL // 2 * self.i + (FIRST + self.j + k - self.slot(k)) // 2

    def periods(eng, body):
        for j in range(-FIRST - 2, 0):
            body(Period(0, j))
        with eng.Fori(0, LOOPS) as i:
            for j in range(UNROLL):
                body(Period(i, j))
        for j in range(NT + 2 - FIRST - UNROLL * LOOPS):
            body(Period(LOOPS, j))

    def statistics(dve, p, k, which):
        t = p.t
        dve.wait_ge(st_done[which], t + k + 1).then_inc(held["dve"], 1)
        dve.bn_aggr(mv[which][:, :], st[which][:, :]).then_inc(mv_done[which], 1)

    def mean_var(dve, p, k, which):
        t = p.t
        dve.wait_ge(mv_done[which], t + k + 1)
        wait_from(dve, shift_done[which], (3 - which) * (t + k))
        dve.tensor_scalar(neg_mean[which][:, :], mv[which][:, 0:1], -1.0, None, ALU.mult)
        dve.tensor_scalar(var_eps[which][:, :], mv[which][:, 1:2], EPS, None, ALU.add)\
            .then_inc(var_done[which], 1)

    def first_norm(dve, p):
        s = p.slot(2)
        dve.wait_ge(x_in[s], 16 * (p.turn(2) + 1))
        dve.bn_stats(st[1][:, :], xt[:, s, :]).then_inc(st_done[1], 1)
        statistics(dve, p, 2, 1)
        mean_var(dve, p, 2, 1)

    def h_low(dve, p):
        s = p.slot(1)
        dve.wait_ge(h_hi_done, p.t + 2)
        dve.tensor_tensor(h_lo[:, s, :], b_th[:, 0:DK * R], h_hi[:, s, :].bitcast(F32), ALU.subtract)\
            .then_inc(h_lo_done, 1)

    def turn(pe, to, rows_of, chunks):
        for k in range(chunks):
            last = pe.transpose(to[:, k * R:(k + 1) * R], rows_of[:, k * P:(k + 1) * P], ident[0:R, 0:R])
        return last

    def turn_h(pe, p):
        pe.wait_ge(h_done, p.t + 2)
        wait_from(pe, h_lo_done, p.t + 1)
        turn(pe, b_th, h[:, p.slot(1), :], DK).then_inc(h_turned, 1)

    with nc.Block() as block:
        @block.sync
        def _(sp):
            def load(c, s):
                sp.dma_start(agg_in[:, s, :], agg[bass.ds(c * R, R), :]).then_inc(agg_loaded[s], 16)

            for c in range(2):
                load(c, c)
            sp.dma_start(ig_bias[:, :], bcast(b_ih)).then_inc(bias_in, 16)
            sp.dma_start(ig_bhh[:, :], bcast(b_hh[0:2 * D])).then_inc(bias_in, 16)
            sp.dma_start(stage2[:, 0, :], whhv[:, 0, :]).then_inc(staged2[0], 16)
            sp.dma_start(stage2[:, 1, :], whhv[:, 1, :]).then_inc(staged2[1], 16)
            for c in range(2, 4):
                sp.wait_ge(t_a, c - 1)
                load(c, c % 2)
            sp.wait_ge(bias_done, 1)
            sp.dma_start(gates_in[E:E + R, :], ig_bias[:, :]).then_inc(bias_stored, 16)
            for c in range(2):
                sp.wait_ge(stage2_lo, c + 1)
                sp.dma_start(stage2[:, c, :], whhv[:, 2 + c, :]).then_inc(staged2[c], 16)
            for t in range(2):
                sp.dma_start(xt[:, t, :], x_tiles[:, t, :]).then_inc(x_in[t], 16)
            for c in range(2):
                sp.wait_ge(g_added, 3 * (c + 1))
                sp.dma_start(gates_in[c * R:(c + 1) * R, :], g_out[:, c, :]).then_inc(g_stored[c], 16)
            with sp.Fori(2, EC // 2) as i:
                row = [sp.snap((2 * i + s) * R) for s in range(2)]
                past = [sp.snap((2 * i + s - 2) * R) for s in range(2)]
                for s in range(2):
                    sp.wait_ge(t_a, 2 * i + s - 1)
                    sp.dma_start(agg_in[:, s, :], agg[bass.ds(row[s], R), :]).then_inc(agg_loaded[s], 16)
                for s in range(2):
                    sp.wait_ge(g_added, 3 * (2 * i + s - 1))
                    sp.dma_start(gates_in[bass.ds(past[s], R), :], g_out[:, s, :]).then_inc(g_stored[s], 16)
            for s in range(2):
                c = EC - 2 + s
                sp.wait_ge(g_added, 3 * (c + 1))
                sp.dma_start(gates_in[c * R:(c + 1) * R, :], g_out[:, s, :]).then_inc(g_stored[s], 16)

        @block.gpsimd
        def _(pool):
            with pool.Fori(0, NSUP) as g:
                copied = pool.snap(2 * (g + 1))
                entered = [pool.snap(16 * (g * SUP + j + 1)) for j in range(SUP)]
                at = bass.ds(g * SUP, SUP)
                pool.tensor_copy(dst_at[:, :], dst_i[:, at]).then_inc(index_copied, 1)
                pool.tensor_copy(slot_at4[:, :], slot_i[:, at]).then_inc(index_copied, 1)
                pool.wait_ge(index_copied, copied).then_inc(held["pool"], 1)
                for j in range(SUP):
                    pool.indirect_dma_start(out=slot_of_node, in_=slot_at4[:, j:j + 1], in_offset=None,
                                            out_offset=bass.IndirectOffsetOnAxis(ap=dst_at[:, j:j + 1], axis=0),
                                            ).then_inc(slots_in, 16)
                    pool.wait_ge(slots_in, entered[j]).then_inc(held["pool"], 1)

        @block.scalar
        def _(act):
            def hi(c, s):
                act.wait_ge(t_a, c + 1)
                wait_from(act, g_prod, 3 * (c - 1))
                act.activation(a_hi[:, s, :], bank[6 + s][:, 0:DK * R], ACT.Copy).then_inc(a_hi_done, 1)

            hi(0, 0)
            for k in range(2):
                act.wait_ge(staged2[k], 16)
                act.activation(whh_hi[:, k, :], stage2[:, k, :], ACT.Copy).then_inc(stage2_hi, 1)
            hi(1, 1)
            hi(2, 0)
            hi(3, 1)
            for k in range(2, 4):
                act.wait_ge(staged2[k % 2], 32)
                act.activation(whh_hi[:, k, :], stage2[:, k % 2, :], ACT.Copy).then_inc(stage2_hi, 1)
            with act.Fori(2, EC // 2) as i:
                for s in range(2):
                    hi(2 * i + s, s)

        @block.vector
        def _(dve):
            def lo(c, s):
                dve.wait_ge(a_hi_done, c + 1)
                dve.tensor_tensor(a_lo[:, s, :], bank[6 + s][:, 0:DK * R], a_hi[:, s, :].bitcast(F32), ALU.subtract)\
                    .then_inc(a_lo_done, 1)

            def add_bias(c, s, i):
                if not isinstance(i, int) or i > 0:
                    dve.wait_ge(g_stored[s], 16 * i)
                for q in range(3):
                    dve.wait_ge(g_prod, 3 * c + q + 1)
                    dve.tensor_tensor(g_out[:, s, q * D:(q + 1) * D], bank[3 * s + q][0:R, :],
                                      ig_bias[:, q * D:(q + 1) * D], ALU.add).then_inc(g_added, 1)

            def split(k):
                dve.wait_ge(stage2_hi, k + 1)
                dve.tensor_tensor(whh_lo[:, k, :], stage2[:, k % 2, :], whh_hi[:, k, :].bitcast(F32), ALU.subtract)\
                    .then_inc(stage2_lo, 1)

            lo(0, 0)
            dve.wait_ge(bias_in, 32)
            dve.tensor_tensor(ig_bias[:, 0:2 * D], ig_bias[:, 0:2 * D], ig_bhh[:, :], ALU.add).then_inc(bias_done, 1)
            dve.wait_ge(bias_done, 1)
            split(0)
            split(1)
            lo(1, 1)
            add_bias(0, 0, 0)

            def pair(i):
                lo(2 * i, 0)
                add_bias(2 * i - 1, 1, i - 1)
                lo(2 * i + 1, 1)
                add_bias(2 * i, 0, i)

            pair(1)
            split(2)
            split(3)
            with dve.Fori(2, EC // 2 - 1) as i:
                pair(i)
            first_norm(dve, Period(0, -FIRST - 2))
            first_norm(dve, Period(0, -FIRST - 1))
            pair(EC // 2 - 1)
            h_low(dve, Period(0, -FIRST - 1))
            add_bias(EC - 1, 1, EC // 2 - 1)

        @block.tensor
        def _(pe):
            def transposes(c, s, i):
                pe.wait_ge(agg_loaded[s], 16 * (i + 1))
                wait_from(pe, a_lo_done, c - 1)
                for k in range(DK):
                    last = pe.transpose(bank[6 + s][:, k * R:(k + 1) * R], agg_in[:, s, k * P:(k + 1) * P],
                                        ident[0:R, 0:R])
                last.then_inc(t_a, 1)

            def product(c, s):
                pe.wait_ge(a_lo_done, c + 1)
                for q in range(3):
                    wait_from(pe, g_added, 3 * (c - 2) + q + 1)
                    n = 0
                    for k in range(DK):
                        for a, w in ((a_hi, wih_hi), (a_hi, wih_lo), (a_lo, wih_hi)):
                            last = pe.matmul(bank[3 * s + q][0:R, :], a[:, s, k * R:(k + 1) * R],
                                             w[:, k, q * D:(q + 1) * D], start=n == 0, stop=n == 3 * DK - 1)
                            n += 1
                    last.then_inc(g_prod, 1)

            transposes(0, 0, 0)
            transposes(1, 1, 0)
            product(0, 0)

            def pair(i):
                transposes(2 * i, 0, i)
                product(2 * i - 1, 1)
                transposes(2 * i + 1, 1, i)
                product(2 * i, 0)

            pair(1)
            with pe.Fori(2, EC // 2) as i:
                pair(i)
            turn_h(pe, Period(0, -FIRST - 1))
            product(EC - 1, 1)
            pe.wait_ge(g_added, 3 * (EC - 1))

        @block.sync
        def _(sp):
            sp.wait_ge(slots_in, 16 * EC)
            sp.dma_start(node_slot[:, :], slot_of_node.rearrange("(p t) o -> p (t o)", t=NT)).then_inc(table_in, 16)

            def store(t, s):
                at = t if isinstance(t, int) else sp.snap(t)
                sp.wait_ge(y_done, t + 1)
                sp.dma_start(out_tiles[:, bass.ds(at, 1), :].rearrange("p o d -> p (o d)"), y[:, s, :])\
                    .then_inc(y_stored[s], 16)

            def body(p):
                t = p.t
                if p.has(2) and not p.early(2):
                    s = p.slot(2)
                    at = t + 2 if isinstance(t, int) else sp.snap(t + 2)
                    wait_from(sp, x_h_done, t + 1)
                    sp.dma_start(xt[:, s, :], x_tiles[:, bass.ds(at, 1), :].rearrange("p o d -> p (o d)"))\
                        .then_inc(x_in[s], 16)
                if p.has(-3):
                    store(t - 3, p.slot(-3))

            periods(sp, body)
            store(NT - 1, (NT - 1) % 2)
            for s in range(2):
                sp.wait_ge(y_stored[s], 16 * (NT // 2))

        @block.gpsimd
        def _(pool):
            def gather(p, k):
                s, t = p.slot(k), p.t
                pool.tensor_copy(slot_at[:, s:s + 1], node_slot[:, bass.ds(t + k, 1)]).then_inc(slot_copied, 1)
                pool.wait_ge(slot_copied, t + k + 1).then_inc(held["pool"], 1)
                pool.indirect_dma_start(out=gates[:, s, :], out_offset=None, in_=gates_in,
                                        in_offset=bass.IndirectOffsetOnAxis(ap=slot_at[:, s:s + 1], axis=0),
                                        ).then_inc(gates_loaded[s], 16)

            def norm(p, k, which):
                s = p.slot(k)
                pool.wait_ge(var_done[which], p.t + k + 1)
                pool.tensor_tensor(rstd[which][:, s:s + 1], var_eps[which][:, :], minus_half[0:R, 0:1], ALU.pow)\
                    .then_inc(rstd_done[which], 1)
                pool.wait_ge(rstd_done[which], p.t + k + 1)
                pool.tensor_tensor(shift[which][:, s:s + 1], neg_mean[which][:, :], rstd[which][:, s:s + 1], ALU.mult)\
                    .then_inc(shift_done[which], 1)
                if which == 1:
                    pool.tensor_tensor(one_rstd[:, s:s + 1], rstd[1][:, s:s + 1], ones_col[:, 0:1], ALU.add)\
                        .then_inc(shift_done[which], 1)

            def body(p):
                t = p.t
                if p.has(-1):
                    norm(p, -1, 2)
                if p.has(0):
                    s = p.slot(0)
                    pool.wait_ge(hn_raw_done, t + 1)
                    wait_from(pool, r_hn_done, t - 1)
                    pool.tensor_tensor(hn[:, s, :], hn_raw[:, s, :], hn_bias[:, :], ALU.add).then_inc(hn_done, 1)
                if p.has(0):
                    s = p.slot(0)
                    pool.wait_ge(r_done, t + 1)
                    pool.wait_ge(hn_done, t + 1)
                    pool.tensor_tensor(r_hn[:, :], r_gate[:, :], hn[:, s, :], ALU.mult).then_inc(r_hn_done, 1)
                    wait_from(pool, n_done, t)
                    pool.wait_ge(gates_loaded[s], 16 * (p.turn(0) + 1))
                    pool.wait_ge(r_hn_done, t + 1)
                    pool.tensor_tensor(n_pre[:, :], r_hn[:, :], gates[:, s, 2 * D:G3], ALU.add).then_inc(n_pre_done, 1)
                if p.has(0):
                    s = p.slot(0)
                    pool.wait_ge(n_done, t + 1)
                    wait_from(pool, z_h_n_done, t)
                    pool.tensor_tensor(h_n[:, :], h[:, s, :], n_gate[:, s, :], ALU.subtract).then_inc(h_n_done, 1)

                if p.has(2):
                    norm(p, 2, 1)
                    if p.has(0):
                        pool.wait_ge(n_pre_done, t + 1)
                        pool.wait_ge(r_pre_done, t + 1)
                        pool.wait_ge(z_pre_done, t + 1).then_inc(held["pool"], 1)
                    if not p.early(2):
                        gather(p, 2)
                    s = p.slot(2)
                    pool.wait_ge(x_h_done, t + 3)
                    wait_from(pool, x1_done, t + 1)
                    pool.tensor_tensor(x_h_b[:, s, :], x_h[:, s, :], bn_shift[:, :], ALU.add).then_inc(x_h_b_done, 1)
                if p.first(1):
                    for s in range(2):
                        pool.wait_ge(g_stored[s], 16 * (EC // 2))
                    pool.wait_ge(bias_stored, 16)
                    for s in range(2):
                        pool.memset(hid[:, s, HE + 3 * V:KF * P], 0.0).then_inc(hid_set, 1)
                    pool.memset(extra[:, V - 1:V], 0.5).then_inc(hid_set, 1)
                    pool.wait_ge(table_in, 16)
                    gather(p, 1)
                    gather(p, 2)

            periods(pool, body)

        @block.scalar
        def _(act):
            def body(p):
                t = p.t
                if p.has(1):
                    s = p.slot(1)
                    act.wait_ge(shift_done[1], 2 * (t + 2))
                    wait_from(act, h_n_done, t)
                    act.activation(h[:, s, :], xt[:, s, :], ACT.Identity, bias=shift[1][:, s:s + 1],
                                   scale=rstd[1][:, s:s + 1]).then_inc(h_done, 1)
                    wait_from(act, x_h_b_done, t)
                    act.activation(x_h[:, s, :], xt[:, s, :], ACT.Identity, bias=shift[1][:, s:s + 1],
                                   scale=one_rstd[:, s:s + 1]).then_inc(x_h_done, 1)
                if p.has(0):
                    s = p.slot(0)
                    act.wait_ge(n_prod, t + 1)
                    wait_from(act, hn_done, t - 1)
                    act.activation(hn_raw[:, s, :], b_n[0:R, :], ACT.Copy).then_inc(hn_raw_done, 1)
                if p.has(-1):
                    s = p.slot(-1)
                    act.wait_ge(shift_done[2], t)
                    wait_from(act, h2_turned, t - 2)
                    act.activation(h2[:, s, :], x1[:, p.slot4(-1), :], ACT.Identity, bias=shift[2][:, s:s + 1],
                                   scale=rstd[2][:, s:s + 1]).then_inc(h2_done, 1)
                if p.has(0):
                    act.wait_ge(r_pre_done, t + 1)
                    wait_from(act, r_hn_done, t)
                    act.activation(r_gate[:, :], r_pre[:, :], ACT.Sigmoid).then_inc(r_done, 1)
                if p.has(1):
                    s = p.slot(1)
                    act.wait_ge(h_turned, t + 2)
                    wait_from(act, z_prod, t)
                    act.activation(h_hi[:, s, :], b_th[:, 0:DK * R], ACT.Copy).then_inc(h_hi_done, 1)
                if p.has(-1):
                    act.wait_ge(h2_turned, t)
                    wait_from(act, f1_prod, t - 1)
                    act.activation(h2_hi[:, :], b_th2[:, 0:DK * R], ACT.Copy).then_inc(h2_hi_done, 1)
                if p.has(-2):
                    act.wait_ge(hid_turned, t - 1)
                    wait_from(act, f2_prod, t - 2)
                    act.activation(hid_hi[:, :], b_thid[:, 0:KF * R], ACT.Copy).then_inc(hid_hi_done, 1)
                if p.has(0):
                    s = p.slot(0)
                    act.wait_ge(n_pre_done, t + 1)
                    wait_from(act, h_new_done, t - 1)
                    act.activation(n_gate[:, s, :], n_pre[:, :], ACT.Tanh).then_inc(n_done, 1)
                    act.wait_ge(z_pre_done, t + 1)
                    wait_from(act, z_h_n_done, t)
                    act.activation(z_gate[:, :], z_pre[:, :], ACT.Sigmoid).then_inc(z_done, 1)
                if p.has(-1):
                    act.wait_ge(gap_done, t)
                    wait_from(act, comb2_done, t - 1)
                    act.activation(weight[:, 0:1], gap[:, :], ACT.Sigmoid).then_inc(weight_done, 1)
                    act.activation(weight[:, 1:2], gap[:, :], ACT.Sigmoid, scale=-1.0).then_inc(weight_done, 1)
            periods(act, body)

        @block.vector
        def _(dve):
            def body(p):
                t = p.t
                if p.first(-2):
                    dve.wait_ge(hid_set, 3)
                if p.has(-2):
                    s = p.slot(-2)
                    dve.wait_ge(weight_done, 2 * (t - 1))
                    dve.wait_ge(comb1_done, 2 * t - 3)
                    dve.tensor_scalar(comb1[:, :], iota8[:, :], top_f[:, 0:1], weight[:, 0:1], ALU.is_equal, ALU.mult)\
                        .then_inc(comb1_done, 1)
                    dve.tensor_scalar(comb2[:, :], iota8[:, :], top_f[:, 1:2], weight[:, 1:2], ALU.is_equal, ALU.mult)\
                        .then_inc(comb2_done, 1)
                    dve.wait_ge(comb1_done, 2 * t - 2)
                    dve.wait_ge(comb2_done, t - 1)
                    wait_from(dve, hid_done, t - 2)
                    dve.tensor_tensor(extra[:, HS:HS + NE], comb1[:, :], comb2[:, :], ALU.add).then_inc(comb_done, 1)
                    dve.tensor_scalar(extra[:, 0:HS], f1[:, NE + HE:F1], 0.0, 0.5, ALU.max, ALU.mult)\
                        .then_inc(shared_done, 1)
                    dve.wait_ge(comb_done, t - 1)
                    wait_from(dve, hid_turned, t - 3)
                    dve.scalar_tensor_tensor(
                        hid[:, s, 0:HE].rearrange("p (e f) -> p e f", e=NE),
                        f1[:, NE:NE + HE].rearrange("p (e f) -> p e f", e=NE), 0.0,
                        extra[:, HS:HS + NE].unsqueeze(2).broadcast_to((R, NE, HF)), ALU.max, ALU.mult)
                    dve.wait_ge(shared_done, t - 1)
                    dve.tensor_copy(extra_hi[:, :], extra[:, :]).then_inc(extra_hi_done, 1)
                    dve.wait_ge(extra_hi_done, t - 1)
                    dve.tensor_copy(hid[:, s, HE:HE + 2 * V].rearrange("p (q v) -> p q v", q=2),
                                    extra_hi[:, :].bitcast(F32).unsqueeze(1).broadcast_to((R, 2, V)))
                    dve.tensor_tensor(hid[:, s, HE + 2 * V:HE + 3 * V], extra[:, :], extra_hi[:, :].bitcast(F32),
                                      ALU.subtract).then_inc(hid_done, 1)
                if p.has(2) and not p.early(2):
                    first_norm(dve, p)
                if p.has(-1):
                    dve.wait_ge(h2_hi_done, t)
                    dve.tensor_tensor(h2_lo[:, :], b_th2[:, 0:DK * R], h2_hi[:, :].bitcast(F32), ALU.subtract)\
                        .then_inc(h2_lo_done, 1)
                if p.has(-2):
                    dve.wait_ge(hid_hi_done, t - 1)
                    dve.tensor_tensor(hid_lo[:, :], b_thid[:, 0:(KF - 1) * R],
                                      hid_hi[:, 0:(KF - 1) * R].bitcast(F32), ALU.subtract)\
                        .then_inc(hid_lo_done, 1)
                if p.has(1) and not p.first(1):
                    h_low(dve, p)
                if p.has(0):
                    s = p.slot(0)
                    dve.wait_ge(z_prod, t + 1)
                    wait_from(dve, z_done, t)
                    dve.tensor_tensor(z_pre[:, :], b_z[0:R, :], gates[:, s, D:2 * D], ALU.add).then_inc(z_pre_done, 1)
                if p.has(-1):
                    dve.wait_ge(f1_prod, t)
                    dve.tensor_tensor(f1[:, :], b_f1[0:R, 0:F1], f1_bias[:, :], ALU.add).then_inc(f1_done, 1)
                    dve.wait_ge(f1_done, t).then_inc(held["dve"], 1)
                    dve.max(top[:, :], f1[:, 0:NE]).then_inc(top_done, 1)
                    dve.wait_ge(top_done, t)
                    wait_from(dve, weight_done, 2 * (t - 1))
                    dve.tensor_tensor(gap[:, :], top[:, 0:1], top[:, 1:2], ALU.subtract).then_inc(gap_done, 1)
                    dve.max_index(top_i[:, :], top[:, :], f1[:, 0:NE]).then_inc(top_i_done, 1)
                    dve.wait_ge(top_i_done, t)
                    dve.tensor_copy(top_f[:, :], top_i[:, 0:2]).then_inc(comb1_done, 1)
                if p.has(0):
                    s = p.slot(0)
                    dve.wait_ge(z_done, t + 1)
                    dve.wait_ge(h_n_done, t + 1)
                    dve.tensor_tensor(z_h_n[:, :], z_gate[:, :], h_n[:, :], ALU.mult).then_inc(z_h_n_done, 1)
                    dve.wait_ge(z_h_n_done, t + 1)
                    dve.tensor_tensor(h_new[:, :], z_h_n[:, :], n_gate[:, s, :], ALU.add).then_inc(h_new_done, 1)
                    dve.wait_ge(h_new_done, t + 1)
                    dve.tensor_tensor(scaled[:, :], h_new[:, :], bn_scale[:, :], ALU.mult).then_inc(scaled_done, 1)
                    dve.wait_ge(scaled_done, t + 1)
                    dve.wait_ge(x_h_b_done, t + 1)
                    wait_from(dve, y_done, t - 3)
                    dve.tensor_tensor(x1[:, p.slot4(0), :], scaled[:, :], x_h_b[:, s, :], ALU.add).then_inc(x1_done, 1)
                    dve.wait_ge(x1_done, t + 1)
                    dve.bn_stats(st[2][:, :], x1[:, p.slot4(0), :]).then_inc(st_done[2], 1)
                    statistics(dve, p, 0, 2)
                    mean_var(dve, p, 0, 2)
                if p.has(1):
                    s = p.slot(1)
                    dve.wait_ge(r_prod, t + 2)
                    dve.wait_ge(gates_loaded[s], 16 * (p.turn(1) + 1))
                    wait_from(dve, r_done, t + 1)
                    dve.tensor_tensor(r_pre[:, :], b_r[0:R, :], gates[:, s, 0:D], ALU.add).then_inc(r_pre_done, 1)
                if p.has(-2):
                    s = p.slot(-2)
                    dve.wait_ge(f2_prod, t - 1)
                    wait_from(dve, y_stored[s], 16 * p.turn(-2))
                    dve.tensor_tensor(y[:, s, :], b_f2[0:R, :], x1[:, p.slot4(-2), :], ALU.add).then_inc(y_done, 1)

            periods(dve, body)

        @block.tensor
        def _(pe):

            def gate(s, to, q, k0=0, k1=DK):
                n = 3 * k0
                for k in range(k0, k1):
                    for a, w in ((h_hi, whh_hi), (h_hi, whh_lo), (h_lo, whh_hi)):
                        last = pe.matmul(to[0:R, :], a[:, s, k * R:(k + 1) * R], w[:, k, q * D:(q + 1) * D],
                                         start=n == 0, stop=n == 3 * DK - 1)
                        n += 1
                return last

            def body(p):
                t = p.t
                if p.has(0):
                    s = p.slot(0)
                    pe.wait_ge(h_lo_done, t + 1)
                    wait_from(pe, r_pre_done, t)
                    gate(s, b_r, 0).then_inc(r_prod, 1)
                    wait_from(pe, hn_raw_done, t)
                    gate(s, b_n, 2).then_inc(n_prod, 1)
                if p.has(1) and not p.first(1):
                    turn_h(pe, p)
                if p.has(0):
                    wait_from(pe, z_pre_done, t)
                    gate(p.slot(0), b_z, 1, 0, 2)
                if p.has(-1):
                    pe.wait_ge(h2_done, t)
                    wait_from(pe, h2_lo_done, t - 1)
                    turn(pe, b_th2, h2[:, p.slot(-1), :], DK).then_inc(h2_turned, 1)
                if p.has(0):
                    gate(p.slot(0), b_z, 1, 2, DK).then_inc(z_prod, 1)
                if p.has(-2):
                    pe.wait_ge(hid_done, t - 1)
                    wait_from(pe, hid_lo_done, t - 2)
                    turn(pe, b_thid, hid[:, p.slot(-2), :], KF).then_inc(hid_turned, 1)
                if p.has(-1):
                    pe.wait_ge(h2_lo_done, t)
                    wait_from(pe, f1_done, t - 1)
                    n = 0
                    for k in range(DK):
                        for a, w in ((h2_hi, f1_hi), (h2_hi, f1_lo), (h2_lo, f1_hi)):
                            last = pe.matmul(b_f1[0:R, 0:F1], a[:, k * R:(k + 1) * R], w[:, k, :],
                                             start=n == 0, stop=n == 3 * DK - 1)
                            n += 1
                    last.then_inc(f1_prod, 1)
                if p.has(-2):
                    pe.wait_ge(hid_lo_done, t - 1)
                    wait_from(pe, y_done, t - 2)
                    n = 0
                    for k in range(KF - 1):
                        for a, w in ((hid_hi, f2_hi), (hid_hi, f2_lo), (hid_lo, f2_hi)):
                            pe.matmul(b_f2[0:R, :], a[:, k * R:(k + 1) * R], w[:, k, :], start=n == 0, stop=False)
                            n += 1
                    last = pe.matmul(b_f2[0:R, :], hid_hi[:, (KF - 1) * R:KF * R], f2_hi[:, KF - 1, :],
                                     start=False, stop=True)
                    last.then_inc(f2_prod, 1)

            periods(pe, body)


def kernel(x, src, dst, edge_attr_128, L0_gnn_W1, L0_gnn_b1, L0_gnn_W2, L0_gnn_b2, L0_gnn_W_ih, L0_gnn_W_hh,
           L0_gnn_b_ih, L0_gnn_b_hh, L0_gnn_gamma, L0_gnn_beta, L0_gnn_run_mean, L0_gnn_run_var, L0_ffn_Wg,
           L0_ffn_bg, L0_ffn_W1, L0_ffn_b1, L0_ffn_W2, L0_ffn_b2, L0_ffn_Ws1, L0_ffn_bs1, L0_ffn_Ws2, L0_ffn_bs2):
    import numpy as np
    import concourse.bacc as bacc
    from concourse.bass_utils import run_bass_kernel_spmd

    rows, edge_tiles, sup = 125, 20, 4
    src, dst, attr = np.asarray(src), np.asarray(dst), np.asarray(edge_attr_128)
    w1, w2 = np.asarray(L0_ffn_W1), np.asarray(L0_ffn_W2)
    by_row = dst.reshape(rows, edge_tiles)
    arrays = dict(
        x=x, src=src.reshape(rows, edge_tiles), dst=by_row,
        dst_rows=by_row.T.reshape(edge_tiles // sup, sup * rows),
        attr_t=attr.reshape(rows, edge_tiles, -1).transpose(2, 1, 0).reshape(attr.shape[1], -1),
        w1t=np.asarray(L0_gnn_W1).T, b1=np.asarray(L0_gnn_b1).reshape(-1, 128).T, w2t=np.asarray(L0_gnn_W2).T, b2=L0_gnn_b2,
        wih_t=np.asarray(L0_gnn_W_ih).T, whh_t=np.asarray(L0_gnn_W_hh).T, b_ih=L0_gnn_b_ih, b_hh=L0_gnn_b_hh,
        gamma=L0_gnn_gamma, beta=L0_gnn_beta, run_mean=L0_gnn_run_mean, run_var=L0_gnn_run_var,
        wg=L0_ffn_Wg, bg=L0_ffn_bg, ew1=w1.transpose(1, 0, 2).reshape(w1.shape[1], -1),
        eb1=np.asarray(L0_ffn_b1).reshape(-1), ew2=w2.reshape(-1, w2.shape[2]), eb2=L0_ffn_b2,
        ws1=L0_ffn_Ws1, bs1=L0_ffn_bs1, ws2=L0_ffn_Ws2, bs2=L0_ffn_bs2)
    arrays = {f"in_{k}": np.ascontiguousarray(v) for k, v in arrays.items()}
    nc = bacc.Bacc("TRN2", target_bir_lowering=False, num_devices=1)
    args = [nc.dram_tensor(k, v.shape, mybir.dt.from_np(v.dtype), kind="ExternalInput").ap()
            for k, v in arrays.items()]
    out = nc.dram_tensor("out", tuple(np.asarray(x).shape), F32, kind="ExternalOutput").ap()
    gnn_ffn(nc, *args, out)
    result = run_bass_kernel_spmd(nc, [arrays], core_ids=[0])
    return result.results[0]["out"]
```
